# Optimizing a Trainium2 kernel written in Bass

```python
import numpy as np
import jax
import jax.numpy as jnp

def _softmax(x, axis=-1):
    return jax.nn.softmax(x, axis=axis)

def _gelu(x):
    return jax.nn.gelu(x, approximate=True)

def _silu(x):
    return jax.nn.silu(x)

def _sigmoid(x):
    return jax.nn.sigmoid(x)

def _layernorm(x, axis=-1, eps=1e-05):
    m = jnp.mean(x, axis=axis, keepdims=True)
    v = jnp.var(x, axis=axis, keepdims=True)
    return (x - m) / jnp.sqrt(v + eps)

def _scatter_add(tgt, idx, src, axis=0):
    return tgt.at[idx].add(src)

def _segment_sum(src, seg, n):
    return jax.ops.segment_sum(src, seg, n)
kernel_name = 'mk_recurrent_d2_jaxref_r8_4e01af'

def setup_inputs(seed: int=0):
    np.random.seed(seed)
    _w = jnp.asarray

    def _L0_attn_setup():
        import jax, jax.numpy as jnp
        import numpy as np
        from jax import lax
        D_MODEL, D_STATE, D_CONV, EXPAND = (128, 16, 4, 2)
        D_INNER = D_MODEL * EXPAND
        LN_EPS = 1e-05

        def _silu(v):
            return v * jax.nn.sigmoid(v)

        def _forward(x, W_in, conv_w, conv_b, W_x, W_dt, b_dt, A_log, D_param, W_out, ln_g, ln_b):
            B, T, _ = x.shape
            xz = jnp.einsum('btd,ed->bte', x, W_in)
            xp, z = (xz[..., :D_INNER], xz[..., D_INNER:])
            xc = lax.conv_general_dilated(jnp.transpose(xp, (0, 2, 1)), conv_w, window_strides=(1,), padding=[(D_CONV - 1, 0)], feature_group_count=D_INNER, dimension_numbers=('NCH', 'OIH', 'NCH')) + conv_b[None, :, None]
            xc = _silu(jnp.transpose(xc, (0, 2, 1)))
            ssm = jnp.einsum('bti,si->bts', xc, W_x)
            Bp, Cp = (ssm[..., :D_STATE], ssm[..., D_STATE:])
            dt = jax.nn.softplus(jnp.einsum('bti,oi->bto', xc, W_dt) + b_dt)
            A = -jnp.exp(A_log)

            def step(h, inp):
                x_t, b_t, c_t, dt_t = inp
                dA = jnp.exp(dt_t[..., None] * A)
                h = dA * h + dt_t[..., None] * b_t[:, None, :] * x_t[..., None]
                y_t = jnp.einsum('bds,bs->bd', h, c_t)
                return (h, y_t)
            h0 = jnp.zeros((B, D_INNER, D_STATE), dtype=x.dtype)
            tm = lambda a: jnp.moveaxis(a, 1, 0)
            _, ys = lax.scan(step, h0, (tm(xc), tm(Bp), tm(Cp), tm(dt)))
            y = jnp.moveaxis(ys, 0, 1)
            mu = jnp.mean(y, axis=-1, keepdims=True)
            var = jnp.mean((y - mu) ** 2, axis=-1, keepdims=True)
            y = (y - mu) * lax.rsqrt(var + LN_EPS) * ln_g + ln_b
            y = y + xc * D_param
            y = y * _silu(z)
            return jnp.einsum('bti,di->btd', y, W_out)
        key = jax.random.key(seed)
        ks = jax.random.split(key, 12)
        B, T = (4, 256)
        x = jax.random.normal(ks[0], (B, T, D_MODEL), dtype=jnp.float32)
        W_in = jax.random.normal(ks[1], (2 * D_INNER, D_MODEL), dtype=jnp.float32) * D_MODEL ** (-0.5)
        conv_w = jax.random.normal(ks[2], (D_INNER, 1, D_CONV), dtype=jnp.float32) * D_CONV ** (-0.5)
        conv_b = jax.random.normal(ks[3], (D_INNER,), dtype=jnp.float32) * 0.01
        W_x = jax.random.normal(ks[4], (2 * D_STATE, D_INNER), dtype=jnp.float32) * D_INNER ** (-0.5)
        dt_init_std = D_INNER ** (-0.5)
        W_dt = jax.random.uniform(ks[5], (D_INNER, D_INNER), minval=-dt_init_std, maxval=dt_init_std, dtype=jnp.float32)
        dt = jnp.exp(jax.random.uniform(ks[6], (D_INNER,)) * (np.log(0.1) - np.log(0.001)) + np.log(0.001))
        b_dt = dt + jnp.log(-jnp.expm1(-dt))
        A_log = jnp.log(jnp.arange(1, D_STATE + 1, dtype=jnp.float32) * 0.5)
        D_param = jnp.ones((D_INNER,), dtype=jnp.float32)
        W_out = jax.random.normal(ks[7], (D_MODEL, D_INNER), dtype=jnp.float32) * D_MODEL ** (-0.5)
        ln_g = jnp.ones((D_INNER,), dtype=jnp.float32)
        ln_b = jnp.zeros((D_INNER,), dtype=jnp.float32)
        return {'x': x, 'W_in': W_in, 'conv_w': conv_w, 'conv_b': conv_b, 'W_x': W_x, 'W_dt': W_dt, 'b_dt': b_dt, 'A_log': A_log, 'D_param': D_param, 'W_out': W_out, 'ln_g': ln_g, 'ln_b': ln_b}
    _L0_attn_in = _L0_attn_setup()

    def _L0_ffn_setup():
        import jax, jax.numpy as jnp
        import numpy as np
        H = 128
        E = 8
        B, S = (4, 256)
        key = jax.random.key(seed)
        k1, k2, k3, k4 = jax.random.split(key, 4)
        x = jax.random.normal(k1, (B, S, H), dtype=jnp.float32)
        wg = jax.random.normal(k2, (H, E), dtype=jnp.float32) * 0.02
        W = jax.random.normal(k3, (E, H, H), dtype=jnp.float32) * 0.02
        b = jax.random.normal(k4, (E, H), dtype=jnp.float32) * 0.02
        return {'x': x, 'wg': wg, 'W': W, 'b': b}
    _L0_ffn_in = _L0_ffn_setup()

    def _L1_attn_setup():
        import jax, jax.numpy as jnp
        import numpy as np
        B, T, D, H = (4, 256, 128, 16)
        HD = D // H
        ROPE_BASE = 10000.0

        def rotate_half(x):
            x1 = x[..., ::2]
            x2 = x[..., 1::2]
            return jnp.stack((-x2, x1), axis=-1).reshape(x.shape)

        def rope_tables(seq_len, dim, dtype=jnp.float32):
            inv = 1.0 / ROPE_BASE ** (jnp.arange(0, dim, 2, dtype=jnp.float32) / dim)
            t = jnp.arange(seq_len, dtype=jnp.float32)
            freqs = jnp.einsum('i,j->ij', t, inv)
            emb = jnp.concatenate((freqs, freqs), axis=-1)
            return (jnp.cos(emb).astype(dtype)[None, None], jnp.sin(emb).astype(dtype)[None, None])
        key = jax.random.key(seed)
        ks = jax.random.split(key, 9)
        s = 0.02
        return {'x': jax.random.normal(ks[0], (B, T, D), jnp.float32), 'Wq': jax.random.normal(ks[1], (D, D), jnp.float32) * s, 'bq': jnp.zeros((D,), jnp.float32), 'Wk': jax.random.normal(ks[2], (D, D), jnp.float32) * s, 'bk': jnp.zeros((D,), jnp.float32), 'Wv': jax.random.normal(ks[3], (D, D), jnp.float32) * s, 'bv': jnp.zeros((D,), jnp.float32), 'Wo': jax.random.normal(ks[4], (D, D), jnp.float32) * s, 'bo': jnp.zeros((D,), jnp.float32)}
    _L1_attn_in = _L1_attn_setup()

    def _L1_ffn_setup():
        import jax, jax.numpy as jnp
        import numpy as np
        N, T, D = (4, 512, 128)
        NUM_EXPERTS = 8
        EXPERT_CAP = 2.0
        MLP_RATIO = 4
        HIDDEN = MLP_RATIO * D
        key = jax.random.key(seed)
        k1, k2, k3, k4 = jax.random.split(key, 4)
        x = jax.random.normal(k1, (N, T, D), dtype=jnp.float32)
        gate_w = jax.random.truncated_normal(k2, -2.0, 2.0, (D, NUM_EXPERTS), dtype=jnp.float32) * 0.02
        w1 = jax.random.normal(k3, (NUM_EXPERTS, D, HIDDEN), dtype=jnp.float32) * 0.02
        w2 = jax.random.normal(k4, (NUM_EXPERTS, HIDDEN, D), dtype=jnp.float32) * 0.02
        return {'x': x, 'gate_w': gate_w, 'w1': w1, 'w2': w2}
    _L1_ffn_in = _L1_ffn_setup()
    _d = {'L0_attn_x': _L0_attn_in['x'], 'L0_attn_W_in': _L0_attn_in['W_in'], 'L0_attn_conv_w': _L0_attn_in['conv_w'], 'L0_attn_conv_b': _L0_attn_in['conv_b'], 'L0_attn_W_x': _L0_attn_in['W_x'], 'L0_attn_W_dt': _L0_attn_in['W_dt'], 'L0_attn_b_dt': _L0_attn_in['b_dt'], 'L0_attn_A_log': _L0_attn_in['A_log'], 'L0_attn_D_param': _L0_attn_in['D_param'], 'L0_attn_W_out': _L0_attn_in['W_out'], 'L0_attn_ln_g': _L0_attn_in['ln_g'], 'L0_attn_ln_b': _L0_attn_in['ln_b'], 'L0_ffn_wg': _L0_ffn_in['wg'], 'L0_ffn_W': _L0_ffn_in['W'], 'L0_ffn_b': _L0_ffn_in['b'], 'L1_attn_Wq': _L1_attn_in['Wq'], 'L1_attn_bq': _L1_attn_in['bq'], 'L1_attn_Wk': _L1_attn_in['Wk'], 'L1_attn_bk': _L1_attn_in['bk'], 'L1_attn_Wv': _L1_attn_in['Wv'], 'L1_attn_bv': _L1_attn_in['bv'], 'L1_attn_Wo': _L1_attn_in['Wo'], 'L1_attn_bo': _L1_attn_in['bo'], 'L1_ffn_gate_w': _L1_ffn_in['gate_w'], 'L1_ffn_w1': _L1_ffn_in['w1'], 'L1_ffn_w2': _L1_ffn_in['w2']}
    _x0 = _d['L0_attn_x']
    _d['L0_attn_x'] = jax.random.normal(jax.random.fold_in(jax.random.key(seed), 1), (4, 1024, 128), dtype=_x0.dtype)
    del _x0
    return _d

def reference(L0_attn_x, L0_attn_W_in, L0_attn_conv_w, L0_attn_conv_b, L0_attn_W_x, L0_attn_W_dt, L0_attn_b_dt, L0_attn_A_log, L0_attn_D_param, L0_attn_W_out, L0_attn_ln_g, L0_attn_ln_b, L0_ffn_wg, L0_ffn_W, L0_ffn_b, L1_attn_Wq, L1_attn_bq, L1_attn_Wk, L1_attn_bk, L1_attn_Wv, L1_attn_bv, L1_attn_Wo, L1_attn_bo, L1_ffn_gate_w, L1_ffn_w1, L1_ffn_w2):

    def _L0_attn_ref(x, W_in, conv_w, conv_b, W_x, W_dt, b_dt, A_log, D_param, W_out, ln_g, ln_b):
        import jax, jax.numpy as jnp
        import numpy as np
        from jax import lax
        D_MODEL, D_STATE, D_CONV, EXPAND = (128, 16, 4, 2)
        D_INNER = D_MODEL * EXPAND
        LN_EPS = 1e-05

        def _silu(v):
            return v * jax.nn.sigmoid(v)

        def _forward(x, W_in, conv_w, conv_b, W_x, W_dt, b_dt, A_log, D_param, W_out, ln_g, ln_b):
            B, T, _ = x.shape
            xz = jnp.einsum('btd,ed->bte', x, W_in)
            xp, z = (xz[..., :D_INNER], xz[..., D_INNER:])
            xc = lax.conv_general_dilated(jnp.transpose(xp, (0, 2, 1)), conv_w, window_strides=(1,), padding=[(D_CONV - 1, 0)], feature_group_count=D_INNER, dimension_numbers=('NCH', 'OIH', 'NCH')) + conv_b[None, :, None]
            xc = _silu(jnp.transpose(xc, (0, 2, 1)))
            ssm = jnp.einsum('bti,si->bts', xc, W_x)
            Bp, Cp = (ssm[..., :D_STATE], ssm[..., D_STATE:])
            dt = jax.nn.softplus(jnp.einsum('bti,oi->bto', xc, W_dt) + b_dt)
            A = -jnp.exp(A_log)

            def step(h, inp):
                x_t, b_t, c_t, dt_t = inp
                dA = jnp.exp(dt_t[..., None] * A)
                h = dA * h + dt_t[..., None] * b_t[:, None, :] * x_t[..., None]
                y_t = jnp.einsum('bds,bs->bd', h, c_t)
                return (h, y_t)
            h0 = jnp.zeros((B, D_INNER, D_STATE), dtype=x.dtype)
            tm = lambda a: jnp.moveaxis(a, 1, 0)
            _, ys = lax.scan(step, h0, (tm(xc), tm(Bp), tm(Cp), tm(dt)))
            y = jnp.moveaxis(ys, 0, 1)
            mu = jnp.mean(y, axis=-1, keepdims=True)
            var = jnp.mean((y - mu) ** 2, axis=-1, keepdims=True)
            y = (y - mu) * lax.rsqrt(var + LN_EPS) * ln_g + ln_b
            y = y + xc * D_param
            y = y * _silu(z)
            return jnp.einsum('bti,di->btd', y, W_out)
        return _forward(x, W_in, conv_w, conv_b, W_x, W_dt, b_dt, A_log, D_param, W_out, ln_g, ln_b)

    def _L0_ffn_ref(x, wg, W, b):
        import jax, jax.numpy as jnp
        import numpy as np
        H = 128
        E = 8
        B, S = (4, 256)
        Bb, Ss, Hh = x.shape
        Ee = wg.shape[1]
        T = Bb * Ss
        C = T // Ee
        xt = x.reshape(T, Hh)
        logits = xt @ wg
        probs = jax.nn.softmax(logits, axis=-1)
        idx = jnp.argmax(probs, axis=-1)
        mask = jax.nn.one_hot(idx, Ee, dtype=xt.dtype)
        locations = jnp.cumsum(mask, axis=0) - mask
        mask = mask * (locations < C).astype(xt.dtype)
        gate = jnp.sum(probs * mask, axis=-1)
        loc_s = jnp.sum(locations * mask, axis=-1).astype(jnp.int32)
        loc_oh = jax.nn.one_hot(loc_s, C, dtype=xt.dtype)
        dispatch = mask[:, :, None] * loc_oh[:, None, :]
        combine = gate[:, None, None] * dispatch
        exp_in = jnp.einsum('tec,th->ech', dispatch, xt)
        exp_out = jnp.einsum('ech,efh->ecf', exp_in, W) + b[:, None, :]
        out = jnp.einsum('tec,ecf->tf', combine, exp_out)
        return out.reshape(Bb, Ss, Hh)

    def _L1_attn_ref(x, Wq, bq, Wk, bk, Wv, bv, Wo, bo):
        import jax, jax.numpy as jnp
        import numpy as np
        B, T, D, H = (4, 256, 128, 16)
        HD = D // H
        ROPE_BASE = 10000.0

        def rotate_half(x):
            x1 = x[..., ::2]
            x2 = x[..., 1::2]
            return jnp.stack((-x2, x1), axis=-1).reshape(x.shape)

        def rope_tables(seq_len, dim, dtype=jnp.float32):
            inv = 1.0 / ROPE_BASE ** (jnp.arange(0, dim, 2, dtype=jnp.float32) / dim)
            t = jnp.arange(seq_len, dtype=jnp.float32)
            freqs = jnp.einsum('i,j->ij', t, inv)
            emb = jnp.concatenate((freqs, freqs), axis=-1)
            return (jnp.cos(emb).astype(dtype)[None, None], jnp.sin(emb).astype(dtype)[None, None])
        b, t, d = x.shape

        def proj(W, bias):
            return (x @ W.T + bias).reshape(b, t, H, HD).transpose(0, 2, 1, 3)
        q, k, v = (proj(Wq, bq), proj(Wk, bk), proj(Wv, bv))
        cos, sin = rope_tables(t, HD, x.dtype)
        q = q * cos + rotate_half(q) * sin
        k = k * cos + rotate_half(k) * sin
        scale = 1.0 / jnp.sqrt(jnp.asarray(HD, x.dtype))
        attn = jnp.einsum('bhqd,bhkd->bhqk', q, k) * scale
        attn = jax.nn.softmax(attn, axis=-1)
        out = jnp.einsum('bhqk,bhkd->bhqd', attn, v)
        out = out.transpose(0, 2, 1, 3).reshape(b, t, d)
        return out @ Wo.T + bo

    def _L1_ffn_ref(x, gate_w, w1, w2):
        import jax, jax.numpy as jnp
        import numpy as np
        N, T, D = (4, 512, 128)
        NUM_EXPERTS = 8
        EXPERT_CAP = 2.0
        MLP_RATIO = 4
        HIDDEN = MLP_RATIO * D
        x = x.astype(jnp.float32)
        n, t, d = x.shape
        k = int(EXPERT_CAP * t / NUM_EXPERTS)
        scores = jnp.einsum('ntd,de->nte', x, gate_w)
        probs = jax.nn.softmax(scores, axis=-1)
        probs = jnp.transpose(probs, (0, 2, 1))
        g, m = jax.lax.top_k(probs, k)
        xin = jax.vmap(lambda xb, mb: xb[mb])(x, m)
        h = jax.nn.gelu(jnp.einsum('nekd,edf->nekf', xin, w1))
        h = jnp.einsum('nekf,efd->nekd', h, w2)
        weighted = g[..., None] * h
        flat_idx = (m + jnp.arange(n, dtype=m.dtype)[:, None, None] * t).reshape(-1)
        out = jnp.zeros((n * t, d), dtype=jnp.float32).at[flat_idx].add(weighted.reshape(-1, d))
        out = out.reshape(n, t, d)
        return out.astype(jnp.bfloat16)
    x = L0_attn_x
    xn = _layernorm(x, axis=-1)
    s = _L0_attn_ref(xn, L0_attn_W_in, L0_attn_conv_w, L0_attn_conv_b, L0_attn_W_x, L0_attn_W_dt, L0_attn_b_dt, L0_attn_A_log, L0_attn_D_param, L0_attn_W_out, L0_attn_ln_g, L0_attn_ln_b)
    g = _silu(_L0_ffn_ref(xn, L0_ffn_wg, L0_ffn_W, L0_ffn_b))
    x = x + s * g
    xn = _layernorm(x, axis=-1)
    s = _L1_attn_ref(xn, L1_attn_Wq, L1_attn_bq, L1_attn_Wk, L1_attn_bk, L1_attn_Wv, L1_attn_bv, L1_attn_Wo, L1_attn_bo)
    g = _silu(_L1_ffn_ref(xn, L1_ffn_gate_w, L1_ffn_w1, L1_ffn_w2))
    x = x + s * g
    return x

_drawn_inputs = setup_inputs


def setup_inputs(seed=0):
    import zlib

    import numpy as np

    out = dict(_drawn_inputs(seed))
    spreads = {'L0_attn_D_param': (1.0, 0.6),
     'L0_attn_ln_g': (1.0, 0.6),
     'L0_attn_ln_b': (0.0, 0.8),
     'L1_attn_bq': (0.0, 0.8),
     'L1_attn_bk': (0.0, 0.8),
     'L1_attn_bv': (0.0, 0.8),
     'L1_attn_bo': (0.0, 0.8)}
    factors = {'L0_attn_W_in': 2.709,
     'L0_attn_conv_w': 2.673,
     'L0_attn_conv_b': 8.0,
     'L0_attn_W_x': 3.276,
     'L0_attn_W_dt': 8.0,
     'L0_attn_b_dt': 4.968,
     'L0_attn_A_log': 5.168,
     'L0_ffn_wg': 2.812,
     'L0_ffn_b': 8.0,
     'L1_attn_Wq': 8.0,
     'L1_attn_Wk': 8.0,
     'L1_attn_Wv': 8.0,
     'L1_attn_Wo': 8.0,
     'L1_ffn_gate_w': 8.0,
     'L1_ffn_w1': 8.0,
     'L1_ffn_w2': 8.0}
    for name, (base, spread) in spreads.items():
        noise = np.random.default_rng([zlib.crc32(name.encode()), seed]).standard_normal(out[name].shape)
        drawn = base * np.exp(spread * noise) if base else spread * noise
        out[name] = jnp.asarray(drawn.astype(out[name].dtype))
    for name, factor in factors.items():
        out[name] = (out[name] * factor).astype(out[name].dtype)
    return out
```

```python
from contextlib import ExitStack

import numpy as np

import concourse.bass as bass
from concourse import mybir

F32 = mybir.dt.float32
BF16 = mybir.dt.bfloat16
I32 = mybir.dt.int32
ALU = mybir.AluOpType
ACT = mybir.ActivationFunctionType
AX_X = mybir.AxisListType.X

P = 128
B, T, D = 4, 1024, 128
NBLK = T // P
HALF = T // 2
DI, NH2 = 256, 2
NS = 16
TAPS = 4
E = 8
CAP0 = B * T // E
K1 = 2 * T // E
H, HD = 16, 8
HG = 4
HID = 512
EPS = 1e-5
PARTS = 96
LOWEST = float(np.finfo(np.float32).min)
ONE_BITS = 29


def mixed_layers(nc, t, out):
    with ExitStack() as ctx:
        def sb(name, shape, dt=F32, stack=ctx):
            return stack.enter_context(nc.sbuf_tensor(name, shape, dt))

        def sem(name):
            return ctx.enter_context(nc.semaphore(name))

        ps = ctx.enter_context(nc.psum_tensor("ps", [P, 8, HALF], F32))

        def banks(b, n, parts=P):
            return ps[0:parts, b:b + n, :].rearrange("p b c -> p (b c)")

        def over(ap, axis, n):
            v = ap.unsqueeze(axis)
            shape = list(v.shape)
            shape[axis] = n
            return v.broadcast_to(shape)

        ident = sb("ident", [P, P])
        before_tok = sb("before_tok", [P, P], BF16)
        ones_bf = sb("ones_bf", [P, P], BF16)
        zeros_bf = sb("zeros_bf", [P, HALF], BF16)
        pick = sb("pick", [PARTS, 2 * NS, P], BF16)
        rank_w = sb("rank_w", [P, E])
        eps_col = sb("eps_col", [P, 1])
        wg1 = sb("wg1", [P, E])
        x_all = sb("x_all", [P, B, NBLK, D])
        xn1T_all = sb("xn1T_all", [P, B, T])
        probs = sb("probs", [P, B, NBLK, E])
        gate1 = sb("gate1", [P, B, NBLK, E])
        bn = sb("bn", [P, NBLK, 6])
        mv = sb("mv", [P, NBLK, 2])
        std = sb("std", [P, NBLK])
        rstd = sb("rstd", [P, NBLK])
        xn = sb("xn", [P, NBLK, D])
        lg = sb("lg", [P, NBLK, E])
        ex = sb("ex", [P, NBLK, E])
        m8 = sb("m8", [P, NBLK])
        s8 = sb("s8", [P, NBLK])
        r8 = sb("r8", [P, NBLK])

        l0 = ExitStack()
        def sb0(name, shape, dt=F32):
            return sb(name, shape, dt, l0)
        w_in = sb0("w_in", [P, 2 * DI])
        tap_b = sb0("tap_b", [P, TAPS, DI])
        w_tap = sb0("w_tap", [P, TAPS, DI])
        w_x = sb0("w_x", [P, NH2, PARTS])
        w_dt = sb0("w_dt", [P, NH2, DI])
        w_out = sb0("w_out", [P, NH2, D])
        chan = sb0("chan", [P, 5, NH2])
        mean_w = sb0("mean_w", [P, P])
        a_log = sb0("a_log", [P, NS])
        a_exp = sb0("a_exp", [P, NS])
        a_neg = sb0("a_neg", [P, NS])
        wg0 = sb0("wg0", [P, E])
        w_e0 = sb0("w_e0", [P, E, D])
        b_e0 = sb0("b_e0", [E, D])
        taken = sb0("taken", [P, E])
        xnT = sb0("xnT", [P, TAPS - 1 + T])
        zs = sb0("zs", [P, NH2, T])
        xc = sb0("xc", [P, NH2, T])
        dt_ = sb0("dt_", [P, NH2, T])
        dtx = sb0("dtx", [P, NH2, T])
        bc = sb0("bc", [PARTS, T], BF16)
        mid = sb0("mid", [PARTS, T], BF16)
        rest = sb0("rest", [PARTS, T])
        dA = [sb0(f"dA{i}", [P, NH2, T]) for i in range(2)]
        hs = [sb0(f"hs{i}", [P, NH2, T]) for i in range(2)]
        hc = [sb0(f"hc{i}", [P, NH2, T]) for i in range(2)]
        c_sb = [sb0(f"c_sb{i}", [P, T]) for i in range(2)]
        probs0 = sb0("probs0", [P, NBLK, E])
        pmax = sb0("pmax", [P, NBLK])
        eqw = sb0("eqw", [P, NBLK, E])
        first = sb0("first", [P, NBLK])
        choice = sb0("choice", [P, NBLK, E])
        choice_bf = sb0("choice_bf", [P, NBLK, E], BF16)
        pos = sb0("pos", [P, NBLK, E])
        kept = sb0("kept", [P, NBLK, E])
        gate0 = sb0("gate0", [P, NBLK, PARTS])
        gateT = sb0("gateT", [E, T])
        gparts = sb0("gparts", [PARTS, T], BF16)
        s_gT = sb0("s_gT", [P, T])
        xg = [sb0(f"xg{i}", [P, T]) for i in range(2)]
        l0.close()

        cos = sb("cos", [P, T])
        sin = sb("sin", [P, T])
        w_qk = sb("w_qk", [P, 4, P])
        b_qk = sb("b_qk", [P, 5])
        w_v = sb("w_v", [P, P])
        b_v = sb("b_v", [P, P])
        w_o = sb("w_o", [P, P])
        xT = sb("xT", [P, T])
        q_op = sb("q_op", [PARTS, H, T], BF16)
        k_op = sb("k_op", [PARTS, H, T], BF16)
        big = [sb(f"big{i}", [P, HG, T]) for i in range(2)]
        v_tok = sb("v_tok", [P, NBLK, P])
        v_grp = sb("v_grp", [P, NBLK, HG, 32])
        top = sb("top", [P, H * NBLK])
        top_parts = sb("top_parts", [P, 3, P], BF16)
        top_rest = sb("top_rest", [P, P])
        o_T = sb("o_T", [P, T])
        rsum = sb("rsum", [P, NBLK, HG])
        att = sb("att", [P, NBLK, P])
        attT = sb("attT", [P, T])
        s1T = sb("s1T", [P, T])
        w1 = [sb(f"w1_{i}", [P, HID]) for i in range(2)]
        w2 = [sb(f"w2_{i}", [P, HID // P, D]) for i in range(2)]
        acc_bf = sb("acc_bf", [P, T], BF16)
        silu_bf = sb("silu_bf", [P, T], BF16)
        gpad = sb("gpad", [P, NBLK, PARTS])
        gparts1 = sb("gparts1", [PARTS, T], BF16)
        thr = sb("thr", [P, B, E], I32)
        bit = sb("bit", [P, B, E], I32)
        cand = sb("cand", [P, B, E], I32)
        step = sb("step", [P, B, E], I32)
        over_thr = sb("over_thr", [P, B, NBLK, E], BF16)
        at_thr = sb("at_thr", [P, B, NBLK, E], BF16)
        need = sb("need", [P, B, E])
        picked = sb("picked", [P, B, NBLK, E])
        flat = [t_[:].rearrange("p h t -> p (h t)") for t_ in big]
        rot = [[flat[i][:, j * T:(j + 1) * T] for j in range(2)] for i in range(2)]
        qk_parts = [flat[i][:, 2 * T:2 * T + 3 * T // 2].bitcast(BF16).rearrange("p (j t) -> p j t", j=3)
                    for i in range(2)]
        acc = attT
        hid = [flat[0][:, j * T:(j + 1) * T] for j in range(4)]
        gate_sb = [flat[1][:, j * T:(j + 1) * T] for j in range(2)]
        grest = flat[1][0:PARTS, 2 * T:3 * T]
        gmid = flat[1][0:PARTS, 3 * T:3 * T + T // 2].bitcast(BF16)
        weighted = flat[1][:, 3 * T + HALF:4 * T]
        top_run = [flat[i][:, 0:T].rearrange("p (k t) -> p k t", k=2) for i in range(2)]
        half_sb = [flat[i][:, 7 * HALF:8 * HALF] for i in range(2)]
        parts_dram = nc.dram_tensor("parts_dram", (2, 3, P, T), BF16, kind="Internal").ap()
        top_dram = nc.dram_tensor("top_dram", (3, H * NBLK, P), BF16, kind="Internal").ap()

        sems = {}

        def S(name):
            if name not in sems:
                sems[name] = sem(name)
            return sems[name]

        loads = [
            (ident[:], t["ident"]), (before_tok[:], t["before_tok"]), (pick[:], t["pick"]),
            (rank_w[:], t["rank_w"]), (wg1[:], t["wg1"]),
            (w_in[:], t["w_in"]), (tap_b[:], t["taps"].partition_broadcast(P)),
            (w_x[:], t["w_x"]), (w_dt[:], t["w_dt"]), (w_out[:], t["w_out"]), (chan[:], t["chan"]),
            (a_log[:], t["a_log"].partition_broadcast(P)), (wg0[:], t["wg0"]), (w_e0[:], t["w_e0"]),
            (b_e0[:], t["b_e0"]),
        ]
        N_LOADS = 16 * len(loads)
        loads1 = [
            (cos[:], t["cos"]), (sin[:], t["sin"]), (w_qk[:], t["w_qk"]), (b_qk[:], t["b_qk"]), (w_v[:], t["w_v"]),
            (b_v[:], t["b_v"].partition_broadcast(P)), (w_o[:], t["w_o"]),
            (q_op[72:PARTS], t["q_tail"]), (k_op[72:PARTS], t["k_tail"]),
        ]
        N_LOADS1 = 16 * len(loads1)
        HID_AHEAD = 8
        EXP_AHEAD = 5
        TILE = (0, 1, 2, 0, 1, 2, 0, 1)
        LAG = (2, 2, 5, 3, 3, 3, 3, 3)
        conv_b, b_dt, ln_g, ln_b, d_par = (chan[:, i, :] for i in range(5))

        def alone(engine):
            engine.sem_inc(S("passed"), 1)

        block = ctx.enter_context(nc.Block())

        @block.sync
        def _(sp):
            for b in range(B):
                sp.dma_start(x_all[:, b], t["x"][b].rearrange("(k p) d -> p k d", p=P)).then_inc(S("x_loaded"), 16)
            for dst, src in loads:
                sp.dma_start(dst, src).then_inc(S("w_loaded"), 16)

            sp.wait_ge(S("probs_ready"), 2 * B)
            for dst, src in loads1:
                sp.dma_start(dst, src).then_inc(S("w1_loaded"), 16)

            def store_parts(b, i):
                sp.wait_ge(S("qk_parts_ready"), 2 * b + i + 1)
                sp.dma_start(parts_dram[i].rearrange("j p t -> p j t"), qk_parts[i]).then_inc(S("parts_stored"), 16)

            with sp.Fori(0, B) as b:
                sp.wait_ge(S("pv_done"), b * 32 + 2)
                sp.dma_start(q_op[72:75], t["q_tail"][0:3]).then_inc(S("ops_loaded"), 16)
                store_parts(b, 0)
                store_parts(b, 1)
                sp.wait_ge(S("parts_stored"), 32 * b + 32)
                for i in range(3):
                    for j in range(3):
                        r = (3 * i + j) * HD
                        sp.dma_start(q_op[r:r + HD], parts_dram[0, i].rearrange("(h d) t -> d h t", d=HD)).then_inc(S("ops_loaded"), 16)
                        sp.dma_start(k_op[r:r + HD], parts_dram[1, j].rearrange("(h d) t -> d h t", d=HD)).then_inc(S("ops_loaded"), 16)
                sp.wait_ge(S("top_parts_ready"), b + 1)
                sp.dma_start(top_dram.rearrange("j r q -> r j q"), top_parts[:]).then_inc(S("top_stored"), 16)
                sp.wait_ge(S("top_stored"), 16 * b + 16)
                sp.dma_start(q_op[72:75], top_dram.rearrange("j (h k) q -> j h (k q)", h=H)).then_inc(S("top_loaded"), 16)
                with sp.Fori(0, E // 2) as e2:
                    for i in range(2):
                        e = e2 * 2 + i
                        sp.wait_ge(S("hid_used"), 4 * (b * E + e) - 4 + HID_AHEAD)
                        sp.dma_start(w1[i][:], t["w1"][e]).then_inc(S(f"expert_loaded{i}"), 16)
                        sp.dma_start(w2[i][:], t["w2"][e].rearrange("(m p) d -> p m d", p=P)).then_inc(S(f"expert_loaded{i}"), 16)
                sp.wait_ge(S("out_ready"), b + 1)
                sp.dma_start(out[b].rearrange("(k p) d -> p k d", p=P), x_all[:, b]).then_inc(S("stored"), 16)
            sp.wait_ge(S("stored"), 16 * B)

        @block.gpsimd
        def _(pool):
            pool.wait_ge(S("w_loaded"), N_LOADS)
            for k in range(TAPS):
                i = nc.gpsimd.tensor_tensor(w_tap[:, k, :], w_in[:, 0:DI], tap_b[:, k, :], ALU.mult)
            i.then_inc(S("taps_ready"), 1)
            pool.sem_inc(S("hc_ready"), 2)

            def times_c(i, n):
                pool.wait_ge(S("scanned"), n + 3)
                pool.wait_ge(S("c_ready"), n + 2)
                pool.wait_ge(S("summed"), n + 1)
                nc.gpsimd.tensor_tensor(hc[i][:, 1], hs[i][:, 1], c_sb[i][:], ALU.mult).then_inc(S("hc_ready"), 1)

            with pool.Fori(0, B) as b:
                pool.wait_ge(S("u1_ready"), b + 1)
                nc.gpsimd.tensor_tensor(hc[0][:], hs[1][:], dA[0][:], ALU.subtract).then_inc(S("lost_ready"), 1)
                with pool.Fori(0, NS // 2) as s2:
                    for i in range(2):
                        times_c(i, b * NS + s2 * 2 + i)

        @block.scalar
        def _(act):
            A = nc.scalar.activation
            act.wait_ge(S("w_loaded"), N_LOADS)
            A(a_exp[:], a_log[:], ACT.Exp).then_inc(S("a_exp_ready"), 1)
            act.sem_inc(S("c_ready"), 1)
            act.wait_ge(S("setup"), 1)

            def decay(i, s, n):
                act.wait_ge(S("scanned"), n + 1)
                act.wait_ge(S("dt_seen"), 1)
                A(dA[i][:, :, 1:], dt_[:, :, 1:], ACT.Exp, scale=a_neg[:, bass.ds(s, 1)]).then_inc(S("decay_ready"), 1)

            def keep_c(i, n):
                act.wait_ge(S("c_ps"), n + 1)
                act.wait_ge(S("hc_ready"), n + 1)
                A(c_sb[i][:], banks(2, 2), ACT.Copy).then_inc(S("c_ready"), 1)

            with act.Fori(0, B) as b:
                act.wait_ge(S("var_ready"), 2 * b + 1)
                A(std[:], mv[:, :, 1], ACT.Sqrt, bias=eps_col[:]).then_inc(S("std_ready"), 1)
                act.wait_ge(S("xnT_ps"), 2 * b + 1)
                A(xnT[:, TAPS - 1:], banks(0, 2), ACT.Copy).then_inc(S("xnT_ready"), 1)
                act.wait_ge(S("z_ps"), b + 1)
                A(zs[:].rearrange("p h t -> p (h t)"), banks(2, 4), ACT.Silu).then_inc(S("zs_ready"), 1)
                act.wait_ge(S("conv_ps"), 2 * b + 1)
                A(xc[:, 1, :], banks(6, 2), ACT.Silu, bias=conv_b[:, 1:2]).then_inc(S("xc_ready"), 1)
                act.wait_ge(S("conv_ps"), 2 * b + 2)
                A(xc[:, 0, :], banks(0, 2), ACT.Silu, bias=conv_b[:, 0:1]).then_inc(S("xc_ready"), 1)
                act.wait_ge(S("lg_ready"), 2 * b + 1)
                A(ex[:], lg[:], ACT.Exp).then_inc(S("ex_ready"), 1)
                act.wait_ge(S("dt_ps"), b + 1)
                for h in range(NH2):
                    A(dt_[:, h, :], banks(2 + 2 * h, 2), ACT.Abs, bias=b_dt[:, h:h + 1]).then_inc(S("abs_ready"), 1)
                act.wait_ge(S("bc_ps"), b + 1)
                A(bc[:], banks(0, 2, PARTS), ACT.Copy).then_inc(S("part1"), 1)
                act.wait_ge(S("abs_ready"), 2 * b + 2)
                A(dA[0][:], dt_[:], ACT.Exp, scale=-1.0).then_inc(S("u_ready"), 1)
                act.wait_ge(S("u_ready"), b + 1)
                A(dA[1][:], dA[0][:], ACT.Ln, bias=1.0).then_inc(S("ln_ready"), 1)
                act.wait_ge(S("rest_ready"), 2 * b + 1)
                A(bc[32:64, :], rest[32:64, :], ACT.Copy)
                A(mid[64:96, :], rest[64:96, :], ACT.Copy).then_inc(S("part2"), 1)
                act.wait_ge(S("gateT_ps"), b + 1)
                A(gateT[:], banks(0, 2, E), ACT.Copy)
                A(gparts[:], banks(0, 2, PARTS), ACT.Copy).then_inc(S("part1"), 1)
                act.wait_ge(S("rest_ready"), 2 * b + 2)
                A(gparts[32:64, :], rest[32:64, :], ACT.Copy)
                A(mid[64:96, :], rest[64:96, :], ACT.Copy).then_inc(S("part2"), 1)
                act.wait_ge(S("ffn_done"), b * E + E + 2)
                A(s_gT[:], banks(6, 2), ACT.Silu).then_inc(S("s_g_ready"), 1)
                act.wait_ge(S("dt_ready"), b + 1)
                with act.Fori(0, NS // 2) as s2:
                    for i in range(2):
                        decay(i, s2 * 2 + i, b * NS + s2 * 2 + i)
                        keep_c(i, b * NS + s2 * 2 + i)
                act.wait_ge(S("summed"), b * NS + NS + 2)
                A(hs[0][:].rearrange("p h t -> p (h t)"), banks(4, 4), ACT.Copy).then_inc(S("y_ready"), 1)
                act.wait_ge(S("yc_ready"), b + 1)
                A(dA[0][:], hs[1][:], ACT.Square).then_inc(S("sq_ready"), 1)
                act.wait_ge(S("yvar_ps"), b + 1)
                A(c_sb[0][:], banks(2, 2), ACT.Ln, bias=eps_col[:]).then_inc(S("lnvar"), 1)
                act.wait_ge(S("lnvar"), b + 1)
                A(c_sb[1][:], c_sb[0][:], ACT.Exp, scale=-0.5).then_inc(S("yrstd_ready"), 1)
                act.wait_ge(S("yn_ready"), b + 1)
                for h in range(NH2):
                    i = A(hc[1][:, h, :], hc[0][:, h, :], ACT.Identity, scale=ln_g[:, h:h + 1], bias=ln_b[:, h:h + 1])
                i.then_inc(S("yg_ready"), 1)
                act.wait_ge(S("var_ready"), 2 * b + 2)
                A(std[:], mv[:, :, 1], ACT.Sqrt, bias=eps_col[:]).then_inc(S("std_ready"), 1)
                act.wait_ge(S("xnT_ps"), 2 * b + 2)
                A(xnT[:, TAPS - 1:], banks(0, 2), ACT.Copy).then_inc(S("xnT_ready"), 1)
                act.wait_ge(S("lg_ready"), 2 * b + 2)
                A(ex[:], lg[:], ACT.Exp).then_inc(S("ex_ready"), 1)
            act.sem_inc(S("hid_ready"), 2)
            act.sem_inc(S("gate_sb_ready"), 1)

            act.wait_ge(S("w1_loaded"), N_LOADS1)

            with act.Fori(0, B) as b:
                for i in range(2):
                    act.wait_ge(S("rot_ready"), 2 * b + i + 1)
                    A(qk_parts[i][:, 0, :], rot[i][0], ACT.Copy).then_inc(S("qk_part1"), 1)
                for i in range(2):
                    act.wait_ge(S("qk_rest"), 2 * b + i + 1)
                    A(qk_parts[i][:, 1, :], rot[i][1], ACT.Copy).then_inc(S("qk_part2"), 1)
                with act.Fori(0, H) as h:
                    for k in range(NBLK):
                        n = b * P + h * NBLK + k
                        act.wait_ge(S("s_ps"), n + 1)
                        act.wait_ge(S("top_done"), n + 3)
                        A(half_sb[k % 2], ps[:, 2 * (k % 4) + 1, :], ACT.Copy).then_inc(S("s_half"), 1)
                act.wait_ge(S("top_ps"), b + 1)
                A(top_parts[:, 0, :], ps[:, 0, 0:P], ACT.Copy).then_inc(S("top_part1"), 1)
                act.wait_ge(S("top_rest_ready"), b + 1)
                A(top_parts[:, 1, :], top_rest[:], ACT.Copy).then_inc(S("top_part2"), 1)
                def exps(i, m):
                    act.wait_ge(S("pv_done"), m + 1)
                    for j in range(HG):
                        act.wait_ge(S("sT_ps"), m * HG + j + 1)
                        A(big[i][:, j, :], banks(2 * TILE[i * HG + j], 2), ACT.Exp, scale=HD ** -0.5).then_inc(S("exp_done"), 1)

                def keep_o(ng):
                    act.wait_ge(S("pv_done"), ng * 8 + 8 + 2)
                    A(o_T[:], banks(6, 2), ACT.Copy).then_inc(S("o_ready"), 1)

                def exp_group(g, first=False):
                    m0 = (b * 4 + g) * 8
                    exps(0, m0)
                    if not first:
                        keep_o(b * 4 + g - 1)
                    exps(1, m0 + 1)
                    with act.Fori(1, NBLK // 2) as k2:
                        for i in range(2):
                            exps(i, m0 + k2 * 2 + i)
                exp_group(0, first=True)
                with act.Fori(1, H // HG) as g:
                    exp_group(g)
                keep_o(b * 4 + 3)
                act.wait_ge(S("attT_ps"), b + 1)
                A(attT[:], banks(0, 2), ACT.Copy).then_inc(S("attT_ready"), 1)
                act.wait_ge(S("s1_ps"), b + 1)
                A(s1T[:], banks(2, 2), ACT.Identity, bias=b_qk[:, 4:5]).then_inc(S("s1_ready"), 1)
                act.wait_ge(S("gpadT_ps"), b + 1)
                A(gparts1[:], banks(0, 2, PARTS), ACT.Copy).then_inc(S("gpart1"), 1)
                act.wait_ge(S("grest_ready"), b + 1)
                A(gparts1[32:64, :], grest[32:64, :], ACT.Copy)
                A(gmid[64:96, :], grest[64:96, :], ACT.Copy).then_inc(S("gpart2"), 1)
                with act.Fori(0, E // 2) as e2:
                    for i in range(2):
                        n = b * E + e2 * 2 + i
                        act.wait_ge(S("gate1_ps"), n + 1)
                        act.wait_ge(S("acc_done"), 2 * n + 2)
                        A(gate_sb[i], banks(0, 2), ACT.Copy).then_inc(S("gate_sb_ready"), 1)
                        for u in range(4):
                            act.wait_ge(S("hid_ps"), 4 * n + u + 1)
                            act.wait_ge(S("hid_used"), 4 * n + u - 3 + HID_AHEAD)
                            A(hid[u], banks(2 + 2 * (u % 2), 2), ACT.Gelu_apprx_tanh).then_inc(S("hid_ready"), 1)
                act.wait_ge(S("acc_done"), 2 * E * b + 2 * E + 4)
                A(acc_bf[:], acc[:], ACT.Copy).then_inc(S("acc_bf_ready"), 1)
                act.wait_ge(S("acc_bf_ready"), b + 1)
                A(silu_bf[:], acc_bf[:], ACT.Silu).then_inc(S("silu_ready"), 1)

        @block.vector
        def _(dve):
            V = nc.vector
            V.memset(eps_col[:], EPS)
            V.memset(ones_bf[:], 1.0)
            V.memset(zeros_bf[:], 0.0)
            V.memset(mean_w[:], 1.0 / DI)
            V.memset(xnT[:, 0:TAPS - 1], 0.0)
            V.memset(gate0[:], 0.0)
            V.memset(taken[:], 0.0)
            dve.wait_ge(S("a_exp_ready"), 1)
            V.tensor_scalar(a_neg[:], a_exp[:], -1.0, None, ALU.mult).then_inc(S("setup"), 1)
            dve.sem_inc(S("scanned"), 2)
            dve.sem_inc(S("b_used"), 1)
            dve.sem_inc(S("c_used"), 1)
            dve.sem_inc(S("parts_ready"), 1)
            dve.sem_inc(S("dt_seen"), 1)
            dve.wait_ge(S("x_loaded"), 16 * B)
            dve.wait_ge(S("w_loaded"), N_LOADS)
            def norm(b, n):
                for k in range(NBLK):
                    i = V.bn_stats(bn[:, k, :], x_all[:, b, k, :])
                i.then_inc(S("stats_ready"), 1)
                dve.wait_ge(S("stats_ready"), n + 1)
                alone(dve)
                for k in range(NBLK):
                    i = V.bn_aggr(mv[:, k, :], bn[:, k, :])
                i.then_inc(S("var_ready"), 1)
                dve.wait_ge(S("std_ready"), n + 1)
                V.reciprocal(rstd[:], std[:]).then_inc(S("rstd_ready"), 1)
                dve.wait_ge(S("rstd_ready"), n + 1)
                for k in range(NBLK):
                    i = V.tensor_scalar(xn[:, k, :], x_all[:, b, k, :], mv[:, k, 0:1], rstd[:, k:k + 1],
                                        ALU.subtract, ALU.mult)
                i.then_inc(S("xn_ready"), 1)

            def router(b, n, bank, result):
                logits = ps[:, bank, 0:NBLK * E].rearrange("p (k e) -> p k e", e=E)
                dve.wait_ge(S("lg_ps"), n + 1)
                V.tensor_reduce(m8[:], logits, AX_X, ALU.max).then_inc(S("m8_ready"), 1)
                dve.wait_ge(S("m8_ready"), n + 1)
                V.tensor_tensor(lg[:], logits, over(m8[:], 2, E), ALU.subtract).then_inc(S("lg_ready"), 1)
                dve.wait_ge(S("ex_ready"), n + 1)
                V.tensor_reduce(s8[:], ex[:], AX_X, ALU.add).then_inc(S("s8_ready"), 1)
                dve.wait_ge(S("s8_ready"), n + 1)
                V.reciprocal(r8[:], s8[:]).then_inc(S("r8_ready"), 1)
                dve.wait_ge(S("r8_ready"), n + 1)
                V.tensor_tensor(result, ex[:], over(r8[:], 2, E), ALU.mult).then_inc(S("probs_ready"), 1)
                dve.wait_ge(S("probs_ready"), n + 1)

            def remainders(parts, n):
                dve.wait_ge(S("part1"), n + 1)
                dve.wait_ge(S("parts_ready"), n + 1)
                V.tensor_tensor(rest[:], banks(0, 2, PARTS), parts[:], ALU.subtract).then_inc(S("rest_ready"), 1)
                dve.wait_ge(S("rest_ready"), n + 1)
                dve.wait_ge(S("part2"), n + 1)
                V.tensor_tensor(parts[64:96, :], rest[64:96, :], mid[64:96, :], ALU.subtract).then_inc(S("parts_ready"), 1)

            def times_c(i, n):
                dve.wait_ge(S("c_ready"), n + 2)
                dve.wait_ge(S("summed"), n + 1)
                dve.wait_ge(S("scanned"), n + 3)
                V.tensor_tensor(hc[i][:, 0], hs[i][:, 0], banks(2, 2), ALU.mult).then_inc(S("c_used"), 1)

            def scan_step(i, n, first=False):
                dve.wait_ge(S("b_ps"), n + 1)
                dve.wait_ge(S("hc_ready"), n + 1)
                dve.wait_ge(S("c_used"), n)
                V.tensor_tensor(hs[i][:], dtx[:], over(banks(0, 2), 1, NH2), ALU.mult).then_inc(S("b_used"), 1)
                if not first:
                    times_c(1 - i, n - 1)
                dve.wait_ge(S("b_used"), n + 2)
                dve.wait_ge(S("decay_ready"), n + 1)
                h = hs[i][:].rearrange("p h t -> p (h t)")
                V.tensor_tensor_scan(h, dA[i][:].rearrange("p h t -> p (h t)"), h, 0.0,
                                     ALU.mult, ALU.add).then_inc(S("scanned"), 1)

            with dve.Fori(0, B) as b:
                norm(b, 2 * b)
                router(b, 2 * b, 0, probs0[:])
                V.tensor_reduce(pmax[:], probs0[:], AX_X, ALU.max).then_inc(S("pmax_ready"), 1)
                dve.wait_ge(S("pmax_ready"), b + 1)
                V.tensor_tensor(eqw[:], probs0[:], over(pmax[:], 2, E), ALU.is_equal).then_inc(S("eq_ready"), 1)
                dve.wait_ge(S("eq_ready"), b + 1)
                V.tensor_tensor(eqw[:], eqw[:], over(rank_w[:], 1, NBLK), ALU.mult).then_inc(S("eqw_ready"), 1)
                dve.wait_ge(S("eqw_ready"), b + 1)
                V.tensor_reduce(first[:], eqw[:], AX_X, ALU.max).then_inc(S("first_ready"), 1)
                dve.wait_ge(S("first_ready"), b + 1)
                V.tensor_tensor(choice_bf[:], eqw[:], over(first[:], 2, E), ALU.is_equal).then_inc(S("choice_ready"), 1)
                V.tensor_tensor(choice[:], eqw[:], over(first[:], 2, E), ALU.is_equal).then_inc(S("choice_f32_ready"), 1)
                dve.wait_ge(S("pos_ps"), b + 1)
                V.tensor_tensor(pos[:], ps[:, 6, 0:NBLK * E].rearrange("p (k e) -> p k e", e=E),
                                over(taken[:], 1, NBLK), ALU.add).then_inc(S("pos_ready"), 1)
                dve.wait_ge(S("pos_ready"), b + 1)
                dve.wait_ge(S("choice_f32_ready"), b + 1)
                V.scalar_tensor_tensor(kept[:], pos[:], float(CAP0), choice[:], ALU.is_lt, ALU.mult).then_inc(S("kept_ready"), 1)
                V.tensor_tensor(taken[:], taken[:], ps[:, 7, 0:E], ALU.add)
                dve.wait_ge(S("kept_ready"), b + 1)
                for g in range(3):
                    i = V.tensor_tensor(gate0[:, :, 32 * g:32 * g + E], kept[:], probs0[:], ALU.mult)
                i.then_inc(S("gate0_ready"), 1)
                for h in range(NH2):
                    dve.wait_ge(S("abs_ready"), 2 * b + 1 + h)
                    i = V.tensor_scalar(hs[0][:, h, :], banks(2 + 2 * h, 2), b_dt[:, h:h + 1], 0.0, ALU.add, ALU.max)
                i.then_inc(S("relu_ready"), 1)
                remainders(bc, 2 * b)
                dve.wait_ge(S("u_ready"), b + 1)
                V.tensor_scalar(hs[1][:], dA[0][:], 1.0, -1.0, ALU.add, ALU.add).then_inc(S("u1_ready"), 1)
                remainders(gparts, 2 * b + 1)
                dve.wait_ge(S("ln_ready"), b + 1)
                V.tensor_tensor(hs[0][:], hs[0][:], dA[1][:], ALU.add).then_inc(S("relu_ln_ready"), 1)
                dve.wait_ge(S("lost_ready"), b + 1)
                dve.wait_ge(S("relu_ln_ready"), b + 1)
                for i in range(2):
                    V.memset(dA[i][:, :, 0:1], 0.0)
                V.tensor_tensor(dt_[:], hs[0][:], hc[0][:], ALU.subtract).then_inc(S("dt_ready"), 1)
                dve.wait_ge(S("dt_ready"), b + 1)
                V.tensor_tensor(dtx[:], dt_[:], xc[:], ALU.mult).then_inc(S("dtx_ready"), 1)
                for e in range(E):
                    dve.wait_ge(S("gate_ps"), b * E + e + 1)
                    dve.wait_ge(S("ffn_done"), b * E + e + 1)
                    V.tensor_tensor(xg[e % 2][:], xnT[:, TAPS - 1:], banks(2 + 2 * (e % 2), 2), ALU.mult).then_inc(S("xg_ready"), 1)
                scan_step(0, b * NS, first=True)
                scan_step(1, b * NS + 1)
                with dve.Fori(1, NS // 2) as s2:
                    for i in range(2):
                        scan_step(i, b * NS + s2 * 2 + i)
                times_c(1, b * NS + NS - 1)
                dve.wait_ge(S("ymean_ps"), b + 1)
                V.tensor_tensor(hs[1][:], hs[0][:], over(banks(0, 2), 1, NH2), ALU.subtract).then_inc(S("yc_ready"), 1)
                dve.wait_ge(S("yc_ready"), b + 1)
                dve.wait_ge(S("yrstd_ready"), b + 1)
                V.tensor_tensor(hc[0][:], hs[1][:], over(c_sb[1][:], 1, NH2), ALU.mult).then_inc(S("yn_ready"), 1)
                dve.wait_ge(S("yg_ready"), b + 1)
                for h in range(NH2):
                    i = V.scalar_tensor_tensor(hc[0][:, h, :], xc[:, h, :], d_par[:, h:h + 1], hc[1][:, h, :], ALU.mult, ALU.add)
                i.then_inc(S("yd_ready"), 1)
                dve.wait_ge(S("yd_ready"), b + 1)
                V.tensor_tensor(hc[1][:], hc[0][:], zs[:], ALU.mult).then_inc(S("mix_ready"), 1)
                dve.wait_ge(S("s0_ps"), b + 1)
                V.tensor_tensor(c_sb[0][:], s_gT[:], banks(0, 2), ALU.mult).then_inc(S("sg_ready"), 1)
                dve.wait_ge(S("sgT_ps"), b + 1)
                V.tensor_tensor(x_all[:, b].rearrange("p k d -> p (k d)"), x_all[:, b].rearrange("p k d -> p (k d)"),
                                banks(2, 2), ALU.add).then_inc(S("x1_ready"), 1)
                dve.wait_ge(S("x1_ready"), b + 1)
                alone(dve)
                norm(b, 2 * b + 1)
                dve.wait_ge(S("xnT_ready"), 2 * b + 2)
                V.tensor_copy(xn1T_all[:, b, :], xnT[:, TAPS - 1:]).then_inc(S("xn1T_ready"), 1)
                router(b, 2 * b + 1, 2, probs[:, b])

            dve.wait_ge(S("probs_ready"), 2 * B)
            V.memset(thr[:], 0)
            V.memset(bit[:], 1 << ONE_BITS)
            V.memset(gpad[:], 0.0)
            V.memset(v_grp[:], 0.0).then_inc(S("setup1"), 1)
            dve.wait_ge(S("setup1"), 1)
            V.memset(v_grp[:, :, :, HD:HD + 1], 1.0).then_inc(S("setup1"), 1)
            dve.sem_inc(S("top_done"), 4)
            dve.sem_inc(S("top_out"), 2)
            dve.sem_inc(S("acc_done"), 4)
            dve.sem_inc(S("thr_step"), 1)

            def by_block(ap):
                return over(ap, 2, NBLK)
            with dve.Fori(0, ONE_BITS + 1) as i:
                dve.wait_ge(S("thr_step"), i + 1)
                V.tensor_tensor(cand[:], thr[:], bit[:], ALU.bitwise_or).then_inc(S("cand_ready"), 1)
                dve.wait_ge(S("cand_ready"), i + 1)
                V.tensor_tensor(over_thr[:], probs[:], by_block(cand[:].bitcast(F32)), ALU.is_ge).then_inc(S("over_ready"), 1)
                dve.wait_ge(S("count_ps"), i + 1)
                V.scalar_tensor_tensor(step[:], ps[:, 0, 0:B * E].rearrange("p (b e) -> p b e", e=E), float(K1), bit[:],
                                       ALU.is_ge, ALU.mult).then_inc(S("step_ready"), 1)
                dve.wait_ge(S("step_ready"), i + 1)
                V.tensor_scalar(bit[:], bit[:], 1, None, ALU.logical_shift_right)
                V.tensor_tensor(thr[:], thr[:], step[:], ALU.bitwise_or).then_inc(S("thr_step"), 1)
            dve.wait_ge(S("thr_step"), ONE_BITS + 2)
            V.tensor_tensor(at_thr[:], probs[:], by_block(thr[:].bitcast(F32)), ALU.is_equal)
            V.tensor_tensor(over_thr[:], probs[:], by_block(thr[:].bitcast(F32)), ALU.is_gt).then_inc(S("split_ready"), 1)
            dve.wait_ge(S("ranks_ps"), 1)
            V.tensor_scalar(need[:], ps[:, 0, 0:B * E].rearrange("p (b e) -> p b e", e=E), -1.0, float(K1),
                            ALU.mult, ALU.add).then_inc(S("need_ready"), 1)
            dve.wait_ge(S("need_ready"), 1)
            V.tensor_tensor(picked[:], ps[:, 1, 0:B * NBLK * E].rearrange("p (b k e) -> p b k e", b=B, e=E),
                            by_block(need[:]), ALU.is_lt).then_inc(S("need_ready"), 1)
            dve.wait_ge(S("need_ready"), 2)
            V.tensor_tensor(picked[:], picked[:], at_thr[:], ALU.mult).then_inc(S("need_ready"), 1)
            dve.wait_ge(S("need_ready"), 3)
            V.tensor_tensor(picked[:], picked[:], over_thr[:], ALU.add).then_inc(S("need_ready"), 1)
            dve.wait_ge(S("need_ready"), 4)
            V.tensor_tensor(gate1[:], picked[:], probs[:], ALU.mult).then_inc(S("need_ready"), 1)
            dve.wait_ge(S("need_ready"), 5)
            dve.wait_ge(S("w1_loaded"), N_LOADS1)

            with dve.Fori(0, B) as b:
                V.tensor_scalar(xT[:], xn1T_all[:, b, :], 1.0, None, ALU.mult).then_inc(S("xT_ready"), 1)
                for i in range(2):
                    dve.wait_ge(S("qk_ps"), 2 * b + i + 1)
                    V.scalar_tensor_tensor(rot[i][0], banks(4 * i, 2), b_qk[:, 2 * i:2 * i + 1], cos[:], ALU.add, ALU.mult)
                    V.scalar_tensor_tensor(rot[i][1], banks(4 * i + 2, 2), b_qk[:, 2 * i + 1:2 * i + 2], sin[:],
                                           ALU.add, ALU.mult).then_inc(S("halves_ready"), 1)
                    dve.wait_ge(S("halves_ready"), 2 * b + i + 1)
                    V.tensor_tensor(rot[i][0], rot[i][0], rot[i][1], ALU.add).then_inc(S("rot_ready"), 1)
                for i in range(2):
                    dve.wait_ge(S("rot_ready"), 2 * b + i + 1)
                    dve.wait_ge(S("qk_part1"), 2 * b + i + 1)
                    V.tensor_tensor(rot[i][1], rot[i][0], qk_parts[i][:, 0, :], ALU.subtract).then_inc(S("qk_rest"), 1)
                for i in range(2):
                    dve.wait_ge(S("qk_rest"), 2 * b + i + 1)
                    dve.wait_ge(S("qk_part2"), 2 * b + i + 1)
                    V.tensor_tensor(qk_parts[i][:, 2, :], rot[i][1], qk_parts[i][:, 1, :], ALU.subtract).then_inc(S("qk_parts_ready"), 1)
                dve.wait_ge(S("v_ps"), b + 1)
                V.tensor_tensor(v_tok[:], banks(0, 2).rearrange("p (k c) -> p k c", k=NBLK), over(b_v[:], 1, NBLK),
                                ALU.add).then_inc(S("v_ready"), 1)
                with dve.Fori(0, H) as h:
                    for k in range(NBLK):
                        n = b * P + h * NBLK + k
                        dve.wait_ge(S("s_half"), n + 1)
                        if k % 2 == 0:
                            dve.wait_ge(S("top_out"), b * 64 + h * 4 + k // 2 + 1)
                        V.tensor_tensor_scan(top_run[k // 2 % 2][:, k % 2, :], half_sb[k % 2], ps[:, 2 * (k % 4), :], LOWEST,
                                             ALU.max, ALU.max).then_inc(S("top_done"), 1)
                        if k % 2:
                            dve.wait_ge(S("top_done"), n + 5)
                            V.tensor_scalar(top[:, bass.ds(h * NBLK + k - 1, 2)], top_run[k // 2 % 2][:, :, HALF - 1], 1.0,
                                            None, ALU.mult).then_inc(S("top_out"), 1)
                dve.wait_ge(S("top_part1"), b + 1)
                V.tensor_tensor(top_rest[:], ps[:, 0, 0:P], top_parts[:, 0, :], ALU.subtract).then_inc(S("top_rest_ready"), 1)
                dve.wait_ge(S("top_rest_ready"), b + 1)
                dve.wait_ge(S("top_part2"), b + 1)
                V.tensor_tensor(top_parts[:, 2, :], top_rest[:], top_parts[:, 1, :], ALU.subtract).then_inc(S("top_parts_ready"), 1)
                dve.wait_ge(S("v_ready"), b + 1)
                def group_v(g):
                    dve.wait_ge(S("pv_done"), (b * 4 + g) * 8 + 2)
                    V.tensor_scalar(v_grp[:, :, :, 0:HD],
                                    v_tok[:, :, bass.ds(g * HG * HD, HG * HD)].rearrange("p k (j d) -> p k j d", j=HG),
                                    1.0, None, ALU.mult).then_inc(S("v_grp_ready"), 1)

                def divide(g):
                    ng = b * 4 + g
                    dve.wait_ge(S("o_ps"), ng + 1)
                    o = banks(6, 2).rearrange("p (k j c) -> p k j c", k=NBLK, j=HG)
                    V.reciprocal(rsum[:], o[:, :, :, HD]).then_inc(S("rsum_ready"), 1)
                    dve.wait_ge(S("rsum_ready"), ng + 1)
                    V.tensor_tensor(att[:, :, bass.ds(g * HG * HD, HG * HD)].rearrange("p k (j d) -> p k j d", j=HG),
                                    o[:, :, :, 0:HD], over(rsum[:], 3, HD), ALU.mult).then_inc(S("att_ready"), 1)
                group_v(0)
                with dve.Fori(1, H // HG) as g:
                    group_v(g)
                    divide(g - 1)
                divide(3)
                for i in range(3):
                    j = V.tensor_scalar(gpad[:, :, 32 * i:32 * i + E], gate1[:, b], 1.0, None, ALU.mult)
                j.then_inc(S("gpad_ready"), 1)
                dve.wait_ge(S("gpart1"), b + 1)
                V.tensor_tensor(grest, banks(0, 2, PARTS), gparts1[:], ALU.subtract).then_inc(S("grest_ready"), 1)
                dve.wait_ge(S("grest_ready"), b + 1)
                dve.wait_ge(S("gpart2"), b + 1)
                V.tensor_tensor(gparts1[64:96, :], grest[64:96, :], gmid[64:96, :], ALU.subtract).then_inc(S("gparts1_ready"), 1)
                V.memset(acc[:], 0.0).then_inc(S("acc_zero"), 1)
                dve.wait_ge(S("acc_zero"), b + 1)
                alone(dve)
                with dve.Fori(0, E // 2) as e2:
                    for i in range(2):
                        n = b * E + e2 * 2 + i
                        dve.wait_ge(S("gate_sb_ready"), n + 2)
                        for c in range(2):
                            cs = slice(c * HALF, (c + 1) * HALF)
                            dve.wait_ge(S("hid_used"), 4 * n + 2 * c + 2 + HID_AHEAD)
                            dve.wait_ge(S("acc_done"), 2 * n + c + 4)
                            V.tensor_tensor(weighted, ps[:, 6 + c, :], gate_sb[i][:, cs], ALU.mult).then_inc(S("weighted_ready"), 1)
                            dve.wait_ge(S("weighted_ready"), 2 * n + c + 1)
                            V.tensor_tensor(acc[:, cs], acc[:, cs], weighted, ALU.add).then_inc(S("acc_done"), 1)
                dve.wait_ge(S("silu_ready"), b + 1)
                dve.wait_ge(S("s1_ready"), b + 1)
                V.tensor_tensor(o_T[:], s1T[:], silu_bf[:], ALU.mult).then_inc(S("sg1_ready"), 1)
                dve.wait_ge(S("sg1_ps"), b + 1)
                xb = x_all[:, b].rearrange("p k d -> p (k d)")
                V.tensor_tensor(xb, xb, banks(0, 2), ALU.add).then_inc(S("out_ready"), 1)

        @block.tensor
        def _(pe):
            M = nc.tensor.matmul
            pe.wait_ge(S("w_loaded"), N_LOADS)
            pe.wait_ge(S("setup"), 1)
            pe.wait_ge(S("taps_ready"), 1)
            pe.sem_inc(S("summed"), 2)
            pe.sem_inc(S("ffn_done"), 2)
            cols = [slice(c * HALF, (c + 1) * HALF) for c in range(2)]

            def turn(src, bank):
                for k in range(NBLK):
                    i = nc.tensor.transpose(ps[:, bank + k // 4, (k % 4) * P:(k % 4 + 1) * P], src(k), ident[:])
                return i

            def logits(wg, bank):
                for k in range(NBLK):
                    i = M(ps[:, bank, k * E:(k + 1) * E], xnT[:, TAPS - 1 + k * P:TAPS - 1 + (k + 1) * P], wg[:],
                          start=True, stop=True)
                i.then_inc(S("lg_ps"), 1)

            def spread(s, bank, done):
                for c in range(2):
                    i = M(ps[:, bank + c, :], pick[:, s, :], bc[:, cols[c]], start=True, stop=True)
                i.then_inc(S(done), 1)

            def spread_b(s, n):
                pe.wait_ge(S("b_used"), n + 1)
                spread(s, 0, "b_ps")

            def spread_c(s, n):
                pe.wait_ge(S("c_ready"), n + 1)
                pe.wait_ge(S("c_used"), n + 1)
                spread(s + NS, 2, "c_ps")

            def sum_states(i, n):
                pe.wait_ge(S("hc_ready"), n + 3)
                pe.wait_ge(S("c_used"), n + 2)
                for h in range(NH2):
                    for c in range(2):
                        m = M(ps[:, 4 + 2 * h + c, :], ident[:], hc[i][:, h, cols[c]], start=False, stop=False,
                              skip_group_check=True)
                m.then_inc(S("summed"), 1)

            with pe.Fori(0, B) as b:
                pe.wait_ge(S("xn_ready"), 2 * b + 1)
                turn(lambda k: xn[:, k, :], 0).then_inc(S("xnT_ps"), 1)
                pe.wait_ge(S("xnT_ready"), 2 * b + 1)
                for h in range(NH2):
                    for c in range(2):
                        i = M(ps[:, 2 + 2 * h + c, :], w_in[:, DI + h * P:DI + (h + 1) * P],
                              xnT[:, TAPS - 1 + c * HALF:TAPS - 1 + (c + 1) * HALF], start=True, stop=True)
                i.then_inc(S("z_ps"), 1)
                logits(wg0, 0)
                for h, bank in ((1, 6), (0, 0)):
                    if h == 0:
                        pe.wait_ge(S("lg_ready"), 2 * b + 1)
                    for c in range(2):
                        for k in range(TAPS):
                            i = M(ps[:, bank + c, :], w_tap[:, k, h * P:(h + 1) * P],
                                  xnT[:, c * HALF + k:c * HALF + k + HALF], start=(k == 0), stop=(k == TAPS - 1))
                    i.then_inc(S("conv_ps"), 1)
                pe.wait_ge(S("choice_ready"), b + 1)
                pe.wait_ge(S("xc_ready"), 2 * b + 1)
                ch = choice_bf[:].rearrange("p k e -> p (k e)")
                M(ps[:, 6, 0:NBLK * E], before_tok[:], ch, start=True, stop=False, skip_group_check=True)
                for k in range(1, NBLK):
                    M(ps[:, 6, k * E:NBLK * E], ones_bf[:], ch[:, 0:(NBLK - k) * E], start=False, stop=(k == NBLK - 1),
                      skip_group_check=True)
                for k in range(NBLK):
                    i = M(ps[:, 7, 0:E], ones_bf[:], choice_bf[:, k, :], start=(k == 0), stop=(k == NBLK - 1))
                i.then_inc(S("pos_ps"), 1)
                pe.wait_ge(S("xc_ready"), 2 * b + 2)
                pe.wait_ge(S("zs_ready"), b + 1)
                for h in range(NH2):
                    for c in range(2):
                        for k in range(NH2):
                            i = M(ps[:, 2 + 2 * h + c, :], w_dt[:, k, h * P:(h + 1) * P], xc[:, k, cols[c]],
                                  start=(k == 0), stop=(k == NH2 - 1))
                i.then_inc(S("dt_ps"), 1)
                for c in range(2):
                    for k in range(NH2):
                        i = M(ps[0:PARTS, c, :], w_x[:, k, :], xc[:, k, cols[c]], start=(k == 0), stop=(k == NH2 - 1))
                i.then_inc(S("bc_ps"), 1)
                pe.wait_ge(S("gate0_ready"), b + 1)
                pe.wait_ge(S("rest_ready"), 2 * b + 1)
                for k in range(NBLK):
                    i = nc.tensor.transpose(ps[0:PARTS, k // 4, (k % 4) * P:(k % 4 + 1) * P], gate0[:, k, :], ident[:])
                i.then_inc(S("gateT_ps"), 1)
                pe.wait_ge(S("parts_ready"), 2 * b + 3)
                pe.wait_ge(S("relu_ready"), b + 1)
                pe.wait_ge(S("kept_ready"), b + 1)
                for c in range(2):
                    M(ps[:, 6 + c, :], b_e0[:], gateT[:, cols[c]], start=True, stop=False, skip_group_check=True)

                def gate_out(e):
                    if e >= 2:
                        pe.wait_ge(S("xg_ready"), b * E + e - 1)
                    for c in range(2):
                        i = M(ps[:, 2 + 2 * (e % 2) + c, :], pick[:, e, :], gparts[:, cols[c]], start=True, stop=True)
                    i.then_inc(S("gate_ps"), 1)
                gate_out(0)
                for e in range(E):
                    if e + 1 < E:
                        gate_out(e + 1)
                    pe.wait_ge(S("xg_ready"), b * E + e + 1)
                    for c in range(2):
                        i = M(ps[:, 6 + c, :], w_e0[:, e, :], xg[e % 2][:, cols[c]], start=False, stop=(e == E - 1),
                              skip_group_check=True)
                    i.then_inc(S("ffn_done"), 1)
                pe.wait_ge(S("s_g_ready"), b + 1)
                for k in range(4):
                    M(ps[:, 4 + k, :], zeros_bf[:, 0:P], zeros_bf[:], start=True, stop=False, skip_group_check=True)
                n0 = b * NS
                spread_b(0, n0)
                for s in range(2):
                    spread_b(s + 1, n0 + s + 1)
                    spread_c(s, n0 + s)
                with pe.Fori(1, NS // 2 - 1) as s2:
                    for i in range(2):
                        s = s2 * 2 + i
                        spread_b(s + 1, n0 + s + 1)
                        spread_c(s, n0 + s)
                        sum_states(i, n0 + s - 2)
                for s in (NS - 2, NS - 1):
                    if s < NS - 1:
                        spread_b(s + 1, n0 + s + 1)
                    spread_c(s, n0 + s)
                    sum_states(s % 2, n0 + s - 2)
                sum_states(0, n0 + NS - 2)
                sum_states(1, n0 + NS - 1)
                for src, bank, ready, done in ((hs[0], 0, "y_ready", "ymean_ps"), (dA[0], 2, "sq_ready", "yvar_ps")):
                    pe.wait_ge(S(ready), b + 1)
                    for c in range(2):
                        for k in range(NH2):
                            i = M(ps[:, bank + c, :], mean_w[:], src[:, k, cols[c]], start=(k == 0), stop=(k == NH2 - 1))
                    i.then_inc(S(done), 1)
                pe.wait_ge(S("mix_ready"), b + 1)
                for c in range(2):
                    for k in range(NH2):
                        i = M(ps[:, c, :], w_out[:, k, :], hc[1][:, k, cols[c]], start=(k == 0), stop=(k == NH2 - 1))
                i.then_inc(S("s0_ps"), 1)
                pe.wait_ge(S("sg_ready"), b + 1)
                turn(lambda k: c_sb[0][:, k * P:(k + 1) * P], 2).then_inc(S("sgT_ps"), 1)
                pe.wait_ge(S("xn_ready"), 2 * b + 2)
                turn(lambda k: xn[:, k, :], 0).then_inc(S("xnT_ps"), 1)
                pe.wait_ge(S("xnT_ready"), 2 * b + 2)
                pe.wait_ge(S("x1_ready"), b + 1)
                logits(wg1, 2)

            def count(what, bank):
                for k in range(NBLK):
                    i = M(ps[:, bank, 0:B * E].rearrange("p (b e) -> p b e", e=E), ones_bf[:], what[:, :, k, :],
                          start=(k == 0), stop=(k == NBLK - 1))
                return i

            with pe.Fori(0, ONE_BITS + 1) as i:
                pe.wait_ge(S("over_ready"), i + 1)
                count(over_thr, 0).then_inc(S("count_ps"), 1)
            pe.wait_ge(S("split_ready"), 1)
            count(over_thr, 0)
            ranks = ps[:, 1, 0:B * NBLK * E].rearrange("p (b k e) -> p b k e", b=B, e=E)
            M(ranks, before_tok[:], at_thr[:], start=True, stop=False, skip_group_check=True)
            for k in range(1, NBLK):
                i = M(ranks[:, :, k:, :], ones_bf[:], at_thr[:, :, 0:NBLK - k, :], start=False, stop=(k == NBLK - 1),
                      skip_group_check=True)
            i.then_inc(S("ranks_ps"), 1)
            pe.wait_ge(S("w1_loaded"), N_LOADS1)
            pe.wait_ge(S("setup1"), 2)
            pe.wait_ge(S("need_ready"), 5)
            pe.sem_inc(S("pv_done"), 2)
            pe.sem_inc(S("exp_done"), EXP_AHEAD)
            pe.sem_inc(S("hid_used"), HID_AHEAD)

            with pe.Fori(0, B) as b:
                pe.wait_ge(S("xT_ready"), b + 1)
                for i in range(2):
                    for j in range(2):
                        for c in range(2):
                            m = M(ps[:, 4 * i + 2 * j + c, :], w_qk[:, 2 * i + j, :], xT[:, cols[c]], start=True, stop=True)
                    m.then_inc(S("qk_ps"), 1)
                pe.wait_ge(S("halves_ready"), 2 * b + 1)
                for k in range(NBLK):
                    m = M(ps[:, k // 4, (k % 4) * P:(k % 4 + 1) * P], xT[:, k * P:(k + 1) * P], w_v[:], start=True, stop=True)
                m.then_inc(S("v_ps"), 1)
                pe.wait_ge(S("ops_loaded"), 16 * 19 * (b + 1))
                pe.wait_ge(S("v_ready"), b + 1)
                pe.wait_ge(S("halves_ready"), 2 * b + 2)
                alone(pe)
                with pe.Fori(0, H) as h:
                    for k in range(NBLK):
                        pe.wait_ge(S("top_done"), b * P + h * NBLK + k + 1)
                        for c in range(2):
                            m = M(ps[:, 2 * (k % 4) + c, :], q_op[:, h, k * P:(k + 1) * P], k_op[:, h, cols[c]],
                                  start=True, stop=True)
                        m.then_inc(S("s_ps"), 1)
                pe.wait_ge(S("top_out"), b * 64 + 64 + 2)
                nc.tensor.transpose(ps[:, 0, 0:P], top[:], ident[:]).then_inc(S("top_ps"), 1)
                pe.wait_ge(S("top_loaded"), 16 * b + 16)

                def scores(g, k):
                    i = k % 2
                    for j in range(HG):
                        n = ((b * 4 + g) * 8 + k) * HG + j
                        pe.wait_ge(S("exp_done"), n + 1 - LAG[i * HG + j] + EXP_AHEAD)
                        for c in range(2):
                            m = M(ps[:, 2 * TILE[i * HG + j] + c, :], k_op[:, g * HG + j, k * P:(k + 1) * P],
                                  q_op[:, g * HG + j, cols[c]], start=True, stop=True)
                        m.then_inc(S("sT_ps"), 1)

                def sum_values(g, k):
                    pe.wait_ge(S("exp_done"), ((b * 4 + g) * 8 + k) * HG + HG + EXP_AHEAD)
                    for c in range(2):
                        for j in range(HG):
                            m = M(ps[32 * j:32 * j + 32, 6 + c, :], v_grp[:, k, j, :], big[k % 2][:, j, cols[c]],
                                  start=False, stop=False, skip_group_check=True)
                    m.then_inc(S("pv_done"), 1)

                def turn_o(g):
                    pe.wait_ge(S("o_ready"), b * 4 + g + 1)
                    turn(lambda k: o_T[:, k * P:(k + 1) * P], 6).then_inc(S("o_ps"), 1)
                    pe.wait_ge(S("att_ready"), b * 4 + g + 1)

                def score_group(g, first=False):
                    scores(g, 0)
                    if not first:
                        sum_values(g - 1, NBLK - 1)
                    scores(g, 1)
                    if not first:
                        turn_o(g - 1)
                    pe.wait_ge(S("v_grp_ready"), b * 4 + g + 1)
                    for c in range(2):
                        M(ps[:, 6 + c, :], zeros_bf[:, 0:P], zeros_bf[:], start=True, stop=False, skip_group_check=True)
                    sum_values(g, 0)
                    for k in range(2, NBLK):
                        scores(g, k)
                        sum_values(g, k - 1)
                score_group(0, first=True)
                with pe.Fori(1, H // HG) as g:
                    score_group(g)
                sum_values(H // HG - 1, NBLK - 1)
                turn_o(H // HG - 1)
                pe.wait_ge(S("exp_done"), (b + 1) * P + EXP_AHEAD)
                turn(lambda k: att[:, k, :], 0).then_inc(S("attT_ps"), 1)
                pe.wait_ge(S("attT_ready"), b + 1)
                for c in range(2):
                    m = M(ps[:, 2 + c, :], w_o[:], attT[:, cols[c]], start=True, stop=True)
                m.then_inc(S("s1_ps"), 1)
                pe.wait_ge(S("gpad_ready"), b + 1)
                for k in range(NBLK):
                    m = nc.tensor.transpose(ps[0:PARTS, k // 4, (k % 4) * P:(k % 4 + 1) * P], gpad[:, k, :], ident[:])
                m.then_inc(S("gpadT_ps"), 1)
                pe.wait_ge(S("gparts1_ready"), b + 1)
                pe.wait_ge(S("s1_ready"), b + 1)
                alone(pe)
                with pe.Fori(0, E // 2) as e2:
                    n2 = b * E + e2 * 2

                    def hidden(i, u):
                        pe.wait_ge(S("hid_ready"), 4 * (n2 + i) + u + 1 - 2 + 2)
                        for q in range(2):
                            m = M(ps[:, 2 + 2 * (u % 2) + q, :], w1[i][:, (2 * (u % 2) + q) * P:(2 * (u % 2) + q + 1) * P],
                                  xT[:, cols[u // 2]], start=True, stop=True)
                        m.then_inc(S("hid_ps"), 1)

                    def down(i, u):
                        pe.wait_ge(S("hid_ready"), 4 * (n2 + i) + u + 1 + 2)
                        if u % 2 == 0:
                            pe.wait_ge(S("acc_done"), 2 * (n2 + i) + u // 2 + 3)
                        for q in range(2):
                            m = M(ps[:, 6 + u // 2, :], w2[i][:, 2 * (u % 2) + q, :], hid[u][:, cols[q]],
                                  start=(u % 2 == 0 and q == 0), stop=(u % 2 == 1 and q == 1))
                        m.then_inc(S("hid_used"), 1)

                    for i in range(2):
                        pe.wait_ge(S("gate_sb_ready"), n2 + i + 1)
                        for c in range(2):
                            m = M(ps[:, c, :], pick[:, e2 * 2 + i, :], gparts1[:, cols[c]], start=True, stop=True)
                        m.then_inc(S("gate1_ps"), 1)
                        pe.wait_ge(S(f"expert_loaded{i}"), 32 * (b * 4 + e2 + 1))
                        hidden(i, 0)
                        if i:
                            down(0, 3)
                        for u in range(1, 4):
                            hidden(i, u)
                            down(i, u - 1)
                    down(1, 3)
                pe.wait_ge(S("sg1_ready"), b + 1)
                turn(lambda k: o_T[:, k * P:(k + 1) * P], 0).then_inc(S("sg1_ps"), 1)


def rotary_tables():
    inv = (np.float32(1.0) / np.float32(10000.0) ** (np.arange(0, HD, 2, dtype=np.float32) / np.float32(HD)))
    angle = np.arange(T, dtype=np.float32)[None, :] * inv[:, None].astype(np.float32)
    angle = np.tile(np.concatenate([angle, angle]), (H, 1)).astype(np.float32)
    sign = np.where(np.arange(P) % 2 == 0, -1.0, 1.0).astype(np.float32)[:, None]
    return {"cos": np.cos(angle), "sin": sign * np.sin(angle)}


def host_constants():
    i = np.arange(P)
    bf = mybir.dt.np(BF16)
    pick = np.zeros((PARTS, 2 * NS, P), np.float32)
    for s in range(2 * NS):
        for g in range(3):
            pick[32 * g + s, s, :] = 1.0
    return {
        "ident": np.eye(P, dtype=np.float32),
        "before_tok": (i[:, None] < i[None, :]).astype(bf),
        "pick": pick.astype(bf),
        **rotary_tables(),
        "q_tail": np.zeros((PARTS - 72, H, T), bf),
        "k_tail": np.concatenate([-np.ones((3, H, T), bf), np.zeros((PARTS - 75, H, T), bf)]),
        "rank_w": np.tile(np.arange(E, 0, -1, dtype=np.float32), (P, 1)),
    }


def kernel(**inputs):
    import concourse.bacc as bacc
    from concourse.bass_utils import run_bass_kernel_spmd

    a = {k: np.ascontiguousarray(v) for k, v in inputs.items()}

    def halves(w):
        return w.reshape(2, P, -1).transpose(1, 0, 2)

    swap = np.arange(P) ^ 1
    w_x = halves(a["L0_attn_W_x"].T)
    arrays = {
        "x": a["L0_attn_x"],
        "w_in": a["L0_attn_W_in"].T,
        "taps": a["L0_attn_conv_w"][:, 0, :].T,
        "w_x": np.concatenate([w_x, w_x, w_x], axis=2),
        "w_dt": halves(a["L0_attn_W_dt"].T),
        "w_out": halves(a["L0_attn_W_out"].T),
        "chan": np.stack([a["L0_attn_" + n].reshape(2, P).T
                          for n in ("conv_b", "b_dt", "ln_g", "ln_b", "D_param")], axis=1),
        "a_log": a["L0_attn_A_log"],
        "wg0": a["L0_ffn_wg"],
        "w_e0": a["L0_ffn_W"].transpose(2, 0, 1),
        "b_e0": a["L0_ffn_b"],
        "wg1": a["L1_ffn_gate_w"],
        "w_qk": np.stack([w.T for w in (a["L1_attn_Wq"], a["L1_attn_Wq"][swap], a["L1_attn_Wk"], a["L1_attn_Wk"][swap])],
                         axis=1),
        "b_qk": np.stack([a["L1_attn_bq"], a["L1_attn_bq"][swap], a["L1_attn_bk"], a["L1_attn_bk"][swap],
                          a["L1_attn_bo"]], axis=1),
        "w_v": a["L1_attn_Wv"].T,
        "b_v": a["L1_attn_bv"],
        "w_o": a["L1_attn_Wo"].T,
        "w1": a["L1_ffn_w1"],
        "w2": a["L1_ffn_w2"],
        **host_constants(),
    }
    nc = bacc.Bacc("TRN2", target_bir_lowering=False, num_devices=1)
    arrays = {f"in_{k}": np.ascontiguousarray(v) for k, v in arrays.items()}
    aps = {k[3:]: nc.dram_tensor(k, v.shape, mybir.dt.from_np(v.dtype), kind="ExternalInput").ap()
           for k, v in arrays.items()}
    out = nc.dram_tensor("out", (B, T, D), F32, kind="ExternalOutput").ap()
    mixed_layers(nc, aps, out)
    r = run_bass_kernel_spmd(nc, [arrays], core_ids=[0])
    return r.results[0]["out"]
```

```python
from contextlib import ExitStack

import numpy as np

import concourse.bass as bass
from concourse import mybir

F32 = mybir.dt.float32
BF16 = mybir.dt.bfloat16
I32 = mybir.dt.int32
ALU = mybir.AluOpType
ACT = mybir.ActivationFunctionType
AX_X = mybir.AxisListType.X

P = 128
B, T, D = 4, 1024, 128
NBLK = T // P
HALF = T // 2
DI, NH2 = 256, 2
NS = 16
TAPS = 4
E = 8
CAP0 = B * T // E
K1 = 2 * T // E
H, HD = 16, 8
HG = 4
HID = 512
EPS = 1e-5
PARTS = 96
LOWEST = float(np.finfo(np.float32).min)
ONE_BITS = 29


def mixed_layers(nc, t, out):
    with ExitStack() as ctx:
        def sb(name, shape, dt=F32, stack=ctx):
            return stack.enter_context(nc.sbuf_tensor(name, shape, dt))

        def sem(name):
            return ctx.enter_context(nc.semaphore(name))

        ps = ctx.enter_context(nc.psum_tensor("ps", [P, 8, HALF], F32))

        def banks(b, n, parts=P):
            return ps[0:parts, b:b + n, :].rearrange("p b c -> p (b c)")

        def over(ap, axis, n):
            v = ap.unsqueeze(axis)
            shape = list(v.shape)
            shape[axis] = n
            return v.broadcast_to(shape)

        ident = sb("ident", [P, P])
        before_tok = sb("before_tok", [P, P], BF16)
        ones_bf = sb("ones_bf", [P, P], BF16)
        zeros_bf = sb("zeros_bf", [P, HALF], BF16)
        pick = sb("pick", [PARTS, 2 * NS, P], BF16)
        rank_w = sb("rank_w", [P, E])
        eps_col = sb("eps_col", [P, 1])
        wg1 = sb("wg1", [P, E])
        x_all = sb("x_all", [P, B, NBLK, D])
        xn1T_all = sb("xn1T_all", [P, B, T])
        probs = sb("probs", [P, B, NBLK, E])
        gate1 = sb("gate1", [P, B, NBLK, E])
        bn = sb("bn", [P, NBLK, 6])
        mv = sb("mv", [P, NBLK, 2])
        std = sb("std", [P, NBLK])
        rstd = sb("rstd", [P, NBLK])
        xn = sb("xn", [P, NBLK, D])
        lg = sb("lg", [P, NBLK, E])
        ex = sb("ex", [P, NBLK, E])
        m8 = sb("m8", [P, NBLK])
        s8 = sb("s8", [P, NBLK])
        r8 = sb("r8", [P, NBLK])

        l0 = ExitStack()
        def sb0(name, shape, dt=F32):
            return sb(name, shape, dt, l0)
        w_in = sb0("w_in", [P, 2 * DI])
        tap_b = sb0("tap_b", [P, TAPS, DI])
        w_tap = sb0("w_tap", [P, TAPS, DI])
        w_x = sb0("w_x", [P, NH2, PARTS])
        w_dt = sb0("w_dt", [P, NH2, DI])
        w_out = sb0("w_out", [P, NH2, D])
        chan = sb0("chan", [P, 5, NH2])
        mean_w = sb0("mean_w", [P, P])
        a_log = sb0("a_log", [P, NS])
        a_exp = sb0("a_exp", [P, NS])
        a_neg = sb0("a_neg", [P, NS])
        wg0 = sb0("wg0", [P, E])
        w_e0 = sb0("w_e0", [P, E, D])
        b_e0 = sb0("b_e0", [E, D])
        taken = sb0("taken", [P, E])
        xnT = sb0("xnT", [P, TAPS - 1 + T])
        zs = sb0("zs", [P, NH2, T])
        xc = sb0("xc", [P, NH2, T])
        dt_ = sb0("dt_", [P, NH2, T])
        dtx = sb0("dtx", [P, NH2, T])
        bc = sb0("bc", [PARTS, T], BF16)
        mid = sb0("mid", [PARTS, T], BF16)
        rest = sb0("rest", [PARTS, T])
        dA = [sb0(f"dA{i}", [P, NH2, T]) for i in range(2)]
        hs = [sb0(f"hs{i}", [P, NH2, T]) for i in range(2)]
        hc = [sb0(f"hc{i}", [P, NH2, T]) for i in range(2)]
        c_sb = [sb0(f"c_sb{i}", [P, T]) for i in range(2)]
        probs0 = sb0("probs0", [P, NBLK, E])
        pmax = sb0("pmax", [P, NBLK])
        eqw = sb0("eqw", [P, NBLK, E])
        first = sb0("first", [P, NBLK])
        choice = sb0("choice", [P, NBLK, E])
        choice_bf = sb0("choice_bf", [P, NBLK, E], BF16)
        pos = sb0("pos", [P, NBLK, E])
        kept = sb0("kept", [P, NBLK, E])
        gate0 = sb0("gate0", [P, NBLK, PARTS])
        gateT = sb0("gateT", [E, T])
        gparts = sb0("gparts", [PARTS, T], BF16)
        s_gT = sb0("s_gT", [P, T])
        xg = [sb0(f"xg{i}", [P, T]) for i in range(2)]
        l0.close()

        cos = sb("cos", [P, T])
        sin = sb("sin", [P, T])
        w_qk = sb("w_qk", [P, 4, P])
        b_qk = sb("b_qk", [P, 5])
        w_v = sb("w_v", [P, P])
        b_v = sb("b_v", [P, P])
        w_o = sb("w_o", [P, P])
        xT = sb("xT", [P, T])
        q_op = sb("q_op", [PARTS, H, T], BF16)
        k_op = sb("k_op", [PARTS, H, T], BF16)
        big = [sb(f"big{i}", [P, HG, T]) for i in range(2)]
        v_tok = sb("v_tok", [P, NBLK, P])
        v_grp = sb("v_grp", [P, NBLK, HG, 32])
        top = sb("top", [P, H * NBLK])
        top_parts = sb("top_parts", [P, 3, P], BF16)
        top_rest = sb("top_rest", [P, P])
        o_T = sb("o_T", [P, T])
        rsum = sb("rsum", [P, NBLK, HG])
        att = sb("att", [P, NBLK, P])
        attT = sb("attT", [P, T])
        s1T = sb("s1T", [P, T])
        w1 = [sb(f"w1_{i}", [P, HID]) for i in range(2)]
        w2 = [sb(f"w2_{i}", [P, HID // P, D]) for i in range(2)]
        acc_bf = sb("acc_bf", [P, T], BF16)
        silu_bf = sb("silu_bf", [P, T], BF16)
        gpad = sb("gpad", [P, NBLK, PARTS])
        gparts1 = sb("gparts1", [PARTS, T], BF16)
        thr = sb("thr", [P, B, E], I32)
        bit = sb("bit", [P, B, E], I32)
        cand = sb("cand", [P, B, E], I32)
        step = sb("step", [P, B, E], I32)
        over_thr = sb("over_thr", [P, B, NBLK, E], BF16)
        at_thr = sb("at_thr", [P, B, NBLK, E], BF16)
        need = sb("need", [P, B, E])
        picked = sb("picked", [P, B, NBLK, E])
        flat = [t_[:].rearrange("p h t -> p (h t)") for t_ in big]
        rot = [flat[0][:, j * T:(j + 1) * T] for j in range(2)]
        qk_parts = [f[:, n:n + 3 * T // 2].bitcast(BF16).rearrange("p (j t) -> p j t", j=3)
                    for f, n in ((flat[0], 2 * T), (flat[1], 0))]
        hid = [flat[1][:, 3 * HALF + j * HALF:3 * HALF + (j + 1) * HALF] for j in range(4)]
        weighted = flat[1][:, 7 * HALF:8 * HALF]
        top_run = [flat[0][:, j * T:(j + 1) * T].rearrange("p (k t) -> p k t", k=2) for j in range(2)]
        half_sb = [flat[0][:, 2 * T + j * HALF:2 * T + (j + 1) * HALF] for j in range(2)]
        gate_sb = [o_T[:, j * HALF:(j + 1) * HALF] for j in range(2)]
        grest = s1T[0:PARTS, :]
        gmid = att[0:PARTS].rearrange("p k c -> p (k c)").bitcast(BF16)[:, 0:T]
        acc = attT
        parts_dram = nc.dram_tensor("parts_dram", (2, 3, P, T), BF16, kind="Internal").ap()
        top_dram = nc.dram_tensor("top_dram", (3, H * NBLK, P), BF16, kind="Internal").ap()

        sems = {}

        def S(name):
            if name not in sems:
                sems[name] = sem(name)
            return sems[name]

        loads = [
            (ident[:], t["ident"]), (before_tok[:], t["before_tok"]), (pick[:], t["pick"]),
            (rank_w[:], t["rank_w"]), (wg1[:], t["wg1"]),
            (w_in[:], t["w_in"]), (tap_b[:], t["taps"].partition_broadcast(P)),
            (w_x[:], t["w_x"]), (w_dt[:], t["w_dt"]), (w_out[:], t["w_out"]), (chan[:], t["chan"]),
            (a_log[:], t["a_log"].partition_broadcast(P)), (wg0[:], t["wg0"]), (w_e0[:], t["w_e0"]),
            (b_e0[:], t["b_e0"]),
        ]
        N_LOADS = 16 * len(loads)
        loads1 = [
            (cos[:], t["cos"]), (sin[:], t["sin"]), (w_qk[:], t["w_qk"]), (b_qk[:], t["b_qk"]), (w_v[:], t["w_v"]),
            (b_v[:], t["b_v"].partition_broadcast(P)), (w_o[:], t["w_o"]),
            (q_op[72:PARTS], t["q_tail"]), (k_op[72:PARTS], t["k_tail"]),
        ]
        N_LOADS1 = 16 * len(loads1)
        HID_AHEAD = 16
        EXP_AHEAD = 5
        TILE = (0, 1, 2, 0, 1, 2, 0, 1)
        LAG = (2, 2, 5, 3, 3, 3, 3, 3)
        conv_b, b_dt, ln_g, ln_b, d_par = (chan[:, i, :] for i in range(5))

        def alone(engine):
            engine.sem_inc(S("passed"), 1)

        block = ctx.enter_context(nc.Block())

        @block.sync
        def _(sp):
            for b in range(B):
                sp.dma_start(x_all[:, b], t["x"][b].rearrange("(k p) d -> p k d", p=P)).then_inc(S("x_loaded"), 16)
            for dst, src in loads:
                sp.dma_start(dst, src).then_inc(S("w_loaded"), 16)

            sp.wait_ge(S("probs_ready"), 2 * B)
            for dst, src in loads1:
                sp.dma_start(dst, src).then_inc(S("w1_loaded"), 16)

            def store_parts(b, i):
                sp.wait_ge(S("qk_parts_ready"), 2 * b + i + 1)
                sp.dma_start(parts_dram[i].rearrange("j p t -> p j t"), qk_parts[i]).then_inc(S("parts_stored"), 16)

            with sp.Fori(0, B) as b:
                sp.wait_ge(S("pv_done"), b * 32 + 2)
                sp.dma_start(q_op[72:75], t["q_tail"][0:3]).then_inc(S("ops_loaded0"), 16)
                for e in range(2):
                    sp.wait_ge(S("hid_used"), 8 * (b * E + e) - 8 + HID_AHEAD)
                    sp.dma_start(w1[e][:], t["w1"][e]).then_inc(S(f"expert_loaded{e}"), 16)
                    sp.dma_start(w2[e][:], t["w2"][e].rearrange("(m p) d -> p m d", p=P)).then_inc(S(f"expert_loaded{e}"), 16)
                store_parts(b, 0)
                store_parts(b, 1)
                sp.wait_ge(S("parts_stored"), 32 * b + 32)
                for h0 in (0, H // 2):
                    hh = slice(h0, h0 + H // 2)
                    for i in range(3):
                        for j in range(3):
                            r = (3 * i + j) * HD
                            sp.dma_start(q_op[r:r + HD, hh], parts_dram[0, i].rearrange("(h d) t -> d h t", d=HD)[:, hh]).then_inc(S(f"ops_loaded{h0}"), 16)
                            sp.dma_start(k_op[r:r + HD, hh], parts_dram[1, j].rearrange("(h d) t -> d h t", d=HD)[:, hh]).then_inc(S(f"ops_loaded{h0}"), 16)
                with sp.Fori(1, E // 2) as e2:
                    for i in range(2):
                        e = e2 * 2 + i
                        sp.wait_ge(S("hid_used"), 8 * (b * E + e) - 8 + HID_AHEAD)
                        sp.dma_start(w1[i][:], t["w1"][e]).then_inc(S(f"expert_loaded{i}"), 16)
                        sp.dma_start(w2[i][:], t["w2"][e].rearrange("(m p) d -> p m d", p=P)).then_inc(S(f"expert_loaded{i}"), 16)
                sp.wait_ge(S("top_parts_ready"), b + 1)
                sp.dma_start(top_dram.rearrange("j r q -> r j q"), top_parts[:]).then_inc(S("top_stored"), 16)
                sp.wait_ge(S("top_stored"), 16 * b + 16)
                sp.dma_start(q_op[72:75], top_dram.rearrange("j (h k) q -> j h (k q)", h=H)).then_inc(S("top_loaded"), 16)
                sp.wait_ge(S("out_ready"), b + 1)
                sp.dma_start(out[b].rearrange("(k p) d -> p k d", p=P), x_all[:, b]).then_inc(S("stored"), 16)
            sp.wait_ge(S("stored"), 16 * B)

        @block.gpsimd
        def _(pool):
            pool.wait_ge(S("w_loaded"), N_LOADS)
            for k in range(TAPS):
                i = nc.gpsimd.tensor_tensor(w_tap[:, k, :], w_in[:, 0:DI], tap_b[:, k, :], ALU.mult)
            i.then_inc(S("taps_ready"), 1)
            pool.sem_inc(S("hc_ready"), 2)

            def times_c(i, n):
                pool.wait_ge(S("scanned"), n + 3)
                pool.wait_ge(S("c_ready"), n + 2)
                pool.wait_ge(S("summed"), n + 1)
                nc.gpsimd.tensor_tensor(hc[i][:, 1], hs[i][:, 1], c_sb[i][:], ALU.mult).then_inc(S("hc_ready"), 1)

            with pool.Fori(0, B) as b:
                pool.wait_ge(S("u1_ready"), b + 1)
                nc.gpsimd.tensor_tensor(hc[0][:], hs[1][:], dA[0][:], ALU.subtract).then_inc(S("lost_ready"), 1)
                with pool.Fori(0, NS // 2) as s2:
                    for i in range(2):
                        times_c(i, b * NS + s2 * 2 + i)

        @block.scalar
        def _(act):
            A = nc.scalar.activation
            act.wait_ge(S("w_loaded"), N_LOADS)
            A(a_exp[:], a_log[:], ACT.Exp).then_inc(S("a_exp_ready"), 1)
            act.sem_inc(S("c_ready"), 1)
            act.wait_ge(S("setup"), 1)

            def decay(i, s, n):
                act.wait_ge(S("scanned"), n + 1)
                act.wait_ge(S("dt_seen"), 1)
                A(dA[i][:, :, 1:], dt_[:, :, 1:], ACT.Exp, scale=a_neg[:, bass.ds(s, 1)]).then_inc(S("decay_ready"), 1)

            def keep_c(i, n):
                act.wait_ge(S("c_ps"), n + 1)
                act.wait_ge(S("hc_ready"), n + 1)
                A(c_sb[i][:], banks(2, 2), ACT.Copy).then_inc(S("c_ready"), 1)

            with act.Fori(0, B) as b:
                act.wait_ge(S("var_ready"), 2 * b + 1)
                A(std[:], mv[:, :, 1], ACT.Sqrt, bias=eps_col[:]).then_inc(S("std_ready"), 1)
                act.wait_ge(S("xnT_ps"), 2 * b + 1)
                A(xnT[:, TAPS - 1:], banks(0, 2), ACT.Copy).then_inc(S("xnT_ready"), 1)
                act.wait_ge(S("z_ps"), b + 1)
                A(zs[:].rearrange("p h t -> p (h t)"), banks(2, 4), ACT.Silu).then_inc(S("zs_ready"), 1)
                act.wait_ge(S("conv_ps"), 2 * b + 1)
                A(xc[:, 1, :], banks(6, 2), ACT.Silu, bias=conv_b[:, 1:2]).then_inc(S("xc_ready"), 1)
                act.wait_ge(S("conv_ps"), 2 * b + 2)
                A(xc[:, 0, :], banks(0, 2), ACT.Silu, bias=conv_b[:, 0:1]).then_inc(S("xc_ready"), 1)
                act.wait_ge(S("lg_ready"), 2 * b + 1)
                A(ex[:], lg[:], ACT.Exp).then_inc(S("ex_ready"), 1)
                act.wait_ge(S("dt_ps"), b + 1)
                for h in range(NH2):
                    A(dt_[:, h, :], banks(2 + 2 * h, 2), ACT.Abs, bias=b_dt[:, h:h + 1]).then_inc(S("abs_ready"), 1)
                act.wait_ge(S("bc_ps"), b + 1)
                A(bc[:], banks(0, 2, PARTS), ACT.Copy).then_inc(S("part1"), 1)
                act.wait_ge(S("abs_ready"), 2 * b + 2)
                A(dA[0][:], dt_[:], ACT.Exp, scale=-1.0).then_inc(S("u_ready"), 1)
                act.wait_ge(S("u_ready"), b + 1)
                A(dA[1][:], dA[0][:], ACT.Ln, bias=1.0).then_inc(S("ln_ready"), 1)
                act.wait_ge(S("rest_ready"), 2 * b + 1)
                A(bc[32:64, :], rest[32:64, :], ACT.Copy)
                A(mid[64:96, :], rest[64:96, :], ACT.Copy).then_inc(S("part2"), 1)
                act.wait_ge(S("gateT_ps"), b + 1)
                A(gateT[:], banks(0, 2, E), ACT.Copy)
                A(gparts[:], banks(0, 2, PARTS), ACT.Copy).then_inc(S("part1"), 1)
                act.wait_ge(S("rest_ready"), 2 * b + 2)
                A(gparts[32:64, :], rest[32:64, :], ACT.Copy)
                A(mid[64:96, :], rest[64:96, :], ACT.Copy).then_inc(S("part2"), 1)
                act.wait_ge(S("ffn_done"), b * E + E + 2)
                A(s_gT[:], banks(6, 2), ACT.Silu).then_inc(S("s_g_ready"), 1)
                act.wait_ge(S("dt_ready"), b + 1)
                with act.Fori(0, NS // 2) as s2:
                    for i in range(2):
                        decay(i, s2 * 2 + i, b * NS + s2 * 2 + i)
                        keep_c(i, b * NS + s2 * 2 + i)
                act.wait_ge(S("summed"), b * NS + NS + 2)
                A(hs[0][:].rearrange("p h t -> p (h t)"), banks(4, 4), ACT.Copy).then_inc(S("y_ready"), 1)
                act.wait_ge(S("yc_ready"), b + 1)
                A(dA[0][:], hs[1][:], ACT.Square).then_inc(S("sq_ready"), 1)
                act.wait_ge(S("yvar_ps"), b + 1)
                A(c_sb[0][:], banks(2, 2), ACT.Ln, bias=eps_col[:]).then_inc(S("lnvar"), 1)
                act.wait_ge(S("lnvar"), b + 1)
                A(c_sb[1][:], c_sb[0][:], ACT.Exp, scale=-0.5).then_inc(S("yrstd_ready"), 1)
                act.wait_ge(S("yn_ready"), b + 1)
                for h in range(NH2):
                    i = A(hc[1][:, h, :], hc[0][:, h, :], ACT.Identity, scale=ln_g[:, h:h + 1], bias=ln_b[:, h:h + 1])
                i.then_inc(S("yg_ready"), 1)
                act.wait_ge(S("var_ready"), 2 * b + 2)
                A(std[:], mv[:, :, 1], ACT.Sqrt, bias=eps_col[:]).then_inc(S("std_ready"), 1)
                act.wait_ge(S("xnT_ps"), 2 * b + 2)
                A(xnT[:, TAPS - 1:], banks(0, 2), ACT.Copy).then_inc(S("xnT_ready"), 1)
                act.wait_ge(S("lg_ready"), 2 * b + 2)
                A(ex[:], lg[:], ACT.Exp).then_inc(S("ex_ready"), 1)
            act.sem_inc(S("hid_ready"), 2)
            act.sem_inc(S("gate_sb_ready"), 1)

            act.wait_ge(S("w1_loaded"), N_LOADS1)

            with act.Fori(0, B) as b:
                for i in range(2):
                    act.wait_ge(S("rot_ready"), 2 * b + i + 1)
                    A(qk_parts[i][:, 0, :], rot[0], ACT.Copy).then_inc(S("qk_part1"), 1)
                    act.wait_ge(S("qk_rest"), 2 * b + i + 1)
                    A(qk_parts[i][:, 1, :], rot[1], ACT.Copy).then_inc(S("qk_part2"), 1)
                act.wait_ge(S("gpadT_ps"), b + 1)
                A(gparts1[:], banks(4, 2, PARTS), ACT.Copy).then_inc(S("gpart1"), 1)
                act.wait_ge(S("grest_ready"), b + 1)
                A(gparts1[32:64, :], grest[32:64, :], ACT.Copy)
                A(gmid[64:96, :], grest[64:96, :], ACT.Copy).then_inc(S("gpart2"), 1)

                def half_out(h, k):
                    v = (b * H + h) * NBLK + k
                    act.wait_ge(S("s_ps"), v + 1)
                    act.wait_ge(S("top_done"), v + 1)
                    A(half_sb[k % 2], ps[:, 2 * (k % 2) + 1, :], ACT.Copy).then_inc(S("s_half"), 1)

                def expert(n, heads=None):
                    for c in range(2):
                        scores_left = iter(range(NBLK))

                        def fill(count):
                            if heads is not None:
                                for _ in range(count):
                                    half_out(heads + c, next(scores_left))
                        act.wait_ge(S("gate1_ps"), 2 * n + c + 1)
                        act.wait_ge(S("acc_done"), 2 * n + c + 1)
                        A(gate_sb[c], ps[:, 4 + c, :], ACT.Copy).then_inc(S("gate_sb_ready"), 1)
                        for q in range(4):
                            u = 8 * n + 4 * c + q
                            act.wait_ge(S("hid_ps"), u + 1)
                            act.wait_ge(S("hid_used"), u - 3 + HID_AHEAD)
                            A(hid[q], ps[:, 4 + (c + 1 + q) % 2, :], ACT.Gelu_apprx_tanh).then_inc(S("hid_ready"), 1)
                            fill((1, 2, 2, 3)[q])
                expert(b * E)
                with act.Fori(1, E) as e:
                    expert(b * E + e, 2 * e - 2)
                for h in (H - 2, H - 1):
                    for k in range(NBLK):
                        half_out(h, k)
                act.wait_ge(S("acc_done"), 2 * E * b + 2 * E + 2)
                A(acc_bf[:], acc[:], ACT.Copy).then_inc(S("acc_bf_ready"), 1)
                act.wait_ge(S("acc_bf_ready"), b + 1)
                A(silu_bf[:], acc_bf[:], ACT.Silu).then_inc(S("silu_ready"), 1)
                act.wait_ge(S("top_ps"), b + 1)
                A(top_parts[:, 0, :], ps[:, 0, 0:P], ACT.Copy).then_inc(S("top_part1"), 1)
                act.wait_ge(S("top_rest_ready"), b + 1)
                A(top_parts[:, 1, :], top_rest[:], ACT.Copy).then_inc(S("top_part2"), 1)
                def exps(i, m):
                    act.wait_ge(S("pv_done"), m + 1)
                    for j in range(HG):
                        act.wait_ge(S("sT_ps"), m * HG + j + 1)
                        A(big[i][:, j, :], banks(2 * TILE[i * HG + j], 2), ACT.Exp, scale=HD ** -0.5).then_inc(S("exp_done"), 1)

                def keep_o(ng):
                    act.wait_ge(S("pv_done"), ng * 8 + 8 + 2)
                    A(o_T[:], banks(6, 2), ACT.Copy).then_inc(S("o_ready"), 1)

                def exp_group(g, first=False):
                    m0 = (b * 4 + g) * 8
                    exps(0, m0)
                    if not first:
                        keep_o(b * 4 + g - 1)
                    exps(1, m0 + 1)
                    with act.Fori(1, NBLK // 2) as k2:
                        for i in range(2):
                            exps(i, m0 + k2 * 2 + i)
                exp_group(0, first=True)
                with act.Fori(1, H // HG) as g:
                    exp_group(g)
                keep_o(b * 4 + 3)
                act.wait_ge(S("attT_ps"), b + 1)
                A(attT[:], banks(0, 2), ACT.Copy).then_inc(S("attT_ready"), 1)
                act.wait_ge(S("s1_ps"), b + 1)
                A(s1T[:], banks(2, 2), ACT.Identity, bias=b_qk[:, 4:5]).then_inc(S("s1_ready"), 1)

        @block.vector
        def _(dve):
            V = nc.vector
            V.memset(eps_col[:], EPS)
            V.memset(ones_bf[:], 1.0)
            V.memset(zeros_bf[:], 0.0)
            V.memset(mean_w[:], 1.0 / DI)
            V.memset(xnT[:, 0:TAPS - 1], 0.0)
            V.memset(gate0[:], 0.0)
            V.memset(taken[:], 0.0)
            dve.wait_ge(S("a_exp_ready"), 1)
            V.tensor_scalar(a_neg[:], a_exp[:], -1.0, None, ALU.mult).then_inc(S("setup"), 1)
            dve.sem_inc(S("scanned"), 2)
            dve.sem_inc(S("b_used"), 1)
            dve.sem_inc(S("c_used"), 1)
            dve.sem_inc(S("parts_ready"), 1)
            dve.sem_inc(S("dt_seen"), 1)
            dve.wait_ge(S("x_loaded"), 16 * B)
            dve.wait_ge(S("w_loaded"), N_LOADS)
            def norm(b, n):
                for k in range(NBLK):
                    i = V.bn_stats(bn[:, k, :], x_all[:, b, k, :])
                i.then_inc(S("stats_ready"), 1)
                dve.wait_ge(S("stats_ready"), n + 1)
                alone(dve)
                for k in range(NBLK):
                    i = V.bn_aggr(mv[:, k, :], bn[:, k, :])
                i.then_inc(S("var_ready"), 1)
                dve.wait_ge(S("std_ready"), n + 1)
                V.reciprocal(rstd[:], std[:]).then_inc(S("rstd_ready"), 1)
                dve.wait_ge(S("rstd_ready"), n + 1)
                for k in range(NBLK):
                    i = V.tensor_scalar(xn[:, k, :], x_all[:, b, k, :], mv[:, k, 0:1], rstd[:, k:k + 1],
                                        ALU.subtract, ALU.mult)
                i.then_inc(S("xn_ready"), 1)

            def router(b, n, bank, result):
                logits = ps[:, bank, 0:NBLK * E].rearrange("p (k e) -> p k e", e=E)
                dve.wait_ge(S("lg_ps"), n + 1)
                V.tensor_reduce(m8[:], logits, AX_X, ALU.max).then_inc(S("m8_ready"), 1)
                dve.wait_ge(S("m8_ready"), n + 1)
                V.tensor_tensor(lg[:], logits, over(m8[:], 2, E), ALU.subtract).then_inc(S("lg_ready"), 1)
                dve.wait_ge(S("ex_ready"), n + 1)
                V.tensor_reduce(s8[:], ex[:], AX_X, ALU.add).then_inc(S("s8_ready"), 1)
                dve.wait_ge(S("s8_ready"), n + 1)
                V.reciprocal(r8[:], s8[:]).then_inc(S("r8_ready"), 1)
                dve.wait_ge(S("r8_ready"), n + 1)
                V.tensor_tensor(result, ex[:], over(r8[:], 2, E), ALU.mult).then_inc(S("probs_ready"), 1)
                dve.wait_ge(S("probs_ready"), n + 1)

            def remainders(parts, n):
                dve.wait_ge(S("part1"), n + 1)
                dve.wait_ge(S("parts_ready"), n + 1)
                V.tensor_tensor(rest[:], banks(0, 2, PARTS), parts[:], ALU.subtract).then_inc(S("rest_ready"), 1)
                dve.wait_ge(S("rest_ready"), n + 1)
                dve.wait_ge(S("part2"), n + 1)
                V.tensor_tensor(parts[64:96, :], rest[64:96, :], mid[64:96, :], ALU.subtract).then_inc(S("parts_ready"), 1)

            def times_c(i, n):
                dve.wait_ge(S("c_ready"), n + 2)
                dve.wait_ge(S("summed"), n + 1)
                dve.wait_ge(S("scanned"), n + 3)
                V.tensor_tensor(hc[i][:, 0], hs[i][:, 0], banks(2, 2), ALU.mult).then_inc(S("c_used"), 1)

            def scan_step(i, n, first=False):
                dve.wait_ge(S("b_ps"), n + 1)
                dve.wait_ge(S("hc_ready"), n + 1)
                dve.wait_ge(S("c_used"), n)
                V.tensor_tensor(hs[i][:], dtx[:], over(banks(0, 2), 1, NH2), ALU.mult).then_inc(S("b_used"), 1)
                if not first:
                    times_c(1 - i, n - 1)
                dve.wait_ge(S("b_used"), n + 2)
                dve.wait_ge(S("decay_ready"), n + 1)
                h = hs[i][:].rearrange("p h t -> p (h t)")
                V.tensor_tensor_scan(h, dA[i][:].rearrange("p h t -> p (h t)"), h, 0.0,
                                     ALU.mult, ALU.add).then_inc(S("scanned"), 1)

            with dve.Fori(0, B) as b:
                norm(b, 2 * b)
                router(b, 2 * b, 0, probs0[:])
                V.tensor_reduce(pmax[:], probs0[:], AX_X, ALU.max).then_inc(S("pmax_ready"), 1)
                dve.wait_ge(S("pmax_ready"), b + 1)
                V.tensor_tensor(eqw[:], probs0[:], over(pmax[:], 2, E), ALU.is_equal).then_inc(S("eq_ready"), 1)
                dve.wait_ge(S("eq_ready"), b + 1)
                V.tensor_tensor(eqw[:], eqw[:], over(rank_w[:], 1, NBLK), ALU.mult).then_inc(S("eqw_ready"), 1)
                dve.wait_ge(S("eqw_ready"), b + 1)
                V.tensor_reduce(first[:], eqw[:], AX_X, ALU.max).then_inc(S("first_ready"), 1)
                dve.wait_ge(S("first_ready"), b + 1)
                V.tensor_tensor(choice_bf[:], eqw[:], over(first[:], 2, E), ALU.is_equal).then_inc(S("choice_ready"), 1)
                V.tensor_tensor(choice[:], eqw[:], over(first[:], 2, E), ALU.is_equal).then_inc(S("choice_f32_ready"), 1)
                dve.wait_ge(S("pos_ps"), b + 1)
                V.tensor_tensor(pos[:], ps[:, 6, 0:NBLK * E].rearrange("p (k e) -> p k e", e=E),
                                over(taken[:], 1, NBLK), ALU.add).then_inc(S("pos_ready"), 1)
                dve.wait_ge(S("pos_ready"), b + 1)
                dve.wait_ge(S("choice_f32_ready"), b + 1)
                V.scalar_tensor_tensor(kept[:], pos[:], float(CAP0), choice[:], ALU.is_lt, ALU.mult).then_inc(S("kept_ready"), 1)
                V.tensor_tensor(taken[:], taken[:], ps[:, 7, 0:E], ALU.add)
                dve.wait_ge(S("kept_ready"), b + 1)
                for g in range(3):
                    i = V.tensor_tensor(gate0[:, :, 32 * g:32 * g + E], kept[:], probs0[:], ALU.mult)
                i.then_inc(S("gate0_ready"), 1)
                for h in range(NH2):
                    dve.wait_ge(S("abs_ready"), 2 * b + 1 + h)
                    i = V.tensor_scalar(hs[0][:, h, :], banks(2 + 2 * h, 2), b_dt[:, h:h + 1], 0.0, ALU.add, ALU.max)
                i.then_inc(S("relu_ready"), 1)
                remainders(bc, 2 * b)
                dve.wait_ge(S("u_ready"), b + 1)
                V.tensor_scalar(hs[1][:], dA[0][:], 1.0, -1.0, ALU.add, ALU.add).then_inc(S("u1_ready"), 1)
                remainders(gparts, 2 * b + 1)
                dve.wait_ge(S("ln_ready"), b + 1)
                V.tensor_tensor(hs[0][:], hs[0][:], dA[1][:], ALU.add).then_inc(S("relu_ln_ready"), 1)
                dve.wait_ge(S("lost_ready"), b + 1)
                dve.wait_ge(S("relu_ln_ready"), b + 1)
                for i in range(2):
                    V.memset(dA[i][:, :, 0:1], 0.0)
                V.tensor_tensor(dt_[:], hs[0][:], hc[0][:], ALU.subtract).then_inc(S("dt_ready"), 1)
                dve.wait_ge(S("dt_ready"), b + 1)
                V.tensor_tensor(dtx[:], dt_[:], xc[:], ALU.mult).then_inc(S("dtx_ready"), 1)
                for e in range(E):
                    dve.wait_ge(S("gate_ps"), b * E + e + 1)
                    dve.wait_ge(S("ffn_done"), b * E + e + 1)
                    V.tensor_tensor(xg[e % 2][:], xnT[:, TAPS - 1:], banks(2 + 2 * (e % 2), 2), ALU.mult).then_inc(S("xg_ready"), 1)
                scan_step(0, b * NS, first=True)
                scan_step(1, b * NS + 1)
                with dve.Fori(1, NS // 2) as s2:
                    for i in range(2):
                        scan_step(i, b * NS + s2 * 2 + i)
                times_c(1, b * NS + NS - 1)
                dve.wait_ge(S("ymean_ps"), b + 1)
                V.tensor_tensor(hs[1][:], hs[0][:], over(banks(0, 2), 1, NH2), ALU.subtract).then_inc(S("yc_ready"), 1)
                dve.wait_ge(S("yc_ready"), b + 1)
                dve.wait_ge(S("yrstd_ready"), b + 1)
                V.tensor_tensor(hc[0][:], hs[1][:], over(c_sb[1][:], 1, NH2), ALU.mult).then_inc(S("yn_ready"), 1)
                dve.wait_ge(S("yg_ready"), b + 1)
                for h in range(NH2):
                    i = V.scalar_tensor_tensor(hc[0][:, h, :], xc[:, h, :], d_par[:, h:h + 1], hc[1][:, h, :], ALU.mult, ALU.add)
                i.then_inc(S("yd_ready"), 1)
                dve.wait_ge(S("yd_ready"), b + 1)
                V.tensor_tensor(hc[1][:], hc[0][:], zs[:], ALU.mult).then_inc(S("mix_ready"), 1)
                dve.wait_ge(S("s0_ps"), b + 1)
                V.tensor_tensor(c_sb[0][:], s_gT[:], banks(0, 2), ALU.mult).then_inc(S("sg_ready"), 1)
                dve.wait_ge(S("sgT_ps"), b + 1)
                V.tensor_tensor(x_all[:, b].rearrange("p k d -> p (k d)"), x_all[:, b].rearrange("p k d -> p (k d)"),
                                banks(2, 2), ALU.add).then_inc(S("x1_ready"), 1)
                dve.wait_ge(S("x1_ready"), b + 1)
                alone(dve)
                norm(b, 2 * b + 1)
                dve.wait_ge(S("xnT_ready"), 2 * b + 2)
                V.tensor_copy(xn1T_all[:, b, :], xnT[:, TAPS - 1:]).then_inc(S("xn1T_ready"), 1)
                router(b, 2 * b + 1, 2, probs[:, b])

            dve.wait_ge(S("probs_ready"), 2 * B)
            V.memset(thr[:], 0)
            V.memset(bit[:], 1 << ONE_BITS)
            V.memset(gpad[:], 0.0)
            V.memset(v_grp[:], 0.0).then_inc(S("setup1"), 1)
            dve.wait_ge(S("setup1"), 1)
            V.memset(v_grp[:, :, :, HD:HD + 1], 1.0).then_inc(S("setup1"), 1)
            dve.sem_inc(S("top_done"), 2)
            dve.sem_inc(S("top_out"), 2)
            dve.sem_inc(S("acc_done"), 2)
            dve.sem_inc(S("thr_step"), 1)

            def by_block(ap):
                return over(ap, 2, NBLK)
            with dve.Fori(0, ONE_BITS + 1) as i:
                dve.wait_ge(S("thr_step"), i + 1)
                V.tensor_tensor(cand[:], thr[:], bit[:], ALU.bitwise_or).then_inc(S("cand_ready"), 1)
                dve.wait_ge(S("cand_ready"), i + 1)
                V.tensor_tensor(over_thr[:], probs[:], by_block(cand[:].bitcast(F32)), ALU.is_ge).then_inc(S("over_ready"), 1)
                dve.wait_ge(S("count_ps"), i + 1)
                V.scalar_tensor_tensor(step[:], ps[:, 0, 0:B * E].rearrange("p (b e) -> p b e", e=E), float(K1), bit[:],
                                       ALU.is_ge, ALU.mult).then_inc(S("step_ready"), 1)
                dve.wait_ge(S("step_ready"), i + 1)
                V.tensor_scalar(bit[:], bit[:], 1, None, ALU.logical_shift_right)
                V.tensor_tensor(thr[:], thr[:], step[:], ALU.bitwise_or).then_inc(S("thr_step"), 1)
            dve.wait_ge(S("thr_step"), ONE_BITS + 2)
            V.tensor_tensor(at_thr[:], probs[:], by_block(thr[:].bitcast(F32)), ALU.is_equal)
            V.tensor_tensor(over_thr[:], probs[:], by_block(thr[:].bitcast(F32)), ALU.is_gt).then_inc(S("split_ready"), 1)
            dve.wait_ge(S("ranks_ps"), 1)
            V.tensor_scalar(need[:], ps[:, 0, 0:B * E].rearrange("p (b e) -> p b e", e=E), -1.0, float(K1),
                            ALU.mult, ALU.add).then_inc(S("need_ready"), 1)
            dve.wait_ge(S("need_ready"), 1)
            V.tensor_tensor(picked[:], ps[:, 1, 0:B * NBLK * E].rearrange("p (b k e) -> p b k e", b=B, e=E),
                            by_block(need[:]), ALU.is_lt).then_inc(S("need_ready"), 1)
            dve.wait_ge(S("need_ready"), 2)
            V.tensor_tensor(picked[:], picked[:], at_thr[:], ALU.mult).then_inc(S("need_ready"), 1)
            dve.wait_ge(S("need_ready"), 3)
            V.tensor_tensor(picked[:], picked[:], over_thr[:], ALU.add).then_inc(S("need_ready"), 1)
            dve.wait_ge(S("need_ready"), 4)
            V.tensor_tensor(gate1[:], picked[:], probs[:], ALU.mult).then_inc(S("need_ready"), 1)
            dve.wait_ge(S("need_ready"), 5)
            dve.wait_ge(S("w1_loaded"), N_LOADS1)

            with dve.Fori(0, B) as b:
                V.tensor_scalar(xT[:], xn1T_all[:, b, :], 1.0, None, ALU.mult).then_inc(S("xT_ready"), 1)
                for i in range(3):
                    j = V.tensor_scalar(gpad[:, :, 32 * i:32 * i + E], gate1[:, b], 1.0, None, ALU.mult)
                j.then_inc(S("gpad_ready"), 1)
                for i in range(2):
                    if i == 1:
                        dve.wait_ge(S("qk_parts_ready"), 2 * b + 1)
                    dve.wait_ge(S("qk_ps"), 2 * b + i + 1)
                    V.scalar_tensor_tensor(rot[0], banks(4 * i, 2), b_qk[:, 2 * i:2 * i + 1], cos[:], ALU.add, ALU.mult)
                    V.scalar_tensor_tensor(rot[1], banks(4 * i + 2, 2), b_qk[:, 2 * i + 1:2 * i + 2], sin[:],
                                           ALU.add, ALU.mult).then_inc(S("halves_ready"), 1)
                    dve.wait_ge(S("halves_ready"), 2 * b + i + 1)
                    V.tensor_tensor(rot[0], rot[0], rot[1], ALU.add).then_inc(S("rot_ready"), 1)
                    dve.wait_ge(S("rot_ready"), 2 * b + i + 1)
                    dve.wait_ge(S("qk_part1"), 2 * b + i + 1)
                    V.tensor_tensor(rot[1], rot[0], qk_parts[i][:, 0, :], ALU.subtract).then_inc(S("qk_rest"), 1)
                    dve.wait_ge(S("qk_rest"), 2 * b + i + 1)
                    dve.wait_ge(S("qk_part2"), 2 * b + i + 1)
                    V.tensor_tensor(qk_parts[i][:, 2, :], rot[1], qk_parts[i][:, 1, :], ALU.subtract).then_inc(S("qk_parts_ready"), 1)
                dve.wait_ge(S("v_ps"), b + 1)
                V.tensor_tensor(v_tok[:], banks(0, 2).rearrange("p (k c) -> p k c", k=NBLK), over(b_v[:], 1, NBLK),
                                ALU.add).then_inc(S("v_ready"), 1)
                dve.wait_ge(S("gpart1"), b + 1)
                V.tensor_tensor(grest, banks(4, 2, PARTS), gparts1[:], ALU.subtract).then_inc(S("grest_ready"), 1)
                dve.wait_ge(S("grest_ready"), b + 1)
                dve.wait_ge(S("gpart2"), b + 1)
                V.tensor_tensor(gparts1[64:96, :], grest[64:96, :], gmid[64:96, :], ALU.subtract).then_inc(S("gparts1_ready"), 1)
                V.memset(acc[:], 0.0).then_inc(S("acc_zero"), 1)
                dve.wait_ge(S("acc_zero"), b + 1)

                def head_tops(h):
                    for k in range(NBLK):
                        n = (b * H + h) * NBLK + k
                        dve.wait_ge(S("s_half"), n + 1)
                        if k % 2 == 0:
                            dve.wait_ge(S("top_out"), (b * H + h) * (NBLK // 2) + k // 2 + 1)
                        V.tensor_tensor_scan(top_run[k // 2 % 2][:, k % 2, :], half_sb[k % 2], ps[:, 2 * (k % 2), :], LOWEST,
                                             ALU.max, ALU.max).then_inc(S("top_done"), 1)
                        if k % 2:
                            dve.wait_ge(S("top_done"), n + 3)
                            V.tensor_scalar(top[:, bass.ds(h * NBLK + k - 1, 2)], top_run[k // 2 % 2][:, :, HALF - 1], 1.0,
                                            None, ALU.mult).then_inc(S("top_out"), 1)

                def weigh(n, c):
                    cs = slice(c * HALF, (c + 1) * HALF)
                    dve.wait_ge(S("gate_sb_ready"), 2 * n + c + 2)
                    dve.wait_ge(S("hid_used"), 8 * n + 4 * c + 4 + HID_AHEAD)
                    dve.wait_ge(S("acc_done"), 2 * n + c + 2)
                    V.tensor_tensor(weighted, ps[:, 6 + c, :], gate_sb[c], ALU.mult).then_inc(S("weighted_ready"), 1)
                    dve.wait_ge(S("weighted_ready"), 2 * n + c + 1)
                    V.tensor_tensor(acc[:, cs], acc[:, cs], weighted, ALU.add).then_inc(S("acc_done"), 1)

                for c in range(2):
                    weigh(b * E, c)
                with dve.Fori(1, E) as e:
                    for c in range(2):
                        head_tops(2 * e - 2 + c)
                        weigh(b * E + e, c)
                for h in (H - 2, H - 1):
                    head_tops(h)
                dve.wait_ge(S("top_part1"), b + 1)
                V.tensor_tensor(top_rest[:], ps[:, 0, 0:P], top_parts[:, 0, :], ALU.subtract).then_inc(S("top_rest_ready"), 1)
                dve.wait_ge(S("top_rest_ready"), b + 1)
                dve.wait_ge(S("top_part2"), b + 1)
                V.tensor_tensor(top_parts[:, 2, :], top_rest[:], top_parts[:, 1, :], ALU.subtract).then_inc(S("top_parts_ready"), 1)
                dve.wait_ge(S("v_ready"), b + 1)
                def group_v(g):
                    dve.wait_ge(S("pv_done"), (b * 4 + g) * 8 + 2)
                    V.tensor_scalar(v_grp[:, :, :, 0:HD],
                                    v_tok[:, :, bass.ds(g * HG * HD, HG * HD)].rearrange("p k (j d) -> p k j d", j=HG),
                                    1.0, None, ALU.mult).then_inc(S("v_grp_ready"), 1)

                def divide(g):
                    ng = b * 4 + g
                    dve.wait_ge(S("o_ps"), ng + 1)
                    o = banks(6, 2).rearrange("p (k j c) -> p k j c", k=NBLK, j=HG)
                    V.reciprocal(rsum[:], o[:, :, :, HD]).then_inc(S("rsum_ready"), 1)
                    dve.wait_ge(S("rsum_ready"), ng + 1)
                    V.tensor_tensor(att[:, :, bass.ds(g * HG * HD, HG * HD)].rearrange("p k (j d) -> p k j d", j=HG),
                                    o[:, :, :, 0:HD], over(rsum[:], 3, HD), ALU.mult).then_inc(S("att_ready"), 1)
                group_v(0)
                with dve.Fori(1, H // HG) as g:
                    group_v(g)
                    divide(g - 1)
                divide(3)
                dve.wait_ge(S("silu_ready"), b + 1)
                dve.wait_ge(S("s1_ready"), b + 1)
                V.tensor_tensor(o_T[:], s1T[:], silu_bf[:], ALU.mult).then_inc(S("sg1_ready"), 1)
                dve.wait_ge(S("sg1_ps"), b + 1)
                xb = x_all[:, b].rearrange("p k d -> p (k d)")
                V.tensor_tensor(xb, xb, banks(0, 2), ALU.add).then_inc(S("out_ready"), 1)

        @block.tensor
        def _(pe):
            M = nc.tensor.matmul
            pe.wait_ge(S("w_loaded"), N_LOADS)
            pe.wait_ge(S("setup"), 1)
            pe.wait_ge(S("taps_ready"), 1)
            pe.sem_inc(S("summed"), 2)
            pe.sem_inc(S("ffn_done"), 2)
            cols = [slice(c * HALF, (c + 1) * HALF) for c in range(2)]

            def turn(src, bank):
                for k in range(NBLK):
                    i = nc.tensor.transpose(ps[:, bank + k // 4, (k % 4) * P:(k % 4 + 1) * P], src(k), ident[:])
                return i

            def logits(wg, bank):
                for k in range(NBLK):
                    i = M(ps[:, bank, k * E:(k + 1) * E], xnT[:, TAPS - 1 + k * P:TAPS - 1 + (k + 1) * P], wg[:],
                          start=True, stop=True)
                i.then_inc(S("lg_ps"), 1)

            def spread(s, bank, done):
                for c in range(2):
                    i = M(ps[:, bank + c, :], pick[:, s, :], bc[:, cols[c]], start=True, stop=True)
                i.then_inc(S(done), 1)

            def spread_b(s, n):
                pe.wait_ge(S("b_used"), n + 1)
                spread(s, 0, "b_ps")

            def spread_c(s, n):
                pe.wait_ge(S("c_ready"), n + 1)
                pe.wait_ge(S("c_used"), n + 1)
                spread(s + NS, 2, "c_ps")

            def sum_states(i, n):
                pe.wait_ge(S("hc_ready"), n + 3)
                pe.wait_ge(S("c_used"), n + 2)
                for h in range(NH2):
                    for c in range(2):
                        m = M(ps[:, 4 + 2 * h + c, :], ident[:], hc[i][:, h, cols[c]], start=False, stop=False,
                              skip_group_check=True)
                m.then_inc(S("summed"), 1)

            with pe.Fori(0, B) as b:
                pe.wait_ge(S("xn_ready"), 2 * b + 1)
                turn(lambda k: xn[:, k, :], 0).then_inc(S("xnT_ps"), 1)
                pe.wait_ge(S("xnT_ready"), 2 * b + 1)
                for h in range(NH2):
                    for c in range(2):
                        i = M(ps[:, 2 + 2 * h + c, :], w_in[:, DI + h * P:DI + (h + 1) * P],
                              xnT[:, TAPS - 1 + c * HALF:TAPS - 1 + (c + 1) * HALF], start=True, stop=True)
                i.then_inc(S("z_ps"), 1)
                logits(wg0, 0)
                for h, bank in ((1, 6), (0, 0)):
                    if h == 0:
                        pe.wait_ge(S("lg_ready"), 2 * b + 1)
                    for c in range(2):
                        for k in range(TAPS):
                            i = M(ps[:, bank + c, :], w_tap[:, k, h * P:(h + 1) * P],
                                  xnT[:, c * HALF + k:c * HALF + k + HALF], start=(k == 0), stop=(k == TAPS - 1))
                    i.then_inc(S("conv_ps"), 1)
                pe.wait_ge(S("choice_ready"), b + 1)
                pe.wait_ge(S("xc_ready"), 2 * b + 1)
                ch = choice_bf[:].rearrange("p k e -> p (k e)")
                M(ps[:, 6, 0:NBLK * E], before_tok[:], ch, start=True, stop=False, skip_group_check=True)
                for k in range(1, NBLK):
                    M(ps[:, 6, k * E:NBLK * E], ones_bf[:], ch[:, 0:(NBLK - k) * E], start=False, stop=(k == NBLK - 1),
                      skip_group_check=True)
                for k in range(NBLK):
                    i = M(ps[:, 7, 0:E], ones_bf[:], choice_bf[:, k, :], start=(k == 0), stop=(k == NBLK - 1))
                i.then_inc(S("pos_ps"), 1)
                pe.wait_ge(S("xc_ready"), 2 * b + 2)
                pe.wait_ge(S("zs_ready"), b + 1)
                for h in range(NH2):
                    for c in range(2):
                        for k in range(NH2):
                            i = M(ps[:, 2 + 2 * h + c, :], w_dt[:, k, h * P:(h + 1) * P], xc[:, k, cols[c]],
                                  start=(k == 0), stop=(k == NH2 - 1))
                i.then_inc(S("dt_ps"), 1)
                for c in range(2):
                    for k in range(NH2):
                        i = M(ps[0:PARTS, c, :], w_x[:, k, :], xc[:, k, cols[c]], start=(k == 0), stop=(k == NH2 - 1))
                i.then_inc(S("bc_ps"), 1)
                pe.wait_ge(S("gate0_ready"), b + 1)
                pe.wait_ge(S("rest_ready"), 2 * b + 1)
                for k in range(NBLK):
                    i = nc.tensor.transpose(ps[0:PARTS, k // 4, (k % 4) * P:(k % 4 + 1) * P], gate0[:, k, :], ident[:])
                i.then_inc(S("gateT_ps"), 1)
                pe.wait_ge(S("parts_ready"), 2 * b + 3)
                pe.wait_ge(S("relu_ready"), b + 1)
                pe.wait_ge(S("kept_ready"), b + 1)
                for c in range(2):
                    M(ps[:, 6 + c, :], b_e0[:], gateT[:, cols[c]], start=True, stop=False, skip_group_check=True)

                def gate_out(e):
                    if e >= 2:
                        pe.wait_ge(S("xg_ready"), b * E + e - 1)
                    for c in range(2):
                        i = M(ps[:, 2 + 2 * (e % 2) + c, :], pick[:, e, :], gparts[:, cols[c]], start=True, stop=True)
                    i.then_inc(S("gate_ps"), 1)
                gate_out(0)
                for e in range(E):
                    if e + 1 < E:
                        gate_out(e + 1)
                    pe.wait_ge(S("xg_ready"), b * E + e + 1)
                    for c in range(2):
                        i = M(ps[:, 6 + c, :], w_e0[:, e, :], xg[e % 2][:, cols[c]], start=False, stop=(e == E - 1),
                              skip_group_check=True)
                    i.then_inc(S("ffn_done"), 1)
                pe.wait_ge(S("s_g_ready"), b + 1)
                for k in range(4):
                    M(ps[:, 4 + k, :], zeros_bf[:, 0:P], zeros_bf[:], start=True, stop=False, skip_group_check=True)
                n0 = b * NS
                spread_b(0, n0)
                for s in range(2):
                    spread_b(s + 1, n0 + s + 1)
                    spread_c(s, n0 + s)
                with pe.Fori(1, NS // 2 - 1) as s2:
                    for i in range(2):
                        s = s2 * 2 + i
                        spread_b(s + 1, n0 + s + 1)
                        spread_c(s, n0 + s)
                        sum_states(i, n0 + s - 2)
                for s in (NS - 2, NS - 1):
                    if s < NS - 1:
                        spread_b(s + 1, n0 + s + 1)
                    spread_c(s, n0 + s)
                    sum_states(s % 2, n0 + s - 2)
                sum_states(0, n0 + NS - 2)
                sum_states(1, n0 + NS - 1)
                for src, bank, ready, done in ((hs[0], 0, "y_ready", "ymean_ps"), (dA[0], 2, "sq_ready", "yvar_ps")):
                    pe.wait_ge(S(ready), b + 1)
                    for c in range(2):
                        for k in range(NH2):
                            i = M(ps[:, bank + c, :], mean_w[:], src[:, k, cols[c]], start=(k == 0), stop=(k == NH2 - 1))
                    i.then_inc(S(done), 1)
                pe.wait_ge(S("mix_ready"), b + 1)
                for c in range(2):
                    for k in range(NH2):
                        i = M(ps[:, c, :], w_out[:, k, :], hc[1][:, k, cols[c]], start=(k == 0), stop=(k == NH2 - 1))
                i.then_inc(S("s0_ps"), 1)
                pe.wait_ge(S("sg_ready"), b + 1)
                turn(lambda k: c_sb[0][:, k * P:(k + 1) * P], 2).then_inc(S("sgT_ps"), 1)
                pe.wait_ge(S("xn_ready"), 2 * b + 2)
                turn(lambda k: xn[:, k, :], 0).then_inc(S("xnT_ps"), 1)
                pe.wait_ge(S("xnT_ready"), 2 * b + 2)
                pe.wait_ge(S("x1_ready"), b + 1)
                logits(wg1, 2)

            def count(what, bank):
                for k in range(NBLK):
                    i = M(ps[:, bank, 0:B * E].rearrange("p (b e) -> p b e", e=E), ones_bf[:], what[:, :, k, :],
                          start=(k == 0), stop=(k == NBLK - 1))
                return i

            with pe.Fori(0, ONE_BITS + 1) as i:
                pe.wait_ge(S("over_ready"), i + 1)
                count(over_thr, 0).then_inc(S("count_ps"), 1)
            pe.wait_ge(S("split_ready"), 1)
            count(over_thr, 0)
            ranks = ps[:, 1, 0:B * NBLK * E].rearrange("p (b k e) -> p b k e", b=B, e=E)
            M(ranks, before_tok[:], at_thr[:], start=True, stop=False, skip_group_check=True)
            for k in range(1, NBLK):
                i = M(ranks[:, :, k:, :], ones_bf[:], at_thr[:, :, 0:NBLK - k, :], start=False, stop=(k == NBLK - 1),
                      skip_group_check=True)
            i.then_inc(S("ranks_ps"), 1)
            pe.wait_ge(S("w1_loaded"), N_LOADS1)
            pe.wait_ge(S("setup1"), 2)
            pe.wait_ge(S("need_ready"), 5)
            pe.sem_inc(S("pv_done"), 2)
            pe.sem_inc(S("exp_done"), EXP_AHEAD)
            pe.sem_inc(S("hid_used"), HID_AHEAD)

            with pe.Fori(0, B) as b:
                pe.wait_ge(S("xT_ready"), b + 1)
                for i in range(2):
                    for j in range(2):
                        for c in range(2):
                            m = M(ps[:, 4 * i + 2 * j + c, :], w_qk[:, 2 * i + j, :], xT[:, cols[c]], start=True, stop=True)
                    m.then_inc(S("qk_ps"), 1)
                pe.wait_ge(S("halves_ready"), 2 * b + 1)
                for k in range(NBLK):
                    m = M(ps[:, k // 4, (k % 4) * P:(k % 4 + 1) * P], xT[:, k * P:(k + 1) * P], w_v[:], start=True, stop=True)
                m.then_inc(S("v_ps"), 1)
                pe.wait_ge(S("gpad_ready"), b + 1)
                pe.wait_ge(S("halves_ready"), 2 * b + 2)
                for k in range(NBLK):
                    m = nc.tensor.transpose(ps[0:PARTS, 4 + k // 4, (k % 4) * P:(k % 4 + 1) * P], gpad[:, k, :], ident[:])
                m.then_inc(S("gpadT_ps"), 1)
                pe.wait_ge(S("gparts1_ready"), b + 1)

                def score(h, k):
                    pe.wait_ge(S("top_done"), (b * H + h) * NBLK + k + 1)
                    for c in range(2):
                        m = M(ps[:, 2 * (k % 2) + c, :], q_op[:, h, k * P:(k + 1) * P], k_op[:, h, cols[c]],
                              start=True, stop=True)
                    m.then_inc(S("s_ps"), 1)

                def expert(e, i, heads=None):
                    n = b * E + e
                    pe.wait_ge(S(f"expert_loaded{i}"), 32 * (b * 4 + (e - i) // 2 + 1) if isinstance(e, int)
                               else b * 128 + (e - i) * 16 + 32)
                    for c in range(2):
                        pe.wait_ge(S("hid_ready"), 8 * n + 4 * c + 1)
                        M(ps[:, 4 + c, :], pick[:, e, :], gparts1[:, cols[c]], start=True, stop=True).then_inc(S("gate1_ps"), 1)
                        scores_left = iter(range(NBLK))

                        def fill():
                            if heads is not None:
                                score(heads + c, next(scores_left))

                        def up(q):
                            if q == 1:
                                pe.wait_ge(S("gate_sb_ready"), 2 * n + c + 2)
                            else:
                                pe.wait_ge(S("hid_ready"), 8 * n + 4 * c + max(q, 1) + 1)
                            M(ps[:, 4 + (c + 1 + q) % 2, :], w1[i][:, q * P:(q + 1) * P], xT[:, cols[c]],
                              start=True, stop=True).then_inc(S("hid_ps"), 1)
                            fill()

                        def down(q):
                            pe.wait_ge(S("hid_ready"), 8 * n + 4 * c + q + 3)
                            if q == 0:
                                pe.wait_ge(S("acc_done"), 2 * n + c + 1)
                            M(ps[:, 6 + c, :], w2[i][:, q, :], hid[q], start=(q == 0), stop=(q == 3)).then_inc(S("hid_used"), 1)
                            fill()
                        up(0)
                        up(1)
                        down(0)
                        up(2)
                        down(1)
                        up(3)
                        down(2)
                        down(3)

                expert(0, 0)
                pe.wait_ge(S("ops_loaded0"), 16 * 19 * (b + 1))
                expert(1, 1, heads=0)
                pe.wait_ge(S(f"ops_loaded{H // 2}"), 16 * 18 * (b + 1))
                pe.wait_ge(S("v_ready"), b + 1)
                alone(pe)
                with pe.Fori(1, E // 2) as e2:
                    for i in range(2):
                        e = e2 * 2 + i
                        expert(e, i, heads=2 * e - 2)
                for h in (H - 2, H - 1):
                    for k in range(NBLK):
                        score(h, k)
                pe.wait_ge(S("top_out"), (b + 1) * P // 2 + 2)
                nc.tensor.transpose(ps[:, 0, 0:P], top[:], ident[:]).then_inc(S("top_ps"), 1)
                pe.wait_ge(S("top_loaded"), 16 * b + 16)

                def scores(g, k):
                    i = k % 2
                    for j in range(HG):
                        n = ((b * 4 + g) * 8 + k) * HG + j
                        pe.wait_ge(S("exp_done"), n + 1 - LAG[i * HG + j] + EXP_AHEAD)
                        for c in range(2):
                            m = M(ps[:, 2 * TILE[i * HG + j] + c, :], k_op[:, g * HG + j, k * P:(k + 1) * P],
                                  q_op[:, g * HG + j, cols[c]], start=True, stop=True)
                        m.then_inc(S("sT_ps"), 1)

                def sum_values(g, k):
                    pe.wait_ge(S("exp_done"), ((b * 4 + g) * 8 + k) * HG + HG + EXP_AHEAD)
                    for c in range(2):
                        for j in range(HG):
                            m = M(ps[32 * j:32 * j + 32, 6 + c, :], v_grp[:, k, j, :], big[k % 2][:, j, cols[c]],
                                  start=False, stop=False, skip_group_check=True)
                    m.then_inc(S("pv_done"), 1)

                def turn_o(g):
                    pe.wait_ge(S("o_ready"), b * 4 + g + 1)
                    turn(lambda k: o_T[:, k * P:(k + 1) * P], 6).then_inc(S("o_ps"), 1)
                    pe.wait_ge(S("att_ready"), b * 4 + g + 1)

                def score_group(g, first=False):
                    scores(g, 0)
                    if not first:
                        sum_values(g - 1, NBLK - 1)
                    scores(g, 1)
                    if not first:
                        turn_o(g - 1)
                    pe.wait_ge(S("v_grp_ready"), b * 4 + g + 1)
                    for c in range(2):
                        M(ps[:, 6 + c, :], zeros_bf[:, 0:P], zeros_bf[:], start=True, stop=False, skip_group_check=True)
                    sum_values(g, 0)
                    for k in range(2, NBLK):
                        scores(g, k)
                        sum_values(g, k - 1)
                score_group(0, first=True)
                with pe.Fori(1, H // HG) as g:
                    score_group(g)
                sum_values(H // HG - 1, NBLK - 1)
                turn_o(H // HG - 1)
                pe.wait_ge(S("exp_done"), (b + 1) * P + EXP_AHEAD)
                turn(lambda k: att[:, k, :], 0).then_inc(S("attT_ps"), 1)
                pe.wait_ge(S("attT_ready"), b + 1)
                for c in range(2):
                    m = M(ps[:, 2 + c, :], w_o[:], attT[:, cols[c]], start=True, stop=True)
                m.then_inc(S("s1_ps"), 1)
                pe.wait_ge(S("sg1_ready"), b + 1)
                turn(lambda k: o_T[:, k * P:(k + 1) * P], 0).then_inc(S("sg1_ps"), 1)


def rotary_tables():
    inv = (np.float32(1.0) / np.float32(10000.0) ** (np.arange(0, HD, 2, dtype=np.float32) / np.float32(HD)))
    angle = np.arange(T, dtype=np.float32)[None, :] * inv[:, None].astype(np.float32)
    angle = np.tile(np.concatenate([angle, angle]), (H, 1)).astype(np.float32)
    sign = np.where(np.arange(P) % 2 == 0, -1.0, 1.0).astype(np.float32)[:, None]
    return {"cos": np.cos(angle), "sin": sign * np.sin(angle)}


def host_constants():
    i = np.arange(P)
    bf = mybir.dt.np(BF16)
    pick = np.zeros((PARTS, 2 * NS, P), np.float32)
    for s in range(2 * NS):
        for g in range(3):
            pick[32 * g + s, s, :] = 1.0
    return {
        "ident": np.eye(P, dtype=np.float32),
        "before_tok": (i[:, None] < i[None, :]).astype(bf),
        "pick": pick.astype(bf),
        **rotary_tables(),
        "q_tail": np.zeros((PARTS - 72, H, T), bf),
        "k_tail": np.concatenate([-np.ones((3, H, T), bf), np.zeros((PARTS - 75, H, T), bf)]),
        "rank_w": np.tile(np.arange(E, 0, -1, dtype=np.float32), (P, 1)),
    }


def kernel(**inputs):
    import concourse.bacc as bacc
    from concourse.bass_utils import run_bass_kernel_spmd

    a = {k: np.ascontiguousarray(v) for k, v in inputs.items()}

    def halves(w):
        return w.reshape(2, P, -1).transpose(1, 0, 2)

    swap = np.arange(P) ^ 1
    w_x = halves(a["L0_attn_W_x"].T)
    arrays = {
        "x": a["L0_attn_x"],
        "w_in": a["L0_attn_W_in"].T,
        "taps": a["L0_attn_conv_w"][:, 0, :].T,
        "w_x": np.concatenate([w_x, w_x, w_x], axis=2),
        "w_dt": halves(a["L0_attn_W_dt"].T),
        "w_out": halves(a["L0_attn_W_out"].T),
        "chan": np.stack([a["L0_attn_" + n].reshape(2, P).T
                          for n in ("conv_b", "b_dt", "ln_g", "ln_b", "D_param")], axis=1),
        "a_log": a["L0_attn_A_log"],
        "wg0": a["L0_ffn_wg"],
        "w_e0": a["L0_ffn_W"].transpose(2, 0, 1),
        "b_e0": a["L0_ffn_b"],
        "wg1": a["L1_ffn_gate_w"],
        "w_qk": np.stack([w.T for w in (a["L1_attn_Wq"], a["L1_attn_Wq"][swap], a["L1_attn_Wk"], a["L1_attn_Wk"][swap])],
                         axis=1),
        "b_qk": np.stack([a["L1_attn_bq"], a["L1_attn_bq"][swap], a["L1_attn_bk"], a["L1_attn_bk"][swap],
                          a["L1_attn_bo"]], axis=1),
        "w_v": a["L1_attn_Wv"].T,
        "b_v": a["L1_attn_bv"],
        "w_o": a["L1_attn_Wo"].T,
        "w1": a["L1_ffn_w1"],
        "w2": a["L1_ffn_w2"],
        **host_constants(),
    }
    nc = bacc.Bacc("TRN2", target_bir_lowering=False, num_devices=1)
    arrays = {f"in_{k}": np.ascontiguousarray(v) for k, v in arrays.items()}
    aps = {k[3:]: nc.dram_tensor(k, v.shape, mybir.dt.from_np(v.dtype), kind="ExternalInput").ap()
           for k, v in arrays.items()}
    out = nc.dram_tensor("out", (B, T, D), F32, kind="ExternalOutput").ap()
    mixed_layers(nc, aps, out)
    r = run_bass_kernel_spmd(nc, [arrays], core_ids=[0])
    return r.results[0]["out"]
```

```python
from contextlib import ExitStack

import numpy as np

import concourse.bass as bass
from concourse import mybir

F32 = mybir.dt.float32
BF16 = mybir.dt.bfloat16
I32 = mybir.dt.int32
ALU = mybir.AluOpType
ACT = mybir.ActivationFunctionType
AX_X = mybir.AxisListType.X

P = 128
B, T, D = 4, 1024, 128
NBLK = T // P
HALF = T // 2
DI, NH2 = 256, 2
NS = 16
TAPS = 4
E = 8
CAP0 = B * T // E
K1 = 2 * T // E
H, HD = 16, 8
HG = 4
HID = 512
EPS = 1e-5
PARTS = 96
LOWEST = float(np.finfo(np.float32).min)
ONE_BITS = 29


def mixed_layers(nc, t, out):
    with ExitStack() as ctx:
        def sb(name, shape, dt=F32, stack=ctx):
            return stack.enter_context(nc.sbuf_tensor(name, shape, dt))

        def sem(name):
            return ctx.enter_context(nc.semaphore(name))

        ps = ctx.enter_context(nc.psum_tensor("ps", [P, 8, HALF], F32))

        def banks(b, n, parts=P):
            return ps[0:parts, b:b + n, :].rearrange("p b c -> p (b c)")

        def over(ap, axis, n):
            v = ap.unsqueeze(axis)
            shape = list(v.shape)
            shape[axis] = n
            return v.broadcast_to(shape)

        ident = sb("ident", [P, P])
        before_tok = sb("before_tok", [P, P], BF16)
        ones_bf = sb("ones_bf", [P, P], BF16)
        zeros_bf = sb("zeros_bf", [P, HALF], BF16)
        pick = sb("pick", [PARTS, 2 * NS, P], BF16)
        rank_w = sb("rank_w", [P, E])
        eps_col = sb("eps_col", [P, 1])
        wg1 = sb("wg1", [P, E])
        x_all = sb("x_all", [P, B, NBLK, D])
        xnT_all = sb("xnT_all", [P, B, TAPS - 1 + T])
        probs = sb("probs", [P, B, NBLK, E])
        gate1 = sb("gate1", [P, B, NBLK, E])
        l0 = ExitStack()
        def sb0(name, shape, dt=F32):
            return sb(name, shape, dt, l0)
        bn = sb0("bn", [P, B * NBLK, 6])
        mv = sb0("mv", [P, B * NBLK, 2])
        std = sb0("std", [P, B * NBLK])
        rstd = sb0("rstd", [P, B * NBLK])
        xn = [sb0(f"xn{i}", [P, NBLK, D]) for i in range(2)]
        lg = sb0("lg", [P, B * NBLK, E])
        ex = sb0("ex", [P, B * NBLK, E])
        m8 = sb0("m8", [P, B * NBLK])
        s8 = sb0("s8", [P, B * NBLK])
        r8 = sb0("r8", [P, B * NBLK])
        w_in = sb0("w_in", [P, 2 * DI])
        tap_b = sb0("tap_b", [P, TAPS, DI])
        w_tap = sb0("w_tap", [P, TAPS, DI])
        w_x = sb0("w_x", [P, NH2, PARTS])
        w_dt = sb0("w_dt", [P, NH2, DI])
        w_out = sb0("w_out", [P, NH2, D])
        chan = sb0("chan", [P, 5, NH2])
        mean_w = sb0("mean_w", [P, P])
        a_log = sb0("a_log", [P, NS])
        a_exp = sb0("a_exp", [P, NS])
        a_neg = sb0("a_neg", [P, NS])
        wg0 = sb0("wg0", [P, E])
        w_e0 = sb0("w_e0", [P, E, D])
        b_e0 = sb0("b_e0", [E, D])
        zs = sb0("zs", [P, NH2, T])
        xc = sb0("xc", [P, NH2, T])
        skip = sb0("skip", [P, NH2, T])
        dt_ = sb0("dt_", [P, NH2, T])
        bc = sb0("bc", [PARTS, T], BF16)
        mid = sb0("mid", [PARTS, T], BF16)
        rest = sb0("rest", [PARTS, T])
        dA = [sb0(f"dA{i}", [P, NH2, T]) for i in range(2)]
        hs = [sb0(f"hs{i}", [P, NH2, T]) for i in range(2)]
        hc = [sb0(f"hc{i}", [P, NH2, T]) for i in range(2)]
        c_sb = [sb0(f"c_sb{i}", [P, T]) for i in range(2)]
        probs0 = sb0("probs0", [P, B * NBLK, E])
        pmax = sb0("pmax", [P, B * NBLK])
        eqw = sb0("eqw", [P, B * NBLK, E])
        first = sb0("first", [P, B * NBLK])
        choice = sb0("choice", [P, B * NBLK, E])
        choice_bf = sb0("choice_bf", [P, B * NBLK, E], BF16)
        kept = sb0("kept", [P, B * NBLK, E])
        gates0 = sb0("gates0", [P, B, NBLK, E])
        gate0 = sb0("gate0", [P, NBLK, PARTS])
        gateT = sb0("gateT", [E, T])
        gparts = sb0("gparts", [PARTS, T], BF16)
        s_gT = sb0("s_gT", [P, T])
        xg = [sb0(f"xg{i}", [P, T]) for i in range(2)]
        l0.close()

        cos = sb("cos", [P, T])
        sin = sb("sin", [P, T])
        w_qk = sb("w_qk", [P, 4, P])
        b_qk = sb("b_qk", [P, 5])
        w_v = sb("w_v", [P, P])
        b_v = sb("b_v", [P, P])
        w_o = sb("w_o", [P, P])
        xT = sb("xT", [P, T])
        q_op = sb("q_op", [PARTS, H, T], BF16)
        k_op = sb("k_op", [PARTS, H, T], BF16)
        big = [sb(f"big{i}", [P, HG, T]) for i in range(2)]
        v_tok = sb("v_tok", [P, NBLK, P])
        v_grp = sb("v_grp", [P, NBLK, HG, 32])
        top = sb("top", [P, H * NBLK])
        top_parts = sb("top_parts", [P, 3, P], BF16)
        top_rest = sb("top_rest", [P, P])
        o_T = sb("o_T", [P, T])
        rsum = sb("rsum", [P, NBLK, HG])
        att = sb("att", [P, NBLK, P])
        attT = sb("attT", [P, T])
        s1T = sb("s1T", [P, T])
        w1 = [sb(f"w1_{i}", [P, HID]) for i in range(2)]
        w2 = [sb(f"w2_{i}", [P, HID // P, D]) for i in range(2)]
        acc_bf = sb("acc_bf", [P, T], BF16)
        silu_bf = sb("silu_bf", [P, T], BF16)
        gpad = sb("gpad", [P, NBLK, PARTS])
        gparts1 = sb("gparts1", [PARTS, T], BF16)
        thr = sb("thr", [P, B, E], I32)
        bit = sb("bit", [P, B, E], I32)
        cand = sb("cand", [P, B, E], I32)
        step = sb("step", [P, B, E], I32)
        over_thr = sb("over_thr", [P, B, NBLK, E], BF16)
        at_thr = sb("at_thr", [P, B, NBLK, E], BF16)
        need = sb("need", [P, B, E])
        picked = sb("picked", [P, B, NBLK, E])
        flat = [t_[:].rearrange("p h t -> p (h t)") for t_ in big]
        rot = [flat[0][:, j * T:(j + 1) * T] for j in range(2)]
        qk_parts = [f[:, n:n + 3 * T // 2].bitcast(BF16).rearrange("p (j t) -> p j t", j=3)
                    for f, n in ((flat[0], 2 * T), (flat[1], 0))]
        hid = [flat[1][:, 3 * HALF + j * HALF:3 * HALF + (j + 1) * HALF] for j in range(4)]
        weighted = flat[1][:, 7 * HALF:8 * HALF]
        top_run = [flat[0][:, j * T:(j + 1) * T].rearrange("p (k t) -> p k t", k=2) for j in range(2)]
        half_sb = [flat[0][:, 2 * T + j * HALF:2 * T + (j + 1) * HALF] for j in range(4)]
        gate_sb = [o_T[:, j * HALF:(j + 1) * HALF] for j in range(2)]
        grest = flat[1][0:PARTS, 3 * HALF:5 * HALF]
        gmid = acc_bf[0:PARTS]
        acc = attT
        parts_dram = nc.dram_tensor("parts_dram", (2, 3, P, T), BF16, kind="Internal").ap()
        top_dram = nc.dram_tensor("top_dram", (3, H * NBLK, P), BF16, kind="Internal").ap()

        sems = {}

        def S(name):
            if name not in sems:
                sems[name] = sem(name)
            return sems[name]

        loads = [
            (ident[:], t["ident"]), (before_tok[:], t["before_tok"]), (pick[:], t["pick"]),
            (rank_w[:], t["rank_w"]), (wg1[:], t["wg1"]),
            (w_in[:], t["w_in"]), (tap_b[:], t["taps"].partition_broadcast(P)),
            (w_x[:], t["w_x"]), (w_dt[:], t["w_dt"]), (w_out[:], t["w_out"]), (chan[:], t["chan"]),
            (a_log[:], t["a_log"].partition_broadcast(P)), (wg0[:], t["wg0"]), (w_e0[:], t["w_e0"]),
            (b_e0[:], t["b_e0"]),
        ]
        N_LOADS = 16 * len(loads)
        loads1 = [
            (cos[:], t["cos"]), (sin[:], t["sin"]), (w_qk[:], t["w_qk"]), (b_qk[:], t["b_qk"]), (w_v[:], t["w_v"]),
            (b_v[:], t["b_v"].partition_broadcast(P)), (w_o[:], t["w_o"]),
            (q_op[72:PARTS], t["q_tail"]), (k_op[72:PARTS], t["k_tail"]),
        ]
        N_LOADS1 = 16 * len(loads1)
        TOP_AHEAD = 4
        HALF_AHEAD = 2
        HID_AHEAD = 16
        DVE_PART = 5 * T // 8
        EXP_AHEAD = 5
        TILE = (0, 1, 2, 0, 1, 2, 0, 1)
        LAG = (2, 2, 5, 3, 3, 3, 3, 3)
        conv_b, b_dt, ln_g, ln_b, d_par = (chan[:, i, :] for i in range(5))

        def y_ps(c):
            return ps[:, 4:8, :].rearrange("p (h c) t -> p c h t", c=2)[:, c]

        def alone(engine):
            engine.sem_inc(S("passed"), 1)

        cols = [slice(c * HALF, (c + 1) * HALF) for c in range(2)]
        block = ctx.enter_context(nc.Block())

        @block.sync
        def _(sp):
            for b in range(B):
                sp.dma_start(x_all[:, b], t["x"][b].rearrange("(k p) d -> p k d", p=P)).then_inc(S(f"x_loaded{b}"), 16)
            for dst, src in loads:
                sp.dma_start(dst, src).then_inc(S("w_loaded"), 16)

            sp.wait_ge(S("probs_ready"), 2)
            for dst, src in loads1:
                sp.dma_start(dst, src).then_inc(S("w1_loaded"), 16)

            def store_parts(b, i):
                sp.wait_ge(S("qk_parts_ready"), 2 * b + i + 1)
                sp.dma_start(parts_dram[i].rearrange("j p t -> p j t"), qk_parts[i]).then_inc(S(f"parts_stored{i}"), 16)

            sp.sem_inc(S(f"ops_loaded{H // 2}"), 1)

            def first_weights(b):
                for e in range(2):
                    sp.wait_ge(S("hid_used"), 8 * (b * E + e) - 8 + HID_AHEAD)
                    sp.dma_start(w1[e][:], t["w1"][e]).then_inc(S(f"expert_loaded{e}"), 16)
                    sp.dma_start(w2[e][:], t["w2"][e].rearrange("(m p) d -> p m d", p=P)).then_inc(S(f"expert_loaded{e}"), 16)

            def sequence(b, more):
                sp.wait_ge(S("pv_done"), b * 32 + 2)
                sp.dma_start(q_op[72:75], t["q_tail"][0:3]).then_inc(S("ops_loaded0"), 16)

                def load_ops(op, i, h0):
                    hh = slice(h0, h0 + H // 2)
                    for j in range(9):
                        part = parts_dram[i, (j // 3, j % 3)[i]].rearrange("(h d) t -> d h t", d=HD)
                        sp.dma_start(op[j * HD:(j + 1) * HD, hh], part[:, hh]).then_inc(S(f"ops_loaded{h0}"), 16)
                store_parts(b, 0)
                sp.wait_ge(S("parts_stored0"), 16 * b + 16)
                load_ops(q_op, 0, 0)
                store_parts(b, 1)
                sp.wait_ge(S("parts_stored1"), 16 * b + 16)
                load_ops(k_op, 1, 0)
                load_ops(q_op, 0, H // 2)
                load_ops(k_op, 1, H // 2)
                with sp.Fori(1, E // 2) as e2:
                    for i in range(2):
                        e = e2 * 2 + i
                        sp.wait_ge(S("hid_used"), 8 * (b * E + e) - 8 + HID_AHEAD)
                        sp.dma_start(w1[i][:], t["w1"][e]).then_inc(S(f"expert_loaded{i}"), 16)
                        sp.dma_start(w2[i][:], t["w2"][e].rearrange("(m p) d -> p m d", p=P)).then_inc(S(f"expert_loaded{i}"), 16)
                sp.wait_ge(S("top_parts_ready"), b + 1)
                sp.dma_start(top_dram.rearrange("j r q -> r j q"), top_parts[:]).then_inc(S("top_stored"), 16)
                sp.wait_ge(S("top_stored"), 16 * b + 16)
                sp.dma_start(q_op[72:75], top_dram.rearrange("j (h k) q -> j h (k q)", h=H)).then_inc(S("top_loaded"), 16)
                if more:
                    first_weights(b + 1)
                sp.wait_ge(S("out_ready"), b + 2)
                sp.dma_start(out[b].rearrange("(k p) d -> p k d", p=P), x_all[:, b]).then_inc(S("stored"), 16)

            first_weights(0)
            with sp.Fori(0, B - 1) as b:
                sequence(b, True)
            sequence(B - 1, False)
            sp.wait_ge(S("stored"), 16 * B)

        @block.gpsimd
        def _(pool):
            pool.wait_ge(S("w_loaded"), N_LOADS)
            for k in range(TAPS):
                i = nc.gpsimd.tensor_tensor(w_tap[:, k, :], w_in[:, 0:DI], tap_b[:, k, :], ALU.mult)
            i.then_inc(S("taps_ready"), 1)
            pool.sem_inc(S("hc_ready"), 2)

            def times_c(i, n):
                pool.wait_ge(S("scanned"), n + 3)
                pool.wait_ge(S("c_ready"), n + 2)
                pool.wait_ge(S("summed"), n + 1)
                nc.gpsimd.tensor_tensor(hc[i][:, 0, DVE_PART:], hs[i][:, 0, DVE_PART:], c_sb[i][:, DVE_PART:], ALU.mult)
                nc.gpsimd.tensor_tensor(hc[i][:, 1], hs[i][:, 1], c_sb[i][:], ALU.mult).then_inc(S("hc_ready"), 1)

            with pool.Fori(0, B) as b:
                for n, h in enumerate((1, 0)):
                    pool.wait_ge(S("u1_ready"), 2 * b + n + 1)
                    nc.gpsimd.tensor_tensor(hc[0][:, h], hs[1][:, h], dA[0][:, h], ALU.subtract).then_inc(S("lost_ready"), 1)
                with pool.Fori(0, NS // 2) as s2:
                    for i in range(2):
                        times_c(i, b * NS + s2 * 2 + i)

            with pool.Fori(0, B) as b:
                pool.wait_ge(S("acc_zero"), b + 1)
                alone(pool)
                with pool.Fori(0, E) as e:
                    for c in range(2):
                        n = (b * E + e) * 2 + c
                        pool.wait_ge(S("weighted_ready"), n + 2)
                        pool.wait_ge(S("acc_done"), n + 2)
                        nc.gpsimd.tensor_tensor(acc[:, cols[c]], acc[:, cols[c]], weighted, ALU.add).then_inc(S("acc_done"), 1)

        @block.scalar
        def _(act):
            A = nc.scalar.activation
            act.wait_ge(S("w_loaded"), N_LOADS)
            A(a_exp[:], a_log[:], ACT.Exp).then_inc(S("a_exp_ready"), 1)
            act.sem_inc(S("c_ready"), 1)
            act.wait_ge(S("setup"), 1)

            def norms(n):
                act.wait_ge(S("var_ready"), n + 1)
                A(std[:], mv[:, :, 1], ACT.Sqrt, bias=eps_col[:]).then_inc(S("std_ready"), 1)
                for b in range(B):
                    act.wait_ge(S("xnT_ps"), n * B + b + 1)
                    A(xnT_all[:, b, TAPS - 1:], banks(2 * (b % 3), 2), ACT.Copy).then_inc(S("xnT_ready"), 1)
                act.wait_ge(S("lg_ready"), n + 1)
                A(ex[:], lg[:], ACT.Exp).then_inc(S("ex_ready"), 1)

            def decay(i, s, n):
                act.wait_ge(S("scanned"), n + 1)
                act.wait_ge(S("dt_seen"), 1)
                A(dA[i][:, :, 1:], dt_[:, :, 1:], ACT.Exp, scale=a_neg[:, bass.ds(s, 1)]).then_inc(S("decay_ready"), 1)

            def keep_c(i, n):
                act.wait_ge(S("c_ps"), n + 1)
                act.wait_ge(S("hc_ready"), n + 1)
                act.wait_ge(S("c_used"), n + 1)
                A(c_sb[i][:], banks(2, 2), ACT.Copy).then_inc(S("c_ready"), 1)

            def front(b):
                act.wait_ge(S("conv_ps"), 2 * b + 1)
                A(xc[:, 0, :], banks(0, 2), ACT.Silu, bias=conv_b[:, 0:1]).then_inc(S("xc_ready"), 1)
                act.wait_ge(S("gateT_ps"), b + 1)
                A(gateT[:], banks(6, 2, E), ACT.Copy)
                A(gparts[:], banks(6, 2, PARTS), ACT.Copy).then_inc(S("part1"), 1)
                act.wait_ge(S("conv_ps"), 2 * b + 2)
                A(xc[:, 1, :], banks(4, 2), ACT.Silu, bias=conv_b[:, 1:2]).then_inc(S("xc_ready"), 1)
                act.wait_ge(S("rest_ready"), 2 * b + 1)
                A(gparts[32:64, :], rest[32:64, :], ACT.Copy)
                A(mid[64:96, :], rest[64:96, :], ACT.Copy).then_inc(S("part2"), 1)

            def middle(b):
                for n, h in enumerate((1, 0)):
                    act.wait_ge(S("dt_ps"), 2 * b + 2)
                    if h == 0:
                        act.wait_ge(S("relu_ready"), 2 * b + 1)
                    A(dt_[:, h, :], banks(2 + 2 * h, 2), ACT.Abs, bias=b_dt[:, h:h + 1]).then_inc(S("abs_ready"), 1)
                for n, h in enumerate((1, 0)):
                    act.wait_ge(S("abs_ready"), 2 * b + n + 1)
                    A(dA[0][:, h], dt_[:, h], ACT.Exp, scale=-1.0).then_inc(S("u_ready"), 1)
                for n, h in enumerate((1, 0)):
                    act.wait_ge(S("u_ready"), 2 * b + n + 1)
                    A(dA[1][:, h], dA[0][:, h], ACT.Ln, bias=1.0).then_inc(S("ln_ready"), 1)
                act.wait_ge(S("bc_ps"), b + 1)
                A(bc[:], banks(0, 2, PARTS), ACT.Copy).then_inc(S("part1"), 1)
                for h in range(NH2):
                    i = A(skip[:, h, :], xc[:, h, :], ACT.Identity, scale=d_par[:, h:h + 1], bias=ln_b[:, h:h + 1])
                i.then_inc(S("skip_ready"), 1)
                act.wait_ge(S("rest_ready"), 2 * b + 2)
                A(bc[32:64, :], rest[32:64, :], ACT.Copy)
                A(mid[64:96, :], rest[64:96, :], ACT.Copy).then_inc(S("part2"), 1)
                act.wait_ge(S("dt_ready"), 2 * b + 2)
                for i in range(2):
                    decay(i, i, b * NS + i)
                act.wait_ge(S("ffn_done"), b * E + E + 2)
                A(s_gT[:], banks(6, 2), ACT.Silu).then_inc(S("s_g_ready"), 1)
                for i in range(2):
                    keep_c(i, b * NS + i)
                with act.Fori(1, NS // 2) as s2:
                    for i in range(2):
                        decay(i, s2 * 2 + i, b * NS + s2 * 2 + i)
                        keep_c(i, b * NS + s2 * 2 + i)

            def tail(b):
                act.wait_ge(S("summed"), b * NS + NS + 2)
                for c in range(2):
                    A(hs[0][:, :, cols[c]], y_ps(c), ACT.Copy).then_inc(S("y_ready"), 1)
                for c in range(2):
                    act.wait_ge(S("yc_ready"), 2 * b + c + 1)
                    A(dA[0][:, :, cols[c]], hs[1][:, :, cols[c]], ACT.Square).then_inc(S("sq_ready"), 1)
                for c in range(2):
                    act.wait_ge(S("yvar_ps"), 2 * b + c + 1)
                    A(c_sb[0][:, cols[c]], ps[:, 2 + c, :], ACT.Ln, bias=eps_col[:]).then_inc(S("lnvar"), 1)
                for c in range(2):
                    act.wait_ge(S("lnvar"), 2 * b + c + 1)
                    A(c_sb[1][:, cols[c]], c_sb[0][:, cols[c]], ACT.Exp, scale=-0.5).then_inc(S("yrstd_ready"), 1)
                for c in range(2):
                    act.wait_ge(S("z_ps"), 2 * b + c + 1)
                    A(zs[:, :, cols[c]], y_ps(c), ACT.Silu).then_inc(S("zs_ready"), 1)

            norms(0)
            act.wait_ge(S("a_neg_ready"), 1)
            front(0)
            with act.Fori(0, B - 1) as b:
                middle(b)
                tail(b)
                front(b + 1)
            middle(B - 1)
            tail(B - 1)
            norms(1)
            act.sem_inc(S("s_half"), HALF_AHEAD)
            act.sem_inc(S("hid_ready"), 2)
            act.sem_inc(S("gate_sb_ready"), 1)

            act.wait_ge(S("w1_loaded"), N_LOADS1)

            def first_gates(b):
                act.wait_ge(S("gpadT_ps"), b + 1)
                A(gparts1[:], banks(4, 2, PARTS), ACT.Copy).then_inc(S("gpart1"), 1)

            def second_gates(b):
                act.wait_ge(S("grest_ready"), b + 1)
                A(gparts1[32:64, :], grest[32:64, :], ACT.Copy)
                A(gmid[64:96, :], grest[64:96, :], ACT.Copy).then_inc(S("gpart2"), 1)

            def first_part(b, i):
                act.wait_ge(S("rot_ready"), 2 * b + i + 1)
                A(qk_parts[i][:, 0, :], rot[0], ACT.Copy).then_inc(S("qk_part1"), 1)

            def second_part(b, i):
                act.wait_ge(S("qk_rest"), 2 * b + i + 1)
                A(qk_parts[i][:, 1, :], rot[1], ACT.Copy).then_inc(S("qk_part2"), 1)

            def middle(b):
                def half_out(h, k):
                    n = (b * H + h) * NBLK + k
                    act.wait_ge(S("s_far_ps"), n + 1)
                    act.wait_ge(S("top_done"), n - 3 + TOP_AHEAD)
                    A(half_sb[k % 4], ps[:, 3 + k % 2, :], ACT.Copy).then_inc(S("s_half"), 1)

                def expert(n, between):
                    for c in range(2):
                        act.wait_ge(S("gate1_ps"), 2 * n + c + 1)
                        act.wait_ge(S("acc_done"), 2 * n + c + 1)
                        A(gate_sb[c], ps[:, 5 + c, :], ACT.Copy).then_inc(S("gate_sb_ready"), 1)
                        between(c, 0)
                        for q in range(4):
                            u = 8 * n + 4 * c + q
                            act.wait_ge(S("hid_ps"), u + 1)
                            act.wait_ge(S("hid_used"), u - 3 + HID_AHEAD)
                            A(hid[q], ps[:, 5 + (c + 1 + q) % 2, :], ACT.Gelu_apprx_tanh).then_inc(S("hid_ready"), 1)
                            between(c, q + 1)

                def qk_between(c, step):
                    if c == 0 and step == 2:
                        first_part(b, 1)
                    if c == 0 and step == 4:
                        second_part(b, 1)

                def nothing(c, step):
                    pass

                expert(b * E, qk_between)
                expert(b * E + 1, nothing)
                with act.Fori(1, E // 2 - 1) as e2:
                    for i in range(2):
                        def halves_between(c, step):
                            for u in ((), range(2), range(2, 6), range(6, 10), range(10, 16))[step]:
                                half_out(e2 * 8 - 8 + i * 4 + c * 2 + u // NBLK, u % NBLK)
                        expert(b * E + e2 * 2 + i, halves_between)
                act.wait_ge(S("top_ps"), b + 1)
                A(top_parts[:, 0, :], ps[:, 0, 0:P], ACT.Copy).then_inc(S("top_part1"), 1)
                act.wait_ge(S("top_rest_ready"), b + 1)
                A(top_parts[:, 1, :], top_rest[:], ACT.Copy).then_inc(S("top_part2"), 1)
                for e in (E - 2, E - 1):
                    expert(b * E + e, nothing)
                def exps(i, m):
                    act.wait_ge(S("pv_done"), m + 1)
                    for j in range(HG):
                        act.wait_ge(S("sT_ps"), m * HG + j + 1)
                        A(big[i][:, j, :], banks(2 * TILE[i * HG + j], 2), ACT.Exp, scale=HD ** -0.5).then_inc(S("exp_done"), 1)

                def keep_o(ng):
                    act.wait_ge(S("pv_done"), ng * 8 + 8 + 2)
                    A(o_T[:], banks(6, 2), ACT.Copy).then_inc(S("o_ready"), 1)

                def exp_group(g, first=False):
                    m0 = (b * 4 + g) * 8
                    exps(0, m0)
                    if not first:
                        keep_o(b * 4 + g - 1)
                    exps(1, m0 + 1)
                    with act.Fori(1, NBLK // 2) as k2:
                        for i in range(2):
                            exps(i, m0 + k2 * 2 + i)
                act.wait_ge(S("acc_done"), 2 * E * b + 2 * E + 2)
                exp_group(0, first=True)
                with act.Fori(1, H // HG) as g:
                    exp_group(g)
                keep_o(b * 4 + 3)

            def tail(b, more):
                if more:
                    first_gates(b + 1)
                A(acc_bf[:], acc[:], ACT.Copy).then_inc(S("acc_bf_ready"), 1)
                act.wait_ge(S("acc_bf_ready"), b + 1)
                A(silu_bf[:], acc_bf[:], ACT.Silu).then_inc(S("silu_ready"), 1)
                act.wait_ge(S("attT_ps"), b + 1)
                A(attT[:], banks(6, 2), ACT.Copy).then_inc(S("attT_ready"), 1)
                if more:
                    act.wait_ge(S("silu_ready"), b + 1)
                    second_gates(b + 1)
                    first_part(b + 1, 0)
                act.wait_ge(S("s1_ps"), b + 1)
                A(s1T[:], banks(4, 2), ACT.Identity, bias=b_qk[:, 4:5]).then_inc(S("s1_ready"), 1)
                if more:
                    second_part(b + 1, 0)

            first_gates(0)
            second_gates(0)
            first_part(0, 0)
            second_part(0, 0)
            with act.Fori(0, B - 1) as b:
                middle(b)
                tail(b, True)
            middle(B - 1)
            tail(B - 1, False)

        @block.vector
        def _(dve):
            V = nc.vector
            V.memset(ones_bf[:], 1.0)
            V.memset(zeros_bf[:], 0.0)
            V.memset(mean_w[:], 1.0 / DI)
            V.memset(xnT_all[:, :, 0:TAPS - 1], 0.0)
            V.memset(gate0[:], 0.0)
            V.memset(eps_col[:], EPS).then_inc(S("setup"), 1)
            dve.sem_inc(S("scanned"), 2)
            dve.sem_inc(S("b_used"), 1)
            dve.sem_inc(S("c_used"), 2)
            dve.sem_inc(S("parts_ready"), 1)
            dve.sem_inc(S("dt_seen"), 1)
            dve.sem_inc(S("x1_ready"), 1)

            def norms(n):
                tokens = x_all[:].rearrange("p b k d -> p (b k) d")
                for k in range(B * NBLK):
                    if n == 0 and k % NBLK == 0:
                        dve.wait_ge(S(f"x_loaded{k // NBLK}"), 16)
                    i = V.bn_stats(bn[:, k, :], tokens[:, k, :])
                i.then_inc(S("stats_ready"), 1)
                dve.wait_ge(S("stats_ready"), n + 1)
                for k in range(B * NBLK):
                    i = V.bn_aggr(mv[:, k, :], bn[:, k, :])
                i.then_inc(S("var_ready"), 1)
                dve.wait_ge(S("std_ready"), n + 1)
                V.reciprocal(rstd[:], std[:]).then_inc(S("rstd_ready"), 1)
                dve.wait_ge(S("rstd_ready"), n + 1)
                for b in range(B):
                    if n * B + b >= 2:
                        dve.wait_ge(S("xnT_ps"), n * B + b - 1)
                    for k in range(NBLK):
                        r = b * NBLK + k
                        i = V.tensor_scalar(xn[b % 2][:, k, :], x_all[:, b, k, :], mv[:, r, 0:1], rstd[:, r:r + 1],
                                            ALU.subtract, ALU.mult)
                    i.then_inc(S("xn_ready"), 1)

            def router(n, result):
                logits = ps[:, 6, 0:B * NBLK * E].rearrange("p (k e) -> p k e", e=E)
                dve.wait_ge(S("lg_ps"), n + 1)
                V.tensor_reduce(m8[:], logits, AX_X, ALU.max).then_inc(S("m8_ready"), 1)
                dve.wait_ge(S("m8_ready"), n + 1)
                V.tensor_tensor(lg[:], logits, over(m8[:], 2, E), ALU.subtract).then_inc(S("lg_ready"), 1)
                dve.wait_ge(S("ex_ready"), n + 1)
                V.tensor_reduce(s8[:], ex[:], AX_X, ALU.add).then_inc(S("s8_ready"), 1)
                dve.wait_ge(S("s8_ready"), n + 1)
                V.reciprocal(r8[:], s8[:]).then_inc(S("r8_ready"), 1)
                dve.wait_ge(S("r8_ready"), n + 1)
                V.tensor_tensor(result, ex[:], over(r8[:], 2, E), ALU.mult).then_inc(S("probs_ready"), 1)
                dve.wait_ge(S("probs_ready"), n + 1)

            def second_parts(parts, bank, n):
                dve.wait_ge(S("part1"), n + 1)
                dve.wait_ge(S("parts_ready"), n + 1)
                V.tensor_tensor(rest[:], banks(bank, 2, PARTS), parts[:], ALU.subtract).then_inc(S("rest_ready"), 1)

            def third_parts(parts, n):
                dve.wait_ge(S("rest_ready"), n + 1)
                dve.wait_ge(S("part2"), n + 1)
                V.tensor_tensor(parts[64:96, :], rest[64:96, :], mid[64:96, :], ALU.subtract).then_inc(S("parts_ready"), 1)

            def times_c(i, n):
                dve.wait_ge(S("c_ready"), n + 2)
                dve.wait_ge(S("summed"), n + 1)
                dve.wait_ge(S("scanned"), n + 3)
                V.tensor_tensor(hc[i][:, 0, 0:DVE_PART], hs[i][:, 0, 0:DVE_PART], c_sb[i][:, 0:DVE_PART],
                                ALU.mult).then_inc(S("c_used"), 1)

            def scan_step(i, n, first=False):
                dve.wait_ge(S("b_ps"), n + 1)
                dve.wait_ge(S("hc_ready"), n + 1)
                dve.wait_ge(S("c_used"), n + 1)
                V.tensor_tensor(hs[i][:], xc[:], over(banks(0, 2), 1, NH2), ALU.mult).then_inc(S("b_used"), 1)
                if not first:
                    times_c(1 - i, n - 1)
                dve.wait_ge(S("b_used"), n + 2)
                dve.wait_ge(S("decay_ready"), n + 1)
                h = hs[i][:].rearrange("p h t -> p (h t)")
                V.tensor_tensor_scan(h, dA[i][:].rearrange("p h t -> p (h t)"), h, 0.0,
                                     ALU.mult, ALU.add).then_inc(S("scanned"), 1)

            norms(0)
            dve.wait_ge(S("w_loaded"), N_LOADS)
            dve.wait_ge(S("a_exp_ready"), 1)
            V.tensor_scalar(a_neg[:], a_exp[:], -1.0, None, ALU.mult).then_inc(S("a_neg_ready"), 1)
            router(0, probs0[:])
            V.tensor_reduce(pmax[:], probs0[:], AX_X, ALU.max).then_inc(S("pmax_ready"), 1)
            dve.wait_ge(S("pmax_ready"), 1)
            V.tensor_tensor(eqw[:], probs0[:], over(pmax[:], 2, E), ALU.is_equal).then_inc(S("eq_ready"), 1)
            dve.wait_ge(S("eq_ready"), 1)
            V.tensor_tensor(eqw[:], eqw[:], over(rank_w[:], 1, B * NBLK), ALU.mult).then_inc(S("eqw_ready"), 1)
            dve.wait_ge(S("eqw_ready"), 1)
            V.tensor_reduce(first[:], eqw[:], AX_X, ALU.max).then_inc(S("first_ready"), 1)
            dve.wait_ge(S("first_ready"), 1)
            V.tensor_tensor(choice_bf[:], eqw[:], over(first[:], 2, E), ALU.is_equal).then_inc(S("choice_ready"), 1)
            V.tensor_tensor(choice[:], eqw[:], over(first[:], 2, E), ALU.is_equal).then_inc(S("choice_f32_ready"), 1)
            dve.wait_ge(S("pos_ps"), 1)
            dve.wait_ge(S("choice_f32_ready"), 1)
            V.scalar_tensor_tensor(kept[:], ps[:, 7, 0:B * NBLK * E].rearrange("p (k e) -> p k e", e=E), float(CAP0),
                                   choice[:], ALU.is_lt, ALU.mult).then_inc(S("kept_ready"), 1)
            dve.wait_ge(S("kept_ready"), 1)
            V.tensor_tensor(gates0[:].rearrange("p b k e -> p (b k) e"), kept[:], probs0[:], ALU.mult).then_inc(S("gates0_ready"), 1)
            dve.wait_ge(S("gates0_ready"), 1)

            def front(b):
                for g in range(3):
                    i = V.tensor_scalar(gate0[:, :, 32 * g:32 * g + E], gates0[:, b], 1.0, None, ALU.mult)
                i.then_inc(S("gate0_ready"), 1)

            def middle(b):
                def expert_in(*experts):
                    for e in experts:
                        dve.wait_ge(S("gate_ps"), b * E + e + 1)
                        dve.wait_ge(S("ffn_done"), b * E + e + 1)
                        V.tensor_tensor(xg[e % 2][:], xnT_all[:, b, TAPS - 1:], banks(2 + 2 * (e % 2), 2),
                                        ALU.mult).then_inc(S("xg_ready"), 1)
                dve.wait_ge(S("dt_ps"), 2 * b + 1)
                for h in range(NH2):
                    if h == 1:
                        dve.wait_ge(S("abs_ready"), 2 * b + 1)
                    V.tensor_scalar(hs[0][:, h, :], banks(2 + 2 * h, 2), b_dt[:, h:h + 1], 0.0, ALU.add,
                                    ALU.max).then_inc(S("relu_ready"), 1)
                for n, h in enumerate((1, 0)):
                    dve.wait_ge(S("u_ready"), 2 * b + n + 1)
                    V.tensor_scalar(hs[1][:, h], dA[0][:, h], 1.0, -1.0, ALU.add, ALU.add).then_inc(S("u1_ready"), 1)
                expert_in(0, 1)
                for n, h in enumerate((1, 0)):
                    dve.wait_ge(S("ln_ready"), 2 * b + n + 1)
                    V.tensor_tensor(hs[0][:, h], hs[0][:, h], dA[1][:, h], ALU.add).then_inc(S("relu_ln_ready"), 1)
                second_parts(bc, 0, 2 * b + 1)
                expert_in(2)
                for n, h in enumerate((1, 0)):
                    dve.wait_ge(S("lost_ready"), 2 * b + n + 1)
                    dve.wait_ge(S("relu_ln_ready"), 2 * b + n + 1)
                    V.tensor_tensor(dt_[:, h], hs[0][:, h], hc[0][:, h], ALU.subtract).then_inc(S("dt_ready"), 1)
                    expert_in(3 + n)
                for i in range(2):
                    V.memset(dA[i][:, :, 0:1], 0.0)
                dve.wait_ge(S("dt_ready"), 2 * b + 2)
                dve.wait_ge(S("skip_ready"), b + 1)
                V.tensor_tensor(xc[:], dt_[:], xc[:], ALU.mult).then_inc(S("dtx_ready"), 1)
                expert_in(5)
                third_parts(bc, 2 * b + 1)
                expert_in(6, 7)
                scan_step(0, b * NS, first=True)
                scan_step(1, b * NS + 1)
                with dve.Fori(1, NS // 2) as s2:
                    for i in range(2):
                        scan_step(i, b * NS + s2 * 2 + i)
                times_c(1, b * NS + NS - 1)

            def tail(b, more):
                if more:
                    front(b + 1)
                for c in range(2):
                    dve.wait_ge(S("ymean_ps"), 2 * b + c + 1)
                    V.tensor_tensor(hs[1][:, :, cols[c]], hs[0][:, :, cols[c]], over(ps[:, c, :], 1, NH2),
                                    ALU.subtract).then_inc(S("yc_ready"), 1)
                for c in range(2):
                    dve.wait_ge(S("yc_ready"), 2 * b + c + 1)
                    dve.wait_ge(S("yrstd_ready"), 2 * b + c + 1)
                    V.tensor_tensor(hc[0][:, :, cols[c]], hs[1][:, :, cols[c]], over(c_sb[1][:, cols[c]], 1, NH2),
                                    ALU.mult).then_inc(S("yn_ready"), 1)
                for c in range(2):
                    dve.wait_ge(S("yn_ready"), 2 * b + c + 1)
                    for h in range(NH2):
                        i = V.scalar_tensor_tensor(hc[1][:, h, cols[c]], hc[0][:, h, cols[c]], ln_g[:, h:h + 1],
                                                   skip[:, h, cols[c]], ALU.mult, ALU.add)
                    i.then_inc(S("yd_ready"), 1)
                for c in range(2):
                    dve.wait_ge(S("yd_ready"), 2 * b + c + 1)
                    dve.wait_ge(S("zs_ready"), 2 * b + c + 1)
                    V.tensor_tensor(hc[0][:, :, cols[c]], hc[1][:, :, cols[c]], zs[:, :, cols[c]], ALU.mult).then_inc(S("mix_ready"), 1)
                if more:
                    second_parts(gparts, 6, 2 * b + 2)
                for c in range(2):
                    dve.wait_ge(S("s0_ps"), 2 * b + c + 1)
                    V.tensor_tensor(c_sb[0][:, cols[c]], s_gT[:, cols[c]], ps[:, 2 + c, :], ALU.mult).then_inc(S("sg_ready"), 1)
                for c in range(2):
                    dve.wait_ge(S("sgT_ps"), 2 * b + c + 1)
                    x_half = x_all[:, b, c * NBLK // 2:(c + 1) * NBLK // 2].rearrange("p k d -> p (k d)")
                    V.tensor_tensor(x_half, x_half, ps[:, c, :], ALU.add).then_inc(S("x1_ready"), 1)
                if more:
                    third_parts(gparts, 2 * b + 2)

            front(0)
            second_parts(gparts, 6, 0)
            third_parts(gparts, 0)
            with dve.Fori(0, B - 1) as b:
                middle(b)
                tail(b, True)
            middle(B - 1)
            tail(B - 1, False)
            dve.wait_ge(S("x1_ready"), 2 * B + 1)
            norms(1)
            router(1, probs[:].rearrange("p b k e -> p (b k) e"))

            V.memset(thr[:], 0)
            V.memset(bit[:], 1 << ONE_BITS)
            V.memset(gpad[:], 0.0)
            V.memset(v_grp[:], 0.0).then_inc(S("setup1"), 1)
            dve.wait_ge(S("setup1"), 1)
            V.memset(v_grp[:, :, :, HD:HD + 1], 1.0).then_inc(S("setup1"), 1)
            dve.sem_inc(S("top_done"), TOP_AHEAD)
            dve.sem_inc(S("out_ready"), 1)
            dve.sem_inc(S("weighted_ready"), 1)
            dve.sem_inc(S("top_out"), 2)
            dve.sem_inc(S("acc_done"), 2)
            dve.sem_inc(S("thr_step"), 1)

            def by_block(ap):
                return over(ap, 2, NBLK)
            with dve.Fori(0, ONE_BITS + 1) as i:
                dve.wait_ge(S("thr_step"), i + 1)
                V.tensor_tensor(cand[:], thr[:], bit[:], ALU.bitwise_or).then_inc(S("cand_ready"), 1)
                dve.wait_ge(S("cand_ready"), i + 1)
                V.tensor_tensor(over_thr[:], probs[:], by_block(cand[:].bitcast(F32)), ALU.is_ge).then_inc(S("over_ready"), 1)
                dve.wait_ge(S("count_ps"), i + 1)
                V.scalar_tensor_tensor(step[:], ps[:, 0, 0:B * E].rearrange("p (b e) -> p b e", e=E), float(K1), bit[:],
                                       ALU.is_ge, ALU.mult).then_inc(S("step_ready"), 1)
                dve.wait_ge(S("step_ready"), i + 1)
                V.tensor_scalar(bit[:], bit[:], 1, None, ALU.logical_shift_right)
                V.tensor_tensor(thr[:], thr[:], step[:], ALU.bitwise_or).then_inc(S("thr_step"), 1)
            dve.wait_ge(S("thr_step"), ONE_BITS + 2)
            V.tensor_tensor(at_thr[:], probs[:], by_block(thr[:].bitcast(F32)), ALU.is_equal)
            V.tensor_tensor(over_thr[:], probs[:], by_block(thr[:].bitcast(F32)), ALU.is_gt).then_inc(S("split_ready"), 1)
            dve.wait_ge(S("ranks_ps"), 1)
            V.tensor_scalar(need[:], ps[:, 0, 0:B * E].rearrange("p (b e) -> p b e", e=E), -1.0, float(K1),
                            ALU.mult, ALU.add).then_inc(S("need_ready"), 1)
            dve.wait_ge(S("need_ready"), 1)
            V.tensor_tensor(picked[:], ps[:, 1, 0:B * NBLK * E].rearrange("p (b k e) -> p b k e", b=B, e=E),
                            by_block(need[:]), ALU.is_lt).then_inc(S("need_ready"), 1)
            dve.wait_ge(S("need_ready"), 2)
            V.tensor_tensor(picked[:], picked[:], at_thr[:], ALU.mult).then_inc(S("need_ready"), 1)
            dve.wait_ge(S("need_ready"), 3)
            V.tensor_tensor(picked[:], picked[:], over_thr[:], ALU.add).then_inc(S("need_ready"), 1)
            dve.wait_ge(S("need_ready"), 4)
            V.tensor_tensor(gate1[:], picked[:], probs[:], ALU.mult).then_inc(S("need_ready"), 1)
            dve.wait_ge(S("need_ready"), 5)
            dve.wait_ge(S("w1_loaded"), N_LOADS1)

            def front(b):
                V.tensor_scalar(xT[:], xnT_all[:, b, TAPS - 1:], 1.0, None, ALU.mult).then_inc(S("xT_ready"), 1)
                for i in range(3):
                    j = V.tensor_scalar(gpad[:, :, 32 * i:32 * i + E], gate1[:, b], 1.0, None, ALU.mult)
                j.then_inc(S("gpad_ready"), 1)

            def rest_gates(b):
                dve.wait_ge(S("gpart1"), b + 1)
                V.tensor_tensor(grest, banks(4, 2, PARTS), gparts1[:], ALU.subtract).then_inc(S("grest_ready"), 1)

            def third_gates(b):
                dve.wait_ge(S("grest_ready"), b + 1)
                dve.wait_ge(S("gpart2"), b + 1)
                V.tensor_tensor(gparts1[64:96, :], grest[64:96, :], gmid[64:96, :], ALU.subtract).then_inc(S("gparts1_ready"), 1)

            def rotary(b, i):
                if i == 1:
                    dve.wait_ge(S("qk_parts_ready"), 2 * b + 1)
                dve.wait_ge(S("qk_ps"), 2 * b + i + 1)
                V.scalar_tensor_tensor(rot[0], banks(0, 2), b_qk[:, 2 * i:2 * i + 1], cos[:], ALU.add, ALU.mult)
                V.scalar_tensor_tensor(rot[1], banks(2, 2), b_qk[:, 2 * i + 1:2 * i + 2], sin[:],
                                       ALU.add, ALU.mult).then_inc(S("halves_ready"), 1)

            def rotary_sum(b, i):
                dve.wait_ge(S("halves_ready"), 2 * b + i + 1)
                V.tensor_tensor(rot[0], rot[0], rot[1], ALU.add).then_inc(S("rot_ready"), 1)

            def remainder(b, i):
                dve.wait_ge(S("rot_ready"), 2 * b + i + 1)
                dve.wait_ge(S("qk_part1"), 2 * b + i + 1)
                V.tensor_tensor(rot[1], rot[0], qk_parts[i][:, 0, :], ALU.subtract).then_inc(S("qk_rest"), 1)

            def third_part(b, i):
                dve.wait_ge(S("qk_rest"), 2 * b + i + 1)
                dve.wait_ge(S("qk_part2"), 2 * b + i + 1)
                V.tensor_tensor(qk_parts[i][:, 2, :], rot[1], qk_parts[i][:, 1, :], ALU.subtract).then_inc(S("qk_parts_ready"), 1)

            def middle(b):
                V.memset(acc[:], 0.0).then_inc(S("acc_zero"), 1)

                def head_tops(h0, odd):
                    for k in range(NBLK):
                        n = (b * H + h0 + odd) * NBLK + k
                        dve.wait_ge(S("s_near_ps"), n + 1)
                        dve.wait_ge(S("s_half"), n + 1 + HALF_AHEAD)
                        if k % 2 == 0:
                            dve.wait_ge(S("top_out"), (b * H + h0 + odd) * (NBLK // 2) + k // 2 + 1)
                        V.tensor_tensor_scan(top_run[k // 2 % 2][:, k % 2, :], half_sb[k % 4], ps[:, (odd * NBLK + k) % 3, :],
                                             LOWEST, ALU.max, ALU.max).then_inc(S("top_done"), 1)
                        if k % 2:
                            dve.wait_ge(S("top_done"), n + 1 + TOP_AHEAD)
                            V.tensor_scalar(top[:, bass.ds((h0 + odd) * NBLK + k - 1, 2)], top_run[k // 2 % 2][:, :, HALF - 1],
                                            1.0, None, ALU.mult).then_inc(S("top_out"), 1)

                def weigh(n, c):
                    dve.wait_ge(S("gate_sb_ready"), 2 * n + c + 2)
                    dve.wait_ge(S("hid_used"), 8 * n + 4 * c + 4 + HID_AHEAD)
                    dve.wait_ge(S("acc_done"), 2 * n + c + 2)
                    V.tensor_tensor(weighted, ps[:, 7, :], gate_sb[c], ALU.mult).then_inc(S("weighted_ready"), 1)

                rotary(b, 1)
                rotary_sum(b, 1)
                remainder(b, 1)
                weigh(b * E, 0)
                third_part(b, 1)
                dve.wait_ge(S("v_ps"), b + 1)
                V.tensor_tensor(v_tok[:], banks(0, 2).rearrange("p (k c) -> p k c", k=NBLK), over(b_v[:], 1, NBLK),
                                ALU.add).then_inc(S("v_ready"), 1)
                weigh(b * E, 1)
                for c in range(2):
                    weigh(b * E + 1, c)
                with dve.Fori(1, E // 2 - 1) as e2:
                    for i in range(2):
                        for c in range(2):
                            for h in range(2):
                                head_tops(e2 * 8 - 8, i * 4 + c * 2 + h)
                            weigh(b * E + e2 * 2 + i, c)
                dve.wait_ge(S("top_part1"), b + 1)
                V.tensor_tensor(top_rest[:], ps[:, 0, 0:P], top_parts[:, 0, :], ALU.subtract).then_inc(S("top_rest_ready"), 1)
                dve.wait_ge(S("top_rest_ready"), b + 1)
                dve.wait_ge(S("top_part2"), b + 1)
                V.tensor_tensor(top_parts[:, 2, :], top_rest[:], top_parts[:, 1, :], ALU.subtract).then_inc(S("top_parts_ready"), 1)
                for e in (E - 2, E - 1):
                    for c in range(2):
                        weigh(b * E + e, c)
                dve.wait_ge(S("v_ready"), b + 1)

                def group_v(g):
                    dve.wait_ge(S("pv_done"), (b * 4 + g) * 8 + 2)
                    V.tensor_scalar(v_grp[:, :, :, 0:HD],
                                    v_tok[:, :, bass.ds(g * HG * HD, HG * HD)].rearrange("p k (j d) -> p k j d", j=HG),
                                    1.0, None, ALU.mult).then_inc(S("v_grp_ready"), 1)

                def divide(g):
                    ng = b * 4 + g
                    dve.wait_ge(S("o_ps"), ng + 1)
                    o = banks(6, 2).rearrange("p (k j c) -> p k j c", k=NBLK, j=HG)
                    V.reciprocal(rsum[:], o[:, :, :, HD]).then_inc(S("rsum_ready"), 1)
                    dve.wait_ge(S("rsum_ready"), ng + 1)
                    V.tensor_tensor(att[:, :, bass.ds(g * HG * HD, HG * HD)].rearrange("p k (j d) -> p k j d", j=HG),
                                    o[:, :, :, 0:HD], over(rsum[:], 3, HD), ALU.mult).then_inc(S("att_ready"), 1)
                group_v(0)
                with dve.Fori(1, H // HG) as g:
                    group_v(g)
                    divide(g - 1)
                return divide

            def tail(b, more, divide):
                if more:
                    front(b + 1)
                divide(3)
                if more:
                    rest_gates(b + 1)
                    rotary(b + 1, 0)
                    third_gates(b + 1)
                    rotary_sum(b + 1, 0)
                dve.wait_ge(S("silu_ready"), b + 1)
                dve.wait_ge(S("s1_ready"), b + 1)
                V.tensor_tensor(o_T[:], s1T[:], silu_bf[:], ALU.mult).then_inc(S("sg1_ready"), 1)
                if more:
                    remainder(b + 1, 0)
                dve.wait_ge(S("sg1_ps"), b + 1)
                xb = x_all[:, b].rearrange("p k d -> p (k d)")
                V.tensor_tensor(xb, xb, banks(6, 2), ALU.add).then_inc(S("out_ready"), 1)
                if more:
                    third_part(b + 1, 0)

            front(0)
            rest_gates(0)
            rotary(0, 0)
            third_gates(0)
            rotary_sum(0, 0)
            remainder(0, 0)
            third_part(0, 0)
            with dve.Fori(0, B - 1) as b:
                tail(b, True, middle(b))
            tail(B - 1, False, middle(B - 1))

        @block.tensor
        def _(pe):
            M = nc.tensor.matmul
            pe.wait_ge(S("w_loaded"), N_LOADS)
            pe.wait_ge(S("setup"), 1)
            pe.sem_inc(S("summed"), 2)
            pe.sem_inc(S("ffn_done"), 2)

            def turn(src, bank):
                for k in range(NBLK):
                    i = nc.tensor.transpose(ps[:, bank + k // 4, (k % 4) * P:(k % 4 + 1) * P], src(k), ident[:])
                return i

            def norms(n, wg):
                def logits(b):
                    pe.wait_ge(S("xnT_ready"), n * B + b + 1)
                    for k in range(NBLK):
                        r = b * NBLK + k
                        i = M(ps[:, 6, r * E:(r + 1) * E], xnT_all[:, b, TAPS - 1 + k * P:TAPS - 1 + (k + 1) * P], wg[:],
                              start=True, stop=True)
                    return i
                for b in range(B):
                    pe.wait_ge(S("xn_ready"), n * B + b + 1)
                    if b == 3:
                        pe.wait_ge(S("xnT_ready"), n * B + 1)
                    turn(lambda k: xn[b % 2][:, k, :], 2 * (b % 3)).then_inc(S("xnT_ps"), 1)
                    if b:
                        logits(b - 1)
                logits(B - 1).then_inc(S("lg_ps"), 1)

            def spread(s, bank, done):
                for c in range(2):
                    i = M(ps[:, bank + c, :], pick[:, s, :], bc[:, cols[c]], start=True, stop=True)
                i.then_inc(S(done), 1)

            def spread_b(s, n):
                pe.wait_ge(S("b_used"), n + 1)
                spread(s, 0, "b_ps")

            def spread_c(s, n):
                pe.wait_ge(S("c_ready"), n + 1)
                spread(s + NS, 2, "c_ps")

            def sum_states(i, n):
                pe.wait_ge(S("hc_ready"), n + 3)
                pe.wait_ge(S("c_used"), n + 3)
                for h in range(NH2):
                    for c in range(2):
                        m = M(ps[:, 4 + 2 * h + c, :], ident[:], hc[i][:, h, cols[c]], start=False, stop=False,
                              skip_group_check=True)
                m.then_inc(S("summed"), 1)

            def conv(b, h, c):
                for k in range(TAPS):
                    i = M(ps[:, 4 * h + c, :], w_tap[:, k, h * P:(h + 1) * P],
                          xnT_all[:, b, c * HALF + k:c * HALF + k + HALF], start=(k == 0), stop=(k == TAPS - 1))
                if c == 1:
                    i.then_inc(S("conv_ps"), 1)

            def gates(b):
                pe.wait_ge(S("gate0_ready"), b + 1)
                for k in range(NBLK):
                    i = nc.tensor.transpose(ps[0:PARTS, 6 + k // 4, (k % 4) * P:(k % 4 + 1) * P], gate0[:, k, :], ident[:])
                i.then_inc(S("gateT_ps"), 1)

            def z_path(b):
                for c in range(2):
                    for h in range(NH2):
                        i = M(ps[:, 4 + 2 * h + c, :], w_in[:, DI + h * P:DI + (h + 1) * P],
                              xnT_all[:, b, TAPS - 1 + c * HALF:TAPS - 1 + (c + 1) * HALF], start=True, stop=True)
                    i.then_inc(S("z_ps"), 1)

            def middle(b):
                pe.wait_ge(S("xc_ready"), 2 * b + 2)
                for h in range(NH2):
                    for c in range(2):
                        for k in range(NH2):
                            i = M(ps[:, 2 + 2 * h + c, :], w_dt[:, k, h * P:(h + 1) * P], xc[:, k, cols[c]],
                                  start=(k == 0), stop=(k == NH2 - 1))
                    i.then_inc(S("dt_ps"), 1)
                pe.wait_ge(S("x1_ready"), 2 * b + 1)
                for c in range(2):
                    for k in range(NH2):
                        i = M(ps[0:PARTS, c, :], w_x[:, k, :], xc[:, k, cols[c]], start=(k == 0), stop=(k == NH2 - 1))
                i.then_inc(S("bc_ps"), 1)
                pe.wait_ge(S("parts_ready"), 2 * b + 2)
                pe.wait_ge(S("relu_ready"), 2 * b + 2)
                pe.wait_ge(S("abs_ready"), 2 * b + 2)
                for c in range(2):
                    M(ps[:, 6 + c, :], b_e0[:], gateT[:, cols[c]], start=True, stop=False, skip_group_check=True)

                def gate_out(e):
                    if e >= 2:
                        pe.wait_ge(S("xg_ready"), b * E + e - 1)
                    for c in range(2):
                        i = M(ps[:, 2 + 2 * (e % 2) + c, :], pick[:, e, :], gparts[:, cols[c]], start=True, stop=True)
                    i.then_inc(S("gate_ps"), 1)
                gate_out(0)
                for e in range(E):
                    if e + 1 < E:
                        gate_out(e + 1)
                    pe.wait_ge(S("xg_ready"), b * E + e + 1)
                    for c in range(2):
                        i = M(ps[:, 6 + c, :], w_e0[:, e, :], xg[e % 2][:, cols[c]], start=False, stop=(e == E - 1),
                              skip_group_check=True)
                    i.then_inc(S("ffn_done"), 1)
                pe.wait_ge(S("parts_ready"), 2 * b + 3)
                n0 = b * NS
                spread_b(0, n0)
                for s in range(2):
                    spread_b(s + 1, n0 + s + 1)
                    spread_c(s, n0 + s)
                    if s == 0:
                        pe.wait_ge(S("s_g_ready"), b + 1)
                        for k in range(4):
                            M(ps[:, 4 + k, :], zeros_bf[:, 0:P], zeros_bf[:], start=True, stop=False, skip_group_check=True)
                with pe.Fori(1, NS // 2 - 1) as s2:
                    for i in range(2):
                        s = s2 * 2 + i
                        spread_c(s, n0 + s)
                        spread_b(s + 1, n0 + s + 1)
                        sum_states(i, n0 + s - 2)
                for s in (NS - 2, NS - 1):
                    if s < NS - 1:
                        spread_b(s + 1, n0 + s + 1)
                    spread_c(s, n0 + s)
                    sum_states(s % 2, n0 + s - 2)
                sum_states(0, n0 + NS - 2)
                sum_states(1, n0 + NS - 1)

            def over_channels(b, src, bank, ready, done):
                for c in range(2):
                    pe.wait_ge(S(ready), 2 * b + c + 1)
                    for k in range(NH2):
                        i = M(ps[:, bank + c, :], mean_w[:], src[:, k, cols[c]], start=(k == 0), stop=(k == NH2 - 1))
                    i.then_inc(S(done), 1)

            def tail(b, more):
                over_channels(b, hs[0], 0, "y_ready", "ymean_ps")
                z_path(b)
                over_channels(b, dA[0], 2, "sq_ready", "yvar_ps")
                if more:
                    pe.wait_ge(S("yc_ready"), 2 * b + 2)
                    conv(b + 1, 0, 0)
                    conv(b + 1, 0, 1)
                    pe.wait_ge(S("zs_ready"), 2 * b + 2)
                    gates(b + 1)
                    conv(b + 1, 1, 0)
                for c in range(2):
                    pe.wait_ge(S("mix_ready"), 2 * b + c + 1)
                    for k in range(NH2):
                        i = M(ps[:, 2 + c, :], w_out[:, k, :], hc[0][:, k, cols[c]], start=(k == 0), stop=(k == NH2 - 1))
                    i.then_inc(S("s0_ps"), 1)
                if more:
                    conv(b + 1, 1, 1)
                    pe.wait_ge(S("xc_ready"), 2 * b + 3)
                for c in range(2):
                    pe.wait_ge(S("sg_ready"), 2 * b + c + 1)
                    for k in range(NBLK // 2):
                        kk = c * NBLK // 2 + k
                        i = nc.tensor.transpose(ps[:, c, k * P:(k + 1) * P], c_sb[0][:, kk * P:(kk + 1) * P], ident[:])
                    i.then_inc(S("sgT_ps"), 1)

            norms(0, wg0)
            pe.wait_ge(S("taps_ready"), 1)
            for h in range(NH2):
                for c in range(2):
                    conv(0, h, c)
            pe.wait_ge(S("choice_ready"), 1)
            ch = choice_bf[:].rearrange("p k e -> p (k e)")
            M(ps[:, 7, 0:B * NBLK * E], before_tok[:], ch, start=True, stop=False, skip_group_check=True)
            for k in range(1, B * NBLK):
                i = M(ps[:, 7, k * E:B * NBLK * E], ones_bf[:], ch[:, 0:(B * NBLK - k) * E], start=False,
                      stop=(k == B * NBLK - 1), skip_group_check=True)
            i.then_inc(S("pos_ps"), 1)
            gates(0)
            with pe.Fori(0, B - 1) as b:
                middle(b)
                tail(b, True)
            middle(B - 1)
            tail(B - 1, False)
            norms(1, wg1)

            def count(what, bank):
                for k in range(NBLK):
                    i = M(ps[:, bank, 0:B * E].rearrange("p (b e) -> p b e", e=E), ones_bf[:], what[:, :, k, :],
                          start=(k == 0), stop=(k == NBLK - 1))
                return i

            with pe.Fori(0, ONE_BITS + 1) as i:
                pe.wait_ge(S("over_ready"), i + 1)
                count(over_thr, 0).then_inc(S("count_ps"), 1)
            pe.wait_ge(S("split_ready"), 1)
            count(over_thr, 0)
            ranks = ps[:, 1, 0:B * NBLK * E].rearrange("p (b k e) -> p b k e", b=B, e=E)
            M(ranks, before_tok[:], at_thr[:], start=True, stop=False, skip_group_check=True)
            for k in range(1, NBLK):
                i = M(ranks[:, :, k:, :], ones_bf[:], at_thr[:, :, 0:NBLK - k, :], start=False, stop=(k == NBLK - 1),
                      skip_group_check=True)
            i.then_inc(S("ranks_ps"), 1)
            pe.wait_ge(S("w1_loaded"), N_LOADS1)
            pe.wait_ge(S("setup1"), 2)
            pe.wait_ge(S("need_ready"), 5)
            pe.sem_inc(S("pv_done"), 2)
            pe.sem_inc(S("exp_done"), EXP_AHEAD)
            pe.sem_inc(S("hid_used"), HID_AHEAD)

            def project(b, i, j):
                for c in range(2):
                    m = M(ps[:, 2 * j + c, :], w_qk[:, 2 * i + j, :], xT[:, cols[c]], start=True, stop=True)
                if j == 1:
                    m.then_inc(S("qk_ps"), 1)

            def front_gates(b):
                pe.wait_ge(S("gpad_ready"), b + 1)
                for k in range(NBLK):
                    m = nc.tensor.transpose(ps[0:PARTS, 4 + k // 4, (k % 4) * P:(k % 4 + 1) * P], gpad[:, k, :], ident[:])
                m.then_inc(S("gpadT_ps"), 1)

            def front_k(b):
                pe.wait_ge(S("halves_ready"), 2 * b + 1)
                for j in range(2):
                    project(b, 1, j)

            def front_q(b):
                pe.wait_ge(S("xT_ready"), b + 1)
                for j in range(2):
                    project(b, 0, j)

            def middle(b):
                def score(h, v):
                    n = (b * H + h) * NBLK + v
                    lag = 1 if v == 0 else 3
                    k = v % NBLK
                    for c, bank, done in ((1, 3 + v % 2, "s_far_ps"), (0, v % 3, "s_near_ps")):
                        if c == 1:
                            pe.wait_ge(S("s_half"), n - 1 + HALF_AHEAD)
                        else:
                            pe.wait_ge(S("top_done"), n + 1 - lag + TOP_AHEAD)
                        M(ps[:, bank, :], q_op[:, h + v // NBLK, k * P:(k + 1) * P], k_op[:, h + v // NBLK, cols[c]],
                          start=True, stop=True).then_inc(S(done), 1)

                def expert(e, i, between):
                    n = b * E + e
                    pe.wait_ge(S(f"expert_loaded{i}"), b * 128 + (e - i) * 16 + 32)
                    for c in range(2):
                        pe.wait_ge(S("hid_ready"), 8 * n + 4 * c + 1)
                        M(ps[:, 5 + c, :], pick[:, e, :], gparts1[:, cols[c]], start=True, stop=True).then_inc(S("gate1_ps"), 1)

                        def up(q):
                            if q == 1:
                                pe.wait_ge(S("gate_sb_ready"), 2 * n + c + 2)
                            else:
                                pe.wait_ge(S("hid_ready"), 8 * n + 4 * c + max(q, 1) + 1)
                            M(ps[:, 5 + (c + 1 + q) % 2, :], w1[i][:, q * P:(q + 1) * P], xT[:, cols[c]],
                              start=True, stop=True).then_inc(S("hid_ps"), 1)

                        def down(q):
                            pe.wait_ge(S("hid_ready"), 8 * n + 4 * c + q + 3)
                            if q == 0:
                                pe.wait_ge(S("weighted_ready"), 2 * n + c + 1)
                            M(ps[:, 7, :], w2[i][:, q, :], hid[q], start=(q == 0), stop=(q == 3)).then_inc(S("hid_used"), 1)
                        for step, (product, q) in enumerate(((up, 0), (up, 1), (down, 0), (up, 2), (down, 1), (up, 3),
                                                             (down, 2), (down, 3))):
                            product(q)
                            between(c, step)

                def values_between(c, step):
                    if c == 1 and step == 0:
                        pe.wait_ge(S("halves_ready"), 2 * b + 2)
                        for k in range(NBLK):
                            m = M(ps[:, k // 4, (k % 4) * P:(k % 4 + 1) * P], xT[:, k * P:(k + 1) * P], w_v[:],
                                  start=True, stop=True)
                        m.then_inc(S("v_ps"), 1)

                def nothing(c, step):
                    pass

                pe.wait_ge(S("gparts1_ready"), b + 1)
                pe.wait_ge(S("out_ready"), b + 1)
                expert(0, 0, values_between)
                expert(1, 1, nothing)
                pe.wait_ge(S("ops_loaded0"), 16 * 19 * (b + 1))
                pe.wait_ge(S("v_ready"), b + 1)
                alone(pe)
                with pe.Fori(1, E // 2 - 1) as e2:
                    pe.wait_ge(S(f"ops_loaded{H // 2}"), 16 * 18 * (b + e2 - 1) + 1)
                    for i in range(2):
                        def scores_between(c, step):
                            for u in range(2):
                                score(e2 * 8 - 8, i * 32 + c * 16 + step * 2 + u)
                        expert(e2 * 2 + i, i, scores_between)
                pe.wait_ge(S("top_out"), (b + 1) * P // 2 + 2)
                nc.tensor.transpose(ps[:, 0, 0:P], top[:], ident[:]).then_inc(S("top_ps"), 1)
                for i in range(2):
                    expert(E - 2 + i, i, nothing)
                pe.wait_ge(S("top_loaded"), 16 * b + 16)

                def scores(g, k):
                    i = k % 2
                    for j in range(HG):
                        n = ((b * 4 + g) * 8 + k) * HG + j
                        pe.wait_ge(S("exp_done"), n + 1 - LAG[i * HG + j] + EXP_AHEAD)
                        for c in range(2):
                            m = M(ps[:, 2 * TILE[i * HG + j] + c, :], k_op[:, g * HG + j, k * P:(k + 1) * P],
                                  q_op[:, g * HG + j, cols[c]], start=True, stop=True)
                        m.then_inc(S("sT_ps"), 1)

                def sum_values(g, k):
                    pe.wait_ge(S("exp_done"), ((b * 4 + g) * 8 + k) * HG + HG + EXP_AHEAD)
                    for c in range(2):
                        for j in range(HG):
                            m = M(ps[32 * j:32 * j + 32, 6 + c, :], v_grp[:, k, j, :], big[k % 2][:, j, cols[c]],
                                  start=False, stop=False, skip_group_check=True)
                    m.then_inc(S("pv_done"), 1)

                def turn_o(g):
                    pe.wait_ge(S("o_ready"), b * 4 + g + 1)
                    turn(lambda k: o_T[:, k * P:(k + 1) * P], 6).then_inc(S("o_ps"), 1)
                    pe.wait_ge(S("att_ready"), b * 4 + g + 1)

                def score_group(g, first=False):
                    scores(g, 0)
                    if not first:
                        sum_values(g - 1, NBLK - 1)
                    scores(g, 1)
                    if not first:
                        turn_o(g - 1)
                    pe.wait_ge(S("v_grp_ready"), b * 4 + g + 1)
                    for c in range(2):
                        M(ps[:, 6 + c, :], zeros_bf[:, 0:P], zeros_bf[:], start=True, stop=False, skip_group_check=True)
                    sum_values(g, 0)
                    for k in range(2, NBLK):
                        scores(g, k)
                        sum_values(g, k - 1)
                score_group(0, first=True)
                with pe.Fori(1, H // HG) as g:
                    score_group(g)
                sum_values(H // HG - 1, NBLK - 1)
                return turn_o

            def tail(b, more, turn_o):
                if more:
                    front_gates(b + 1)
                turn_o(H // HG - 1)
                if more:
                    front_q(b + 1)
                turn(lambda k: att[:, k, :], 6).then_inc(S("attT_ps"), 1)
                pe.wait_ge(S("attT_ready"), b + 1)
                if more:
                    pe.wait_ge(S("grest_ready"), b + 2)
                for c in range(2):
                    m = M(ps[:, 4 + c, :], w_o[:], attT[:, cols[c]], start=True, stop=True)
                m.then_inc(S("s1_ps"), 1)
                if more:
                    front_k(b + 1)
                pe.wait_ge(S("sg1_ready"), b + 1)
                turn(lambda k: o_T[:, k * P:(k + 1) * P], 6).then_inc(S("sg1_ps"), 1)

            front_gates(0)
            front_q(0)
            front_k(0)
            with pe.Fori(0, B - 1) as b:
                tail(b, True, middle(b))
            tail(B - 1, False, middle(B - 1))


def rotary_tables():
    inv = (np.float32(1.0) / np.float32(10000.0) ** (np.arange(0, HD, 2, dtype=np.float32) / np.float32(HD)))
    angle = np.arange(T, dtype=np.float32)[None, :] * inv[:, None].astype(np.float32)
    angle = np.tile(np.concatenate([angle, angle]), (H, 1)).astype(np.float32)
    sign = np.where(np.arange(P) % 2 == 0, -1.0, 1.0).astype(np.float32)[:, None]
    return {"cos": np.cos(angle), "sin": sign * np.sin(angle)}


def host_constants():
    i = np.arange(P)
    bf = mybir.dt.np(BF16)
    pick = np.zeros((PARTS, 2 * NS, P), np.float32)
    for s in range(2 * NS):
        for g in range(3):
            pick[32 * g + s, s, :] = 1.0
    return {
        "ident": np.eye(P, dtype=np.float32),
        "before_tok": (i[:, None] < i[None, :]).astype(bf),
        "pick": pick.astype(bf),
        **rotary_tables(),
        "q_tail": np.zeros((PARTS - 72, H, T), bf),
        "k_tail": np.concatenate([-np.ones((3, H, T), bf), np.zeros((PARTS - 75, H, T), bf)]),
        "rank_w": np.tile(np.arange(E, 0, -1, dtype=np.float32), (P, 1)),
    }


def kernel(**inputs):
    import concourse.bacc as bacc
    from concourse.bass_utils import run_bass_kernel_spmd

    a = {k: np.ascontiguousarray(v) for k, v in inputs.items()}

    def halves(w):
        return w.reshape(2, P, -1).transpose(1, 0, 2)

    swap = np.arange(P) ^ 1
    w_x = halves(a["L0_attn_W_x"].T)
    arrays = {
        "x": a["L0_attn_x"],
        "w_in": a["L0_attn_W_in"].T,
        "taps": a["L0_attn_conv_w"][:, 0, :].T,
        "w_x": np.concatenate([w_x, w_x, w_x], axis=2),
        "w_dt": halves(a["L0_attn_W_dt"].T),
        "w_out": halves(a["L0_attn_W_out"].T),
        "chan": np.stack([a["L0_attn_" + n].reshape(2, P).T
                          for n in ("conv_b", "b_dt", "ln_g", "ln_b", "D_param")], axis=1),
        "a_log": a["L0_attn_A_log"],
        "wg0": a["L0_ffn_wg"],
        "w_e0": a["L0_ffn_W"].transpose(2, 0, 1),
        "b_e0": a["L0_ffn_b"],
        "wg1": a["L1_ffn_gate_w"],
        "w_qk": np.stack([w.T for w in (a["L1_attn_Wq"], a["L1_attn_Wq"][swap], a["L1_attn_Wk"], a["L1_attn_Wk"][swap])],
                         axis=1),
        "b_qk": np.stack([a["L1_attn_bq"], a["L1_attn_bq"][swap], a["L1_attn_bk"], a["L1_attn_bk"][swap],
                          a["L1_attn_bo"]], axis=1),
        "w_v": a["L1_attn_Wv"].T,
        "b_v": a["L1_attn_bv"],
        "w_o": a["L1_attn_Wo"].T,
        "w1": a["L1_ffn_w1"],
        "w2": a["L1_ffn_w2"],
        **host_constants(),
    }
    nc = bacc.Bacc("TRN2", target_bir_lowering=False, num_devices=1)
    arrays = {f"in_{k}": np.ascontiguousarray(v) for k, v in arrays.items()}
    aps = {k[3:]: nc.dram_tensor(k, v.shape, mybir.dt.from_np(v.dtype), kind="ExternalInput").ap()
           for k, v in arrays.items()}
    out = nc.dram_tensor("out", (B, T, D), F32, kind="ExternalOutput").ap()
    mixed_layers(nc, aps, out)
    r = run_bass_kernel_spmd(nc, [arrays], core_ids=[0])
    return r.results[0]["out"]
```
